# Optimizing a Trainium2 kernel written in Bass

```python
import numpy as np
import jax
import jax.numpy as jnp

def _softmax(x, axis=-1):
    return jax.nn.softmax(x, axis=axis)

def _gelu(x):
    return jax.nn.gelu(x, approximate=True)

def _silu(x):
    return jax.nn.silu(x)

def _sigmoid(x):
    return jax.nn.sigmoid(x)

def _layernorm(x, axis=-1, eps=1e-05):
    m = jnp.mean(x, axis=axis, keepdims=True)
    v = jnp.var(x, axis=axis, keepdims=True)
    return (x - m) / jnp.sqrt(v + eps)

def _scatter_add(tgt, idx, src, axis=0):
    return tgt.at[idx].add(src)

def _segment_sum(src, seg, n):
    return jax.ops.segment_sum(src, seg, n)
kernel_name = 'mk_adaln_d2_jaxref_r4_621a87'

def setup_inputs(seed: int=0):
    np.random.seed(seed)
    _w = jnp.asarray

    def _L0_attn_setup():
        import jax, jax.numpy as jnp
        import numpy as np
        MODEL_DIM = 256
        D_STATE = 16
        EXPAND = 2
        D_CONV = 4
        D_INNER = MODEL_DIM * EXPAND
        B, L = (4, 256)

        def _causal_depthwise_conv(x_bdl, conv_w, conv_b):
            kern = conv_w[:, None, :]
            out = jax.lax.conv_general_dilated(x_bdl, kern, window_strides=(1,), padding=[(D_CONV - 1, 0)], dimension_numbers=('NCH', 'OIH', 'NCH'), feature_group_count=D_INNER)
            return out + conv_b[None, :, None]
        key = jax.random.key(seed)
        ks = jax.random.split(key, 8)
        s_in = 1.0 / np.sqrt(MODEL_DIM)
        s_inner = 1.0 / np.sqrt(D_INNER)
        x = jax.random.normal(ks[0], (B, L, MODEL_DIM), dtype=jnp.float32)
        W_in = jax.random.normal(ks[1], (MODEL_DIM, 2 * D_INNER), dtype=jnp.float32) * s_in
        conv_w = jax.random.normal(ks[2], (D_INNER, D_CONV), dtype=jnp.float32) * (1.0 / np.sqrt(D_CONV))
        conv_b = jnp.zeros((D_INNER,), dtype=jnp.float32)
        W_x = jax.random.normal(ks[3], (D_INNER, 2 * D_STATE + 1), dtype=jnp.float32) * s_inner
        dt_w = jax.random.normal(ks[4], (D_INNER,), dtype=jnp.float32)
        dt_b = jax.random.normal(ks[5], (D_INNER,), dtype=jnp.float32) * 0.1
        A_log = jnp.broadcast_to(jnp.log(jnp.arange(1, D_STATE + 1, dtype=jnp.float32)), (D_INNER, D_STATE))
        D = jnp.ones((D_INNER,), dtype=jnp.float32)
        W_out = jax.random.normal(ks[6], (D_INNER, MODEL_DIM), dtype=jnp.float32) * s_inner
        return {'x': x, 'W_in': W_in, 'conv_w': conv_w, 'conv_b': conv_b, 'W_x': W_x, 'dt_w': dt_w, 'dt_b': dt_b, 'A_log': A_log, 'D': D, 'W_out': W_out}
    _L0_attn_in = _L0_attn_setup()

    def _L0_ffn_setup():
        import jax, jax.numpy as jnp
        import numpy as np
        DIM = 256
        NUM_EXPERTS = 8
        TOP_K = 2
        HIDDEN = int(DIM * 1.5)
        key = jax.random.key(seed)
        k_x, k_r, k_w1, k_w2, k_w3 = jax.random.split(key, 5)
        B, T = (2, 1024)
        s_in = 1.0 / np.sqrt(DIM)
        s_h = 1.0 / np.sqrt(HIDDEN)
        return {'x': jax.random.normal(k_x, (B, T, DIM), dtype=jnp.float32), 'Wr': jax.random.uniform(k_r, (DIM, NUM_EXPERTS), minval=-s_in, maxval=s_in, dtype=jnp.float32), 'W1': jax.random.uniform(k_w1, (NUM_EXPERTS, DIM, HIDDEN), minval=-s_in, maxval=s_in, dtype=jnp.float32), 'W2': jax.random.uniform(k_w2, (NUM_EXPERTS, HIDDEN, DIM), minval=-s_h, maxval=s_h, dtype=jnp.float32), 'W3': jax.random.uniform(k_w3, (NUM_EXPERTS, DIM, HIDDEN), minval=-s_in, maxval=s_in, dtype=jnp.float32)}
    _L0_ffn_in = _L0_ffn_setup()
    _L0_c = _w((lambda *s: np.random.randn(*s).astype(np.float32) * 0.05)(4, 256))
    _L0_wmod = _w((lambda *s: np.random.randn(*s).astype(np.float32) * 0.05)(256, 6 * 256) * 256 ** (-0.5))

    def _L1_attn_setup():
        import jax, jax.numpy as jnp
        import numpy as np
        H = 8
        D = 128
        E = 256

        def sinusoidal_pe(T, d, dtype=jnp.float32):
            pos = jnp.arange(T, dtype=jnp.float32)[:, None]
            div = jnp.exp(jnp.arange(0, d, 2, dtype=jnp.float32) * (-np.log(10000.0) / d))
            ang = pos * div
            pe = jnp.stack([jnp.sin(ang), jnp.cos(ang)], axis=-1).reshape(T, d)
            return pe.astype(dtype)
        key = jax.random.key(seed)
        k1, k2, k3 = jax.random.split(key, 3)
        B, T = (2, 512)
        x = jax.random.normal(k1, (B, T, E), dtype=jnp.float32)
        Wqkv = jax.random.normal(k2, (3 * H * D, E), dtype=jnp.float32) * (1.0 / np.sqrt(E))
        Wo = jax.random.normal(k3, (E, H * D), dtype=jnp.float32) * (1.0 / np.sqrt(H * D))
        return {'x': x, 'Wqkv': Wqkv, 'Wo': Wo}
    _L1_attn_in = _L1_attn_setup()

    def _L1_ffn_setup():
        import jax, jax.numpy as jnp
        import numpy as np
        D_MODEL = 256
        D_FF = 512
        NUM_EXPERTS = 16
        TOP_K = 2
        CAPACITY_FACTOR = 1.25
        BATCH, SEQ = (4, 512)
        key = jax.random.key(seed)
        k0, k1, k2, k3 = jax.random.split(key, 4)
        x = jax.random.normal(k0, (BATCH, SEQ, D_MODEL), jnp.float32)
        gate_w = jax.random.normal(k1, (NUM_EXPERTS, D_MODEL), jnp.float32) / np.float32(np.sqrt(D_MODEL))
        w1 = jax.random.normal(k2, (NUM_EXPERTS, D_MODEL, D_FF), jnp.float32) / np.float32(np.sqrt(D_MODEL))
        w2 = jax.random.normal(k3, (NUM_EXPERTS, D_FF, D_MODEL), jnp.float32) / np.float32(np.sqrt(D_FF))
        return {'x': x, 'gate_w': gate_w, 'w1': w1, 'w2': w2}
    _L1_ffn_in = _L1_ffn_setup()
    _L1_c = _w((lambda *s: np.random.randn(*s).astype(np.float32) * 0.05)(4, 256))
    _L1_wmod = _w((lambda *s: np.random.randn(*s).astype(np.float32) * 0.05)(256, 6 * 256) * 256 ** (-0.5))
    _d = {'L0_attn_x': _L0_attn_in['x'], 'L0_attn_W_in': _L0_attn_in['W_in'], 'L0_attn_conv_w': _L0_attn_in['conv_w'], 'L0_attn_conv_b': _L0_attn_in['conv_b'], 'L0_attn_W_x': _L0_attn_in['W_x'], 'L0_attn_dt_w': _L0_attn_in['dt_w'], 'L0_attn_dt_b': _L0_attn_in['dt_b'], 'L0_attn_A_log': _L0_attn_in['A_log'], 'L0_attn_D': _L0_attn_in['D'], 'L0_attn_W_out': _L0_attn_in['W_out'], 'L0_ffn_Wr': _L0_ffn_in['Wr'], 'L0_ffn_W1': _L0_ffn_in['W1'], 'L0_ffn_W2': _L0_ffn_in['W2'], 'L0_ffn_W3': _L0_ffn_in['W3'], 'L0_c': _L0_c, 'L0_wmod': _L0_wmod, 'L1_attn_Wqkv': _L1_attn_in['Wqkv'], 'L1_attn_Wo': _L1_attn_in['Wo'], 'L1_ffn_gate_w': _L1_ffn_in['gate_w'], 'L1_ffn_w1': _L1_ffn_in['w1'], 'L1_ffn_w2': _L1_ffn_in['w2'], 'L1_c': _L1_c, 'L1_wmod': _L1_wmod}
    _x0 = _d['L0_attn_x']
    _d['L0_attn_x'] = jax.random.normal(jax.random.fold_in(jax.random.key(seed), 1), (4, 1024, 256), dtype=_x0.dtype)
    del _x0
    return _d

def reference(L0_attn_x, L0_attn_W_in, L0_attn_conv_w, L0_attn_conv_b, L0_attn_W_x, L0_attn_dt_w, L0_attn_dt_b, L0_attn_A_log, L0_attn_D, L0_attn_W_out, L0_ffn_Wr, L0_ffn_W1, L0_ffn_W2, L0_ffn_W3, L0_c, L0_wmod, L1_attn_Wqkv, L1_attn_Wo, L1_ffn_gate_w, L1_ffn_w1, L1_ffn_w2, L1_c, L1_wmod):

    def _L0_attn_ref(x, W_in, conv_w, conv_b, W_x, dt_w, dt_b, A_log, D, W_out):
        import jax, jax.numpy as jnp
        import numpy as np
        MODEL_DIM = 256
        D_STATE = 16
        EXPAND = 2
        D_CONV = 4
        D_INNER = MODEL_DIM * EXPAND
        B, L = (4, 256)

        def _causal_depthwise_conv(x_bdl, conv_w, conv_b):
            kern = conv_w[:, None, :]
            out = jax.lax.conv_general_dilated(x_bdl, kern, window_strides=(1,), padding=[(D_CONV - 1, 0)], dimension_numbers=('NCH', 'OIH', 'NCH'), feature_group_count=D_INNER)
            return out + conv_b[None, :, None]
        xz = x @ W_in
        x_main, z = jnp.split(xz, 2, axis=-1)
        xc = _causal_depthwise_conv(jnp.swapaxes(x_main, 1, 2), conv_w, conv_b)
        x_conv = jax.nn.silu(jnp.swapaxes(xc, 1, 2))
        ssm = x_conv @ W_x
        delta_raw = ssm[..., 0:1]
        B_in = ssm[..., 1:1 + D_STATE]
        C_in = ssm[..., 1 + D_STATE:]
        delta = jax.nn.softplus(delta_raw * dt_w + dt_b)
        A = -jnp.exp(A_log)
        dA = jnp.exp(delta[..., None] * A)
        dBx = (delta * x_conv)[..., None] * B_in[:, :, None, :]

        def step(h, inp):
            dA_t, dBx_t, C_t = inp
            h = dA_t * h + dBx_t
            y_t = jnp.einsum('bdn,bn->bd', h, C_t)
            return (h, y_t)
        h0 = jnp.zeros((x.shape[0], D_INNER, D_STATE), dtype=x.dtype)
        xs = (jnp.swapaxes(dA, 0, 1), jnp.swapaxes(dBx, 0, 1), jnp.swapaxes(C_in, 0, 1))
        _, ys = jax.lax.scan(step, h0, xs)
        y = jnp.swapaxes(ys, 0, 1)
        y = y + D * x_conv
        y = y * jax.nn.silu(z)
        return y @ W_out

    def _L0_ffn_ref(x, Wr, W1, W2, W3):
        import jax, jax.numpy as jnp
        import numpy as np
        DIM = 256
        NUM_EXPERTS = 8
        TOP_K = 2
        HIDDEN = int(DIM * 1.5)
        B, T, C = x.shape
        xf = x.reshape(-1, C)
        gate_logits = xf @ Wr
        w, idx = jax.lax.top_k(gate_logits, TOP_K)
        w = jax.nn.softmax(w, axis=-1)
        comb = jnp.sum(w[:, :, None] * jax.nn.one_hot(idx, NUM_EXPERTS, dtype=w.dtype), axis=1)
        h = jnp.einsum('nc,ech->neh', xf, W1)
        g = jnp.einsum('nc,ech->neh', xf, W3)
        y = jnp.einsum('neh,ehc->nec', jax.nn.silu(h) * g, W2)
        out = jnp.einsum('nec,ne->nc', y, comb)
        return out.reshape(B, T, C)

    def _L1_attn_ref(x, Wqkv, Wo):
        import jax, jax.numpy as jnp
        import numpy as np
        H = 8
        D = 128
        E = 256

        def sinusoidal_pe(T, d, dtype=jnp.float32):
            pos = jnp.arange(T, dtype=jnp.float32)[:, None]
            div = jnp.exp(jnp.arange(0, d, 2, dtype=jnp.float32) * (-np.log(10000.0) / d))
            ang = pos * div
            pe = jnp.stack([jnp.sin(ang), jnp.cos(ang)], axis=-1).reshape(T, d)
            return pe.astype(dtype)
        B, T, _ = x.shape
        qkv = jnp.einsum('bte,fe->btf', x, Wqkv)
        qkv = qkv.reshape(B, T, H, 3 * D)
        q, k, v = jnp.split(qkv, 3, axis=-1)
        q = q.transpose(0, 2, 1, 3)
        k = k.transpose(0, 2, 1, 3)
        v = v.transpose(0, 2, 1, 3)
        pe = sinusoidal_pe(T, D, q.dtype)
        q = q + pe[None, None]
        k = k + pe[None, None]
        causal = jnp.tril(jnp.ones((T, T), dtype=bool))
        scores = jnp.einsum('bhtd,bhsd->bhts', q, k) / jnp.sqrt(jnp.asarray(D, q.dtype))
        scores = jnp.where(causal[None, None], scores, jnp.asarray(-jnp.inf, q.dtype))
        probs = jax.nn.softmax(scores, axis=-1)
        attn = jnp.einsum('bhts,bhsd->bhtd', probs, v)
        out = attn.transpose(0, 2, 1, 3).reshape(B, T, H * D)
        out = jnp.einsum('btf,ef->bte', out, Wo)
        return out

    def _L1_ffn_ref(x, gate_w, w1, w2):
        import jax, jax.numpy as jnp
        import numpy as np
        D_MODEL = 256
        D_FF = 512
        NUM_EXPERTS = 16
        TOP_K = 2
        CAPACITY_FACTOR = 1.25
        BATCH, SEQ = (4, 512)
        B, S, d = x.shape
        T = B * S
        E, K = (NUM_EXPERTS, TOP_K)
        capacity = int(CAPACITY_FACTOR * T * K / E)
        xf = x.reshape(T, d)
        logits = xf @ gate_w.T
        probs = jax.nn.sigmoid(logits)
        top_vals, sel = jax.lax.top_k(probs, K)
        weights = top_vals / (top_vals.sum(-1, keepdims=True) + 1e-06)
        flat_sel = sel.reshape(-1)
        onehot = jax.nn.one_hot(flat_sel, E, dtype=jnp.int32)
        ranks = jnp.take_along_axis(jnp.cumsum(onehot, axis=0), flat_sel[:, None], axis=1)[:, 0] - 1
        valid = ranks < capacity
        sentinel = E * capacity
        slot = jnp.where(valid, flat_sel * capacity + ranks, sentinel)
        x_rep = jnp.repeat(xf, K, axis=0)
        padded = jnp.zeros((sentinel + 1, d), xf.dtype).at[slot].set(x_rep)
        padded = padded[:sentinel].reshape(E, capacity, d)
        h = jax.nn.gelu(jnp.einsum('ecd,edf->ecf', padded, w1), approximate=False)
        out_padded = jnp.einsum('ecf,efd->ecd', h, w2).reshape(sentinel, d)
        gathered = out_padded[jnp.minimum(slot, sentinel - 1)]
        gathered = jnp.where(valid[:, None], gathered, jnp.zeros((), xf.dtype))
        out = (gathered * weights.reshape(-1)[:, None]).reshape(T, K, d).sum(axis=1)
        return out.reshape(B, S, d)
    x = L0_attn_x
    mod = (_silu(L0_c) @ L0_wmod).reshape(L0_c.shape[0], 6, 1, -1)
    sa, ca, ga, sb, cb, gb = (mod[:, 0], mod[:, 1], mod[:, 2], mod[:, 3], mod[:, 4], mod[:, 5])
    ga = (2 * (ga >= 0) - 1) * jnp.maximum(jnp.abs(ga), 0.25)
    gb = (2 * (gb >= 0) - 1) * jnp.maximum(jnp.abs(gb), 0.25)
    h = _layernorm(x, axis=-1) * (1 + ca) + sa
    x = x + ga * _L0_attn_ref(h, L0_attn_W_in, L0_attn_conv_w, L0_attn_conv_b, L0_attn_W_x, L0_attn_dt_w, L0_attn_dt_b, L0_attn_A_log, L0_attn_D, L0_attn_W_out)
    h = _layernorm(x, axis=-1) * (1 + cb) + sb
    x = x + gb * _L0_ffn_ref(h, L0_ffn_Wr, L0_ffn_W1, L0_ffn_W2, L0_ffn_W3)
    mod = (_silu(L1_c) @ L1_wmod).reshape(L1_c.shape[0], 6, 1, -1)
    sa, ca, ga, sb, cb, gb = (mod[:, 0], mod[:, 1], mod[:, 2], mod[:, 3], mod[:, 4], mod[:, 5])
    ga = (2 * (ga >= 0) - 1) * jnp.maximum(jnp.abs(ga), 0.25)
    gb = (2 * (gb >= 0) - 1) * jnp.maximum(jnp.abs(gb), 0.25)
    h = _layernorm(x, axis=-1) * (1 + ca) + sa
    x = x + ga * _L1_attn_ref(h, L1_attn_Wqkv, L1_attn_Wo)
    h = _layernorm(x, axis=-1) * (1 + cb) + sb
    x = x + gb * _L1_ffn_ref(h, L1_ffn_gate_w, L1_ffn_w1, L1_ffn_w2)
    return x

_drawn_inputs = setup_inputs


def setup_inputs(seed=0):
    import zlib

    import numpy as np

    out = dict(_drawn_inputs(seed))
    spreads = {'L0_attn_conv_b': (0.0, 0.294), 'L0_attn_D': (1.0, 0.6)}
    factors = {'L0_attn_dt_b': 5.017}
    for name, (base, spread) in spreads.items():
        noise = np.random.default_rng([zlib.crc32(name.encode()), seed]).standard_normal(out[name].shape)
        drawn = base * np.exp(spread * noise) if base else spread * noise
        out[name] = jnp.asarray(drawn.astype(out[name].dtype))
    for name, factor in factors.items():
        out[name] = (out[name] * factor).astype(out[name].dtype)
    return out
```

```python
from contextlib import ExitStack

import numpy as np

import concourse.bass as bass
from concourse import mybir

ALU = mybir.AluOpType
ACT = mybir.ActivationFunctionType
F32 = mybir.dt.float32
U32, I32 = mybir.dt.uint32, mybir.dt.int32
AX_X = mybir.AxisListType.X

P = 128
B, T, E = 4, 1024, 256
TILES = B * T // P
TPB = T // P
KE = E // P
EPS_LN = 1e-5

DI, NS, DC = 512, 16, 4
MD = DI // P
CH = 512
CPB = T // CH
CT = CH // P
G = 2
NG = NS // G
STEPS = NG * MD
RING, RING_A, RING_B = 4, 4, 4

EXPERTS0, H0 = 8, 384
MH0 = H0 // P
SLOTS0 = 2 * B * T + EXPERTS0 * P
TILES0 = SLOTS0 // P

HEADS, DH = 8, 128
EXPERTS1, F1 = 16, 512
MF1 = F1 // P
CAP1 = int(1.25 * B * T * 2 / EXPERTS1)
SLOTS1 = EXPERTS1 * CAP1 + P
FILL0, FILL1 = TILES0 // (B * CPB), EXPERTS1 * CAP1 // P // (B * CPB)


def token_tiles(ap):
    return ap.rearrange("b (j p) e -> p (b j) e", p=P)


class Shared:
    pass


class Semaphores:

    def __init__(self, nc, prefix):
        self.nc, self.prefix, self.taken = nc, prefix, []

    def __enter__(self):
        return self

    def __call__(self, name):
        self.taken.append(self.nc.alloc_semaphore(self.prefix + name))
        return self.taken[-1]

    def __exit__(self, *failure):
        if not any(failure):
            self.nc.clear_and_free_semaphores(self.taken)
            self.nc.all_engine_barrier()


def link_on(eng, sem):
    count = [0]

    def link(ins):
        count[0] += 1
        ins.then_inc(sem, 1)
        eng.wait_ge(sem, count[0])

    return link


def phase_prepare(nc, d, sh):
    with ExitStack() as ctx:
        sb = lambda name, shape: ctx.enter_context(nc.sbuf_tensor(name, shape, F32))
        sem = ctx.enter_context(Semaphores(nc, "prep_"))
        wmod = sb("wmod", [P, 2, KE, 6 * E])
        c_t = sb("c_t", [P, 2, KE, B])
        c_act = sb("c_act", [P, 2, KE, B])
        rows = sb("rows", [P, 2, 6, E])
        sign = sb("sign", [P, E])
        a_log = sb("a_log", [P, MD, NS])
        mod_ps = ctx.enter_context(nc.psum_tensor("mod_ps", [P, 2, 3, 512], F32))
        c_in, wmod_in, a_in, x_in = sem("c_in"), [sem("wmod0_in"), sem("wmod1_in")], sem("a_in"), [sem(f"x{b}_in") for b in range(B)]
        small_in, c_ready, mod_done, a_exp = sem("small_in"), sem("c_ready"), sem("mod_done"), sem("a_exp")
        rows_ready, rows_out, chain = sem("rows_ready"), sem("rows_out"), sem("chain")
        ident_set, wx_set = sem("ident_set"), sem("wx_set")
        block = ctx.enter_context(nc.Block())

        @block.sync
        def _(sp):
            sp.dma_start(c_t[:], d["cT"]).then_inc(c_in, 16)
            for l, name in enumerate(("L0_wmod", "L1_wmod")):
                sp.dma_start(wmod[:, l], d[name].rearrange("(k p) f -> p k f", p=P)).then_inc(wmod_in[l], 16)
            sp.dma_start(a_log[:], d["L0_attn_A_log"].rearrange("(m p) n -> p m n", p=P)).then_inc(a_in, 16)
            xt = token_tiles(d["L0_attn_x"])
            for b in range(B):
                sp.dma_start(sh.x[:, b * TPB:(b + 1) * TPB], xt[:, b * TPB:(b + 1) * TPB]).then_inc(x_in[b], 16)
            for dst, src in (
                (sh.w_in[:], d["L0_attn_W_in"].rearrange("(k p) f -> p k f", p=P)),
                (sh.w_out[:], d["L0_attn_W_out"].rearrange("(k p) f -> p k f", p=P)),
                (sh.w_x[:], d["L0_attn_W_x"].rearrange("(k p) f -> p k f", p=P)),
                (sh.conv_w[:], d["L0_attn_conv_w"].rearrange("(m p) j -> p m j", p=P)),
                (sh.vecs[:], d["vecs"]),
            ):
                sp.dma_start(dst, src).then_inc(small_in, 16)
            sp.wait_ge(rows_ready, 1)
            sp.dma_start(d["mod_rows"].rearrange("l j b e -> b l j e"), rows[0:B]).then_inc(rows_out, 16)
            sp.wait_ge(rows_out, 16)
            sp.wait_ge(small_in, 80)

        @block.gpsimd
        def _(pool):
            nc.gpsimd.memset(sh.zeros[:], 0.0)
            nc.gpsimd.memset(sh.ident[:], 0.0).then_inc(ident_set, 1)
            pool.wait_ge(ident_set, 1)
            nc.gpsimd.affine_select(out=sh.ident[:], in_=sh.ident[:], compare_op=ALU.not_equal, fill=1.0, base=0,
                                    pattern=[[-1, P]], channel_multiplier=1).then_inc(ident_set, 1)

        @block.scalar
        def _(act):
            act.wait_ge(c_in, 16)
            nc.scalar.activation(c_act[:], c_t[:], ACT.Silu).then_inc(c_ready, 1)
            act.wait_ge(a_in, 16)
            nc.scalar.activation(a_log[:], a_log[:], ACT.Exp).then_inc(a_exp, 1)

        @block.tensor
        def _(pe):
            pe.wait_ge(c_ready, 1)
            for l in range(2):
                pe.wait_ge(wmod_in[l], 16)
                for n in range(3):
                    for k in range(KE):
                        last = nc.tensor.matmul(mod_ps[0:B, l, n, :], c_act[:, l, k, :], wmod[:, l, k, n * 512:(n + 1) * 512],
                                                start=(k == 0), stop=(k == KE - 1))
                last.then_inc(mod_done, 1)

        @block.vector
        def _(dve):
            link = link_on(dve, chain)
            dve.wait_ge(a_exp, 1)
            nc.vector.tensor_scalar(sh.a_neg[:], a_log[:], -1.0, None, ALU.mult)
            for l in range(2):
                dve.wait_ge(mod_done, l + 1)
                for j in range(6):
                    src = mod_ps[0:B, l, j // 2, (j % 2) * E:(j % 2 + 1) * E]
                    dst = rows[0:B, l, j, :]
                    if j % 3 == 0:
                        last = nc.vector.tensor_copy(dst, src)
                    elif j % 3 == 1:
                        last = nc.vector.tensor_scalar(dst, src, 1.0, None, ALU.add)
                    else:
                        link(nc.vector.tensor_scalar(sign[0:B], src, 0.0, 2.0, ALU.is_ge, ALU.mult))
                        link(nc.vector.tensor_scalar(sign[0:B], sign[0:B], 1.0, None, ALU.subtract))
                        link(nc.vector.tensor_copy(dst, src))
                        link(nc.vector.scalar_tensor_tensor(out=dst, in0=dst, scalar=-1.0, in1=dst, op0=ALU.mult, op1=ALU.max))
                        link(nc.vector.tensor_scalar(dst, dst, 0.25, None, ALU.max))
                        link(nc.vector.tensor_tensor(dst, dst, sign[0:B], ALU.mult))
            dve.sem_inc(rows_ready, 1)
            for b in range(B):
                dve.wait_ge(x_in[b], 16)
                for i in range(b * TPB, (b + 1) * TPB):
                    nc.vector.bn_stats(sh.stats[:, i, :], sh.x[:, i, :])
            dve.wait_ge(small_in, 80)
            for k in range(MD):
                last = nc.vector.tensor_copy(sh.w_delta[:, k, :], sh.w_x[:, k, 0:1].broadcast_to([P, P]))
            last.then_inc(wx_set, 1)


def finish_stats(nc, dve, link, sh, std_ready, rstd_wait):
    s = sh.stats
    link(nc.vector.tensor_tensor(sh.mean[:], s[:, :, 1], s[:, :, 4], ALU.add))
    link(nc.vector.tensor_scalar(sh.mean[:], sh.mean[:], 0.5, None, ALU.mult))
    link(nc.vector.tensor_tensor(sh.dif[:], s[:, :, 1], s[:, :, 4], ALU.subtract))
    link(nc.vector.tensor_tensor(sh.dif[:], sh.dif[:], sh.dif[:], ALU.mult))
    link(nc.vector.tensor_tensor(sh.var[:], s[:, :, 2], s[:, :, 5], ALU.add))
    link(nc.vector.tensor_scalar(sh.dif[:], sh.dif[:], 0.25, EPS_LN, ALU.mult, ALU.add))
    nc.vector.scalar_tensor_tensor(out=sh.var[:], in0=sh.var[:], scalar=1.0 / E, in1=sh.dif[:],
                                   op0=ALU.mult, op1=ALU.add).then_inc(std_ready, 1)
    dve.wait_ge(rstd_wait, 1)
    link(nc.vector.reciprocal(sh.rstd[:], sh.var[:]))


def load_mods(sp, d, sh, layer, part, mods_in):
    sp.dma_start(sh.mods[:], d["mod_rows"][layer, 3 * part:3 * part + 3].partition_broadcast(P)).then_inc(mods_in, 16)


def norm_rows(nc, dve, sh, half, rows, half_ready, row_ready, rows_freed):
    ring = rows.shape[1]
    with dve.Fori(0, B) as b:
        for j in range(TPB):
            tile = b * TPB + j
            nc.vector.scalar_tensor_tensor(out=half[:, j % 2, :], in0=sh.x[:, tile, :], scalar=sh.mean[:, bass.ds(tile, 1)],
                                           in1=sh.mods[:, 1, b, :], op0=ALU.subtract, op1=ALU.mult).then_inc(half_ready, 1)
            dve.wait_ge(half_ready, b * TPB + j + 1)
            dve.wait_ge(rows_freed, b * TPB + j + 1)
            nc.vector.scalar_tensor_tensor(out=rows[:, j % ring, :], in0=half[:, j % 2, :], scalar=sh.rstd[:, bass.ds(tile, 1)],
                                           in1=sh.mods[:, 0, b, :], op0=ALU.mult, op1=ALU.add).then_inc(row_ready, 1)


def phase_norm_turn(nc, d, sh, layer):
    with ExitStack() as ctx:
        sb = lambda name, shape: ctx.enter_context(nc.sbuf_tensor(f"nt{layer}_{name}", shape, F32))
        sem = ctx.enter_context(Semaphores(nc, f"nt{layer}_"))
        half = sb("half", [P, 2, E])
        h_row = sb("h_row", [P, 2, E])
        h_chunk = sb("h_chunk", [P, CPB, KE, CH])
        turned = [ctx.enter_context(nc.psum_tensor(f"nt{layer}_turned{i}", [P, KE, P], F32)) for i in range(4)]
        mods_in, var_ready, std_ready, chain = sem("mods_in"), sem("var_ready"), sem("std_ready"), sem("chain")
        half_ready, row_ready, turn_done, turn_copied = sem("half_ready"), sem("row_ready"), sem("turn_done"), sem("turn_copied")
        stored = [sem(f"stored{i}") for i in range(CPB)]
        block = ctx.enter_context(nc.Block())

        @block.sync
        def _(sp):
            load_mods(sp, d, sh, layer, 0, mods_in)
            with sp.Fori(0, B) as b:
                for th in range(CPB):
                    sp.wait_ge(turn_copied, b * TPB + (th + 1) * CT + 4)
                    sp.dma_start(d["h_turned"][bass.ds(b * CPB + th, 1)].rearrange("o p k t -> (o p) k t"),
                                 h_chunk[:, th]).then_inc(stored[th], 16)
            for th in range(CPB):
                sp.wait_ge(stored[th], 16 * B + 1)

        @block.scalar
        def _(act):
            act.wait_ge(var_ready, 1)
            nc.scalar.activation(sh.var[:], sh.var[:], ACT.Sqrt).then_inc(std_ready, 1)
            with act.Fori(0, B) as b:
                for j in range(TPB):
                    if j % CT == 0:
                        act.wait_ge(stored[j // CT], b * 16 + 1)
                    act.wait_ge(turn_done, b * TPB + j + 3)
                    nc.scalar.copy(h_chunk[:, j // CT, :, (j % CT) * P:(j % CT + 1) * P], turned[j % 4][:]).then_inc(turn_copied, 1)

        @block.tensor
        def _(pe):
            pe.sem_inc(turn_done, 2)
            pe.sem_inc(turn_copied, 4)
            for th in range(CPB):
                pe.sem_inc(stored[th], 1)
            with pe.Fori(0, B) as b:
                for j in range(TPB):
                    pe.wait_ge(row_ready, b * TPB + j + 1)
                    pe.wait_ge(turn_copied, b * TPB + j + 1)
                    for k in range(KE):
                        last = nc.tensor.transpose(turned[j % 4][:, k, :], h_row[:, j % 2, k * P:(k + 1) * P], sh.ident[:])
                    last.then_inc(turn_done, 1)

        @block.vector
        def _(dve):
            link = link_on(dve, chain)
            finish_stats(nc, dve, link, sh, var_ready, std_ready)
            dve.wait_ge(mods_in, 16)
            norm_rows(nc, dve, sh, half, h_row, half_ready, row_ready, turn_done)


def phase_mamba(nc, d, sh):
    with ExitStack() as ctx:
        sb = lambda name, shape: ctx.enter_context(nc.sbuf_tensor(name, shape, F32))
        ps = lambda name, shape: ctx.enter_context(nc.psum_tensor(name, shape, F32))
        sem = ctx.enter_context(Semaphores(nc, "ss_"))
        x_main = sb("x_main", [P, 2, DC - 1 + CH])
        tail = sb("tail", [P, MD, DC - 1])
        x_conv = sb("x_conv", [P, 2, MD, CH])
        gate = sb("gate", [P, 2, MD, CH])
        delta = sb("delta", [P, 2, MD, CH])
        u = sb("u", [P, 2, MD, CH])
        h_in = sb("h_in", [P, 2, KE, CH])
        bc_sb = sb("bc_sb", [P, CH])
        b_all = sb("b_all", [P, RING_B, G, CH])
        c_all = sb("c_all", [P, RING_B, G, CH])
        da = sb("da", [P, RING_A, G, CH])
        dbx = sb("dbx", [P, RING, G, CH])
        state = sb("state", [P, STEPS, G])
        gated = sb("gated", [P, 2, E])
        y_ps = [ps(f"y_ps{m}", [P, CH]) for m in range(MD)]
        proj_ps = [ps(f"proj_ps{i}", [P, CH]) for i in range(2)]
        out_ps = [ps(f"out_ps{i}", [P, E]) for i in range(2)]

        PE_MAIN, PE_OUT, PE_BC, PE_Z = (0, 2, 4, 6), 9, 16, (19, 21, 23, 25)
        ACT_MAIN, ACT_SILU, ACT_BC, ACT_SOFT, ACT_Z = (6, 8, 10, 12), 17, 22, 24, (25, 27, 29, 31)
        DVE_CONV, DVE_OUT, DVE_RAW, DVE_DELTA = (6, 8, 10, 12), 13, 20, 28
        POOL_GATE = 6

        names = ("proj_done proj_copied conv_chain conv_done conv_act z_act bc_done delta_done bc_copied bc_stored raw_ready "
                 "soft_chain soft_ready delta_ready u_ready da_ready dbx_ready scanned states_kept hc_ready summed "
                 "y_taken y_gated out_done out_chain out_added tail_kept head_set filled").split()
        S = {n: sem(n) for n in names}
        bc_loaded = [sem(f"bc_loaded{i}") for i in range(RING_B)]
        h_loaded = [sem("h_loaded0"), sem("h_loaded1")]
        block = ctx.enter_context(nc.Block())

        def chunks(eng, body):
            for th in range(CPB):
                body(th, 0, th, th == 0, False)
            with eng.Fori(1, B - 1) as b:
                for th in range(CPB):
                    body(b * CPB + th, b, th, False, False)
            for th in range(CPB):
                body((B - 1) * CPB + th, B - 1, th, False, th == CPB - 1)

        zeros_over = lambda tiles: sh.zeros[:].rearrange("p (o e) -> p o e", o=1).broadcast_to([P, tiles, E])

        @block.sync
        def _(sp):
            def store_rows(c):
                sp.wait_ge(S["bc_copied"], c + 1)
                sp.dma_start(d["bc_rows"][bass.ds(c, 1)].rearrange("o n t -> (o n) t"), bc_sb[0:2 * NS, :]).then_inc(S["bc_stored"], 16)

            def load_group(c, g, first):
                if not (first and g < RING_B):
                    sp.wait_ge(S["dbx_ready"], c * STEPS + (g + 1 - RING_B) * MD)
                    sp.wait_ge(S["hc_ready"], c * STEPS + (g + 1 - RING_B) * MD)
                if g == 0:
                    sp.wait_ge(S["bc_stored"], c * 16 + 16)
                for dst, row in ((b_all, 0), (c_all, NS)):
                    src = d["bc_rows"][bass.ds(c, 1), row + g * G:row + (g + 1) * G, :].rearrange("o n t -> (o n) t")
                    sp.dma_start(dst[:, g % RING_B], src.partition_broadcast(P)).then_inc(bc_loaded[g % RING_B], 16)

            def load_h(c, b, p, first):
                if not first:
                    sp.wait_ge(S["proj_done"], c * 8 - 8)
                sp.dma_start(h_in[:, p], d["h_turned"][bass.ds(c, 1)].rearrange("o p k t -> (o p) k t")).then_inc(h_loaded[p], 16)

            def fill(c, g):
                rows, n, tiles = (d["slots0"], g, 3) if g < FILL0 // 3 else (d["slots1"], g - FILL0 // 3, 2)
                first_row = c * ((FILL0 if g < FILL0 // 3 else FILL1) * P) + n * tiles * P
                part = rows[bass.ds(first_row, tiles * P), :].rearrange("(a p) e -> p a e", p=P)
                sp.dma_start(part, zeros_over(tiles)).then_inc(S["filled"], 16)

            def body(c, b, th, first, last):
                for g in range(NG):
                    load_group(c, g, first)
                    fill(c, g)
                    if g == 4 and not (last or (isinstance(c, int) and c >= B * CPB - 2)):
                        load_h(c + 2, b + 1, th, False)
                if not last:
                    store_rows(c + 1)

            load_h(0, 0, 0, True)
            load_h(1, 0, 1, True)
            store_rows(0)
            for rows in (d["slots1"][FILL1 * P * B * CPB:], d["outs1"][EXPERTS1 * CAP1:]):
                sp.dma_start(rows.rearrange("(a p) e -> p a e", p=P), zeros_over(rows.shape[0] // P)).then_inc(S["filled"], 16)
            chunks(sp, body)
            sp.wait_ge(S["filled"], 16 * (NG * B * CPB + 2))

        @block.tensor
        def _(pe):
            def project(c, b, p, m, first):
                if m == 0:
                    pe.wait_ge(h_loaded[p], b * 16 + 16)
                if m in (MD, MD + 1):
                    pe.wait_ge(S["raw_ready" if m > MD else "bc_copied"], c + 1)
                elif not (first and m < 2):
                    pe.wait_ge(S["proj_copied"], c * 8 + m - 1)
                for k in range(KE):
                    mm = nc.tensor.matmul(proj_ps[m % 2][:], sh.w_in[:, k, m * P:(m + 1) * P], h_in[:, p, k, :],
                                          start=(k == 0), stop=(k == KE - 1))
                mm.then_inc(S["proj_done"], 1)

            def bc_product(c, p):
                pe.wait_ge(S["conv_act"], c + 1)
                pe.wait_ge(S["proj_copied"], c * 8 + 3)
                for k in range(MD):
                    mm = nc.tensor.matmul(proj_ps[0][0:2 * NS, :], sh.w_x[:, k, 1:1 + 2 * NS], x_conv[:, p, k, :],
                                          start=(k == 0), stop=(k == MD - 1))
                mm.then_inc(S["bc_done"], 1)

            def delta_product(c, p):
                pe.wait_ge(S["proj_copied"], c * 8 + 4)
                for k in range(MD):
                    mm = nc.tensor.matmul(proj_ps[1][:], sh.w_delta[:, k, :], x_conv[:, p, k, :],
                                          start=(k == 0), stop=(k == MD - 1))
                mm.then_inc(S["delta_done"], 1)

            def sum_states(c, s, first):
                g, m = s // MD, s % MD
                pe.wait_ge(S["hc_ready"], c * STEPS + s + 1)
                if g == 0 and not first:
                    pe.wait_ge(S["y_taken"], (c - 1) * MD + m + 1)
                for i in range(G):
                    mm = nc.tensor.matmul(y_ps[m][:], sh.ident[:], da[:, s % RING_A, i, :],
                                          start=(g == 0 and i == 0), stop=(g == NG - 1 and i == G - 1))
                mm.then_inc(S["summed"], 1)

            def out_product(c, p, j, first):
                pe.wait_ge(S["y_gated"], (c + 1) * MD)
                if not (first and j < 2):
                    pe.wait_ge(S["out_added"], c * CT + j - 1)
                for k in range(MD):
                    mm = nc.tensor.matmul(out_ps[j % 2][:], u[:, p, k, j * P:(j + 1) * P], sh.w_out[:, k, :],
                                          start=(k == 0), stop=(k == MD - 1))
                mm.then_inc(S["out_done"], 1)

            def body(c, b, th, first, last):
                for s in range(STEPS):
                    sum_states(c, s, first)
                    if not last:
                        if s in PE_MAIN:
                            project(c + 1, b + th, 1 - th, PE_MAIN.index(s), False)
                        if s == PE_BC:
                            bc_product(c + 1, 1 - th)
                        if s == PE_BC + 1:
                            delta_product(c + 1, 1 - th)
                        if s in PE_Z:
                            project(c + 1, b + th, 1 - th, MD + PE_Z.index(s), False)
                    if not first and PE_OUT <= s < PE_OUT + CT:
                        out_product(c - 1, 1 - th, s - PE_OUT, isinstance(c, int) and c == 1)

            for m in range(MD):
                project(0, 0, 0, m, True)
            bc_product(0, 0)
            delta_product(0, 0)
            for m in range(MD, 2 * MD):
                project(0, 0, 0, m, True)
            chunks(pe, body)
            for j in range(CT):
                out_product(B * CPB - 1, 1, j, False)

        @block.scalar
        def _(act):
            def copy_out(c, p, m):
                act.wait_ge(S["proj_done"], c * 8 + m + 1)
                if m < MD:
                    dst = x_main[:, m % 2, DC - 1:]
                    if m >= 2 or not (isinstance(c, int) and c == 0):
                        act.wait_ge(S["tail_kept"], (c * MD + m - 1))
                else:
                    dst = gate[:, p, m - MD, :]
                nc.scalar.copy(dst, proj_ps[m % 2][:]).then_inc(S["proj_copied"], 1)

            def silu_conv(c, p):
                act.wait_ge(S["conv_done"], (c + 1) * MD)
                nc.scalar.activation(x_conv[:, p], delta[:, p], ACT.Silu).then_inc(S["conv_act"], 1)

            def silu_z(c, p):
                act.wait_ge(S["proj_copied"], c * 8 + 8)
                nc.scalar.activation(gate[:, p], gate[:, p], ACT.Silu).then_inc(S["z_act"], 1)

            def copy_bc(c, first):
                act.wait_ge(S["bc_done"], c + 1)
                if not first:
                    act.wait_ge(S["bc_stored"], c * 16)
                nc.scalar.copy(bc_sb[0:2 * NS, :], proj_ps[0][0:2 * NS, :]).then_inc(S["bc_copied"], 1)

            def softplus(c, p):
                act.wait_ge(S["raw_ready"], c + 1)
                nc.scalar.activation(u[:, p], delta[:, p], ACT.Abs).then_inc(S["soft_chain"], 1)
                act.wait_ge(S["soft_chain"], c * 2 + 1)
                nc.scalar.activation(u[:, p], u[:, p], ACT.Exp, scale=-1.0).then_inc(S["soft_chain"], 1)
                act.wait_ge(S["soft_chain"], c * 2 + 2)
                nc.scalar.activation(u[:, p], u[:, p], ACT.Ln, bias=1.0).then_inc(S["soft_ready"], 1)

            def decays(c, p, s, first):
                g, m = s // MD, s % MD
                if s == 0:
                    act.wait_ge(S["delta_ready"], c + 1)
                if not (first and s < RING_A):
                    act.wait_ge(S["summed"], c * STEPS + s + 1 - RING_A)
                for i in range(G):
                    ex = nc.scalar.activation(da[:, s % RING_A, i, :], delta[:, p, m, :], ACT.Exp,
                                              scale=sh.a_neg[:, m, g * G + i:g * G + i + 1])
                ex.then_inc(S["da_ready"], 1)

            def body(c, b, th, first, last):
                for s in range(STEPS):
                    decays(c, th, s, first)
                    if s == ACT_SILU:
                        silu_z(c, th)
                        if not last:
                            silu_conv(c + 1, 1 - th)
                    if not last:
                        if s in ACT_MAIN:
                            copy_out(c + 1, 1 - th, ACT_MAIN.index(s))
                        if s == ACT_BC:
                            copy_bc(c + 1, False)
                        if s == ACT_SOFT:
                            softplus(c + 1, 1 - th)
                        if s in ACT_Z:
                            if s == ACT_Z[0] and not first:
                                act.wait_ge(S["y_gated"], c * MD)
                            copy_out(c + 1, 1 - th, MD + ACT_Z.index(s))

            for m in range(MD):
                copy_out(0, 0, m)
            silu_conv(0, 0)
            copy_bc(0, True)
            softplus(0, 0)
            for m in range(MD, 2 * MD):
                copy_out(0, 0, m)
            chunks(act, body)

        @block.gpsimd
        def _(pool):
            def products(c, p, s, first):
                g, m = s // MD, s % MD
                if s == 0:
                    pool.wait_ge(S["u_ready"], c + 1)
                if m == 0:
                    pool.wait_ge(bc_loaded[g % RING_B], c * (32 * NG // RING_B) + 32 * (g // RING_B + 1))
                if not (first and s < RING):
                    pool.wait_ge(S["scanned"], c * STEPS + s + 1 - RING)
                nc.gpsimd.tensor_tensor(dbx[:, s % RING], u[:, p, m:m + 1, :].broadcast_to([P, G, CH]), b_all[:, g % RING_B],
                                        ALU.mult).then_inc(S["dbx_ready"], 1)

            def gate_y(c, p, m):
                pool.wait_ge(S["y_taken"], c * MD + m + 1)
                if m == 0:
                    pool.wait_ge(S["z_act"], c + 1)
                nc.gpsimd.tensor_tensor(u[:, p, m, :], u[:, p, m, :], gate[:, p, m, :], ALU.mult).then_inc(S["y_gated"], 1)

            def body(c, b, th, first, last):
                for s in range(STEPS):
                    products(c, th, s, first)
                    if not first and POOL_GATE <= s < POOL_GATE + MD:
                        gate_y(c - 1, 1 - th, s - POOL_GATE)

            chunks(pool, body)
            for m in range(MD):
                gate_y(B * CPB - 1, 1, m)

        @block.vector
        def _(dve):
            def convolve(c, p, m, fresh):
                dve.wait_ge(S["proj_copied"], c * 8 + m + 1)
                if not fresh:
                    dve.wait_ge(S["tail_kept"], (c - 1) * MD + m + 1)
                acc, xm = delta[:, p, m, :], x_main[:, m % 2, :]
                if fresh:
                    nc.vector.memset(xm[:, 0:DC - 1], 0.0).then_inc(S["head_set"], 1)
                else:
                    nc.vector.tensor_copy(xm[:, 0:DC - 1], tail[:, m, :]).then_inc(S["head_set"], 1)
                dve.wait_ge(S["head_set"], c * MD + m + 1)
                nc.vector.tensor_scalar(acc, xm[:, 0:CH], sh.conv_w[:, m, 0:1], sh.vecs[:, 0, m:m + 1],
                                        ALU.mult, ALU.add).then_inc(S["conv_chain"], 1)
                for j in range(1, DC):
                    dve.wait_ge(S["conv_chain"], (c * MD + m) * (DC - 1) + j)
                    ins = nc.vector.scalar_tensor_tensor(out=acc, in0=xm[:, j:j + CH], scalar=sh.conv_w[:, m, j:j + 1],
                                                         in1=acc, op0=ALU.mult, op1=ALU.add)
                    ins.then_inc(S["conv_chain"] if j < DC - 1 else S["conv_done"], 1)
                nc.vector.tensor_copy(tail[:, m, :], xm[:, CH:]).then_inc(S["tail_kept"], 1)

            def raw_delta(c, p):
                dve.wait_ge(S["delta_done"], c + 1)
                for m in range(MD):
                    ins = nc.vector.tensor_scalar(delta[:, p, m, :], proj_ps[1][:], sh.vecs[:, 1, m:m + 1], sh.vecs[:, 2, m:m + 1],
                                                  ALU.mult, ALU.add)
                ins.then_inc(S["raw_ready"], 1)

            def finish_delta(c, p):
                dve.wait_ge(S["soft_ready"], c + 1)
                nc.vector.scalar_tensor_tensor(out=delta[:, p], in0=delta[:, p], scalar=0.0, in1=u[:, p],
                                               op0=ALU.max, op1=ALU.add).then_inc(S["delta_ready"], 1)
                dve.wait_ge(S["delta_ready"], c + 1)
                nc.vector.tensor_tensor(u[:, p], delta[:, p], x_conv[:, p], ALU.mult).then_inc(S["u_ready"], 1)

            def scans(c, b, th, s):
                g, m = s // MD, s % MD
                dve.wait_ge(S["da_ready"], c * STEPS + s + 1)
                dve.wait_ge(S["dbx_ready"], c * STEPS + s + 1)
                if th == 1:
                    dve.wait_ge(S["states_kept"], b * STEPS + s + 1)
                for i in range(G):
                    h = da[:, s % RING_A, i, :]
                    ins = nc.vector.tensor_tensor_scan(h, h, dbx[:, s % RING, i, :], 0.0 if th == 0 else state[:, s, i:i + 1],
                                                       ALU.mult, ALU.add)
                ins.then_inc(S["scanned"], 1)

            def outputs(c, b, th, s):
                g, m = s // MD, s % MD
                dve.wait_ge(S["scanned"], c * STEPS + s + 1)
                if th == 0:
                    nc.vector.tensor_copy(state[:, s, :], da[:, s % RING_A, :, CH - 1]).then_inc(S["states_kept"], 1)
                    dve.wait_ge(S["states_kept"], b * STEPS + s + 1)
                if m == 0:
                    dve.wait_ge(bc_loaded[g % RING_B], c * (32 * NG // RING_B) + 32 * (g // RING_B + 1))
                nc.vector.tensor_tensor(da[:, s % RING_A], da[:, s % RING_A], c_all[:, g % RING_B], ALU.mult).then_inc(S["hc_ready"], 1)

            def take_y(c, p, m):
                dve.wait_ge(S["summed"], (c + 1) * STEPS - MD + m + 1)
                nc.vector.scalar_tensor_tensor(out=u[:, p, m, :], in0=x_conv[:, p, m, :], scalar=sh.vecs[:, 3, m:m + 1],
                                               in1=y_ps[m][:], op0=ALU.mult, op1=ALU.add).then_inc(S["y_taken"], 1)

            def add_out(c, b, th, j):
                tile = c * CT + j
                dve.wait_ge(S["out_done"], c * CT + j + 1)
                nc.vector.tensor_tensor(gated[:, j % 2, :], out_ps[j % 2][:], sh.mods[:, 2, b, :], ALU.mult).then_inc(S["out_added"], 1)
                dve.wait_ge(S["out_added"], c * CT + j + 1)
                nc.vector.tensor_tensor(sh.x[:, tile, :], sh.x[:, tile, :], gated[:, j % 2, :], ALU.add).then_inc(S["out_chain"], 1)
                dve.wait_ge(S["out_chain"], c * CT + j + 1)
                nc.vector.bn_stats(sh.stats[:, tile, :], sh.x[:, tile, :])

            def body(c, b, th, first, last):
                for s in range(STEPS):
                    scans(c, b, th, s)
                    outputs(c, b, th, s)
                    if not last:
                        if s in DVE_CONV:
                            convolve(c + 1, 1 - th, DVE_CONV.index(s), th == CPB - 1)
                        if s == DVE_RAW:
                            raw_delta(c + 1, 1 - th)
                        if s == DVE_DELTA:
                            finish_delta(c + 1, 1 - th)
                    if not first:
                        if s < MD:
                            take_y(c - 1, 1 - th, s)
                        if DVE_OUT <= s < DVE_OUT + CT:
                            add_out(c - 1, b if th == 1 else b - 1, 1 - th, s - DVE_OUT)

            for m in range(MD):
                convolve(0, 0, m, True)
            raw_delta(0, 0)
            finish_delta(0, 0)
            chunks(dve, body)
            for m in range(MD):
                take_y(B * CPB - 1, 1, m)
            for j in range(CT):
                add_out(B * CPB - 1, B - 1, 1, j)


def phase_route(nc, d, sh, layer, gate_name, slots_name):
    NE = (EXPERTS0, EXPERTS1)[layer]
    with ExitStack() as ctx:
        sb = lambda name, shape, dt=F32: ctx.enter_context(nc.sbuf_tensor(f"rt{layer}_{name}", shape, dt))
        ps = lambda name, shape: ctx.enter_context(nc.psum_tensor(f"rt{layer}_{name}", shape, F32))
        sem = ctx.enter_context(Semaphores(nc, f"rt{layer}_"))
        gate_w = sb("gate_w", [P, KE, NE])
        half = sb("half", [P, 2, E])
        row8 = sb("row8", [P, TPB, E])
        h_rows = sb("h_rows", [P, TILES, E])
        h_tr = sb("h_tr", [P, 2, KE, P])
        logits = sb("logits", [P, TILES, NE])
        scores = sb("scores", [P, TILES, NE])
        cand = sb("cand", [P, TILES, NE])
        rank = sb("rank", [P, TILES, NE])
        mask = sb("mask", [P, 2, TILES, NE])
        both = sb("both", [P, TILES, NE])
        iota_e = sb("iota_e", [P, TILES, NE])
        top = sb("top", [P, 2, TILES])
        idx = sb("idx", [P, TILES])
        tri = sb("tri", [P, P])
        ones = sb("ones", [P, P])
        run_on = sb("run_on", [P, NE, TILES])
        total = sb("total", [P, NE, TILES])
        before = sb("before", [P, NE, TILES])
        count = sb("count", [P, NE])
        count_i = sb("count_i", [P, NE], I32)
        padded = sb("padded", [P, NE])
        ends = sb("ends", [P, NE])
        offs = sb("offs", [P, NE])
        slot = sb("slot", [P, 2, TILES])
        valid = sb("valid", [P, 2, TILES])
        spare = sb("spare", [P, 1])
        wsum = sb("wsum", [P, TILES])
        tiles_at = sb("tiles_at", [P, TILES0])
        owner = sb("owner", [P, TILES0])
        turned = [ps(f"turned{i}", [P, KE, P]) for i in range(2)]
        logit_ps = ps("logit_ps", [P, TPB, NE])
        tri_ps, tot_ps = ps("tri_ps", [P, TILES, NE]), ps("tot_ps", [P, TILES, NE])
        (mods_in, gate_in, var_ready, std_ready, chain, half_ready, row_ready, row_turned, turn_copied, logits_done, rows_copied,
         logits_copied, consts_ready, score_ready, masks_ready, ranked, gap_ready, exp_ready, slots_ready, scattered, pool_chain) = (
            sem(n) for n in ("mods_in gate_in var_ready std_ready chain half_ready row_ready row_turned turn_copied logits_done "
                             "rows_copied logits_copied consts_ready score_ready masks_ready ranked gap_ready exp_ready "
                             "slots_ready scattered pool_chain").split())
        block = ctx.enter_context(nc.Block())

        @block.sync
        def _(sp):
            load_mods(sp, d, sh, layer, 1, mods_in)
            sp.dma_start(gate_w[:], d[gate_name].rearrange("(k p) n -> p k n", p=P)).then_inc(gate_in, 16)

        @block.gpsimd
        def _(pool):
            nc.gpsimd.memset(tri[:], 1.0).then_inc(pool_chain, 1)
            nc.gpsimd.memset(ones[:], 1.0).then_inc(pool_chain, 1)
            pool.wait_ge(pool_chain, 2)
            nc.gpsimd.affine_select(out=tri[:], in_=tri[:], compare_op=ALU.is_gt, fill=0.0, base=0, pattern=[[1, P]],
                                    channel_multiplier=-1).then_inc(consts_ready, 1)
            nc.gpsimd.iota(iota_e[:], pattern=[[0, TILES], [1, NE]], base=0, channel_multiplier=0,
                           allow_small_or_imprecise_dtypes=True).then_inc(consts_ready, 1)
            nc.gpsimd.memset(run_on[:], 1.0).then_inc(pool_chain, 1)
            pool.wait_ge(pool_chain, 3)
            nc.gpsimd.memset(run_on[:, :, 0:1], 0.0).then_inc(consts_ready, 1)
            nc.gpsimd.iota(offs[:], pattern=[[CAP1, NE]], base=0, channel_multiplier=0,
                           allow_small_or_imprecise_dtypes=True).then_inc(consts_ready, 1)
            nc.gpsimd.iota(spare[:], pattern=[[0, 1]], base=EXPERTS1 * CAP1, channel_multiplier=1,
                           allow_small_or_imprecise_dtypes=True).then_inc(consts_ready, 1)
            nc.gpsimd.iota(tiles_at[:], pattern=[[P, TILES0]], base=0, channel_multiplier=0,
                           allow_small_or_imprecise_dtypes=True).then_inc(consts_ready, 1)
            pool.wait_ge(slots_ready, 1)
            pool.wait_ge(rows_copied, TILES + 1)
            for i in range(TILES):
                for k in range(2):
                    nc.gpsimd.indirect_dma_start(out=d[slots_name], out_offset=bass.IndirectOffsetOnAxis(ap=sh.slot_of[:, k, i:i + 1], axis=0),
                                                 in_=h_rows[:, i, :], in_offset=None).then_inc(scattered, 16)
            pool.wait_ge(scattered, 2 * TILES * 16)

        @block.scalar
        def _(act):
            act.wait_ge(var_ready, 1)
            nc.scalar.activation(sh.var[:], sh.var[:], ACT.Sqrt).then_inc(std_ready, 1)
            with act.Fori(0, B) as b:
                for j in range(TPB):
                    act.wait_ge(row_ready, b * TPB + j + 1)
                    nc.scalar.copy(h_rows[:, b * TPB + j, :], row8[:, j, :]).then_inc(rows_copied, 1)
                    act.wait_ge(row_turned, b * TPB + j + 1 + TPB)
                    act.wait_ge(logits_done, b * TPB + j + 1)
                    nc.scalar.copy(h_tr[:, j % 2], turned[j % 2][:]).then_inc(turn_copied, 1)
                act.wait_ge(logits_done, b * TPB + TPB + 2)
                nc.scalar.copy(logits[:, bass.ds(b * TPB, TPB), :], logit_ps[:]).then_inc(logits_copied, 1)
            act.wait_ge(logits_copied, B + 1)
            if layer == 1:
                nc.scalar.activation(logits[:], logits[:], ACT.Sigmoid).then_inc(score_ready, 1)
            else:
                act.sem_inc(score_ready, 1)
                act.wait_ge(gap_ready, 1)
                nc.scalar.activation(sh.weight[:, 1], sh.weight[:, 1], ACT.Exp).then_inc(exp_ready, 1)

        @block.tensor
        def _(pe):
            pe.sem_inc(row_turned, TPB)
            pe.sem_inc(logits_done, 2)
            pe.sem_inc(turn_copied, 2)
            pe.sem_inc(logits_copied, 1)
            pe.sem_inc(rows_copied, 1)
            pe.wait_ge(gate_in, 16)

            with pe.Fori(0, B) as b:
                def turn(j):
                    pe.wait_ge(row_ready, b * TPB + j + 1)
                    pe.wait_ge(turn_copied, b * TPB + j + 1)
                    for k in range(KE):
                        last = nc.tensor.transpose(turned[j % 2][:, k, :], row8[:, j, k * P:(k + 1) * P], sh.ident[:])
                    last.then_inc(row_turned, 1)

                def product(j):
                    pe.wait_ge(turn_copied, b * TPB + j + 3)
                    if j == 0:
                        pe.wait_ge(logits_copied, b + 1)
                    for k in range(KE):
                        last = nc.tensor.matmul(logit_ps[:, j, :], h_tr[:, j % 2, k, :], gate_w[:, k, :],
                                                start=(k == 0), stop=(k == KE - 1))
                    last.then_inc(logits_done, 1)

                turn(0)
                for j in range(1, TPB):
                    turn(j)
                    product(j - 1)
                product(TPB - 1)
            pe.wait_ge(masks_ready, 1)
            pe.wait_ge(consts_ready, 1)
            nc.tensor.matmul(tri_ps[:], tri[:], both[:], start=True, stop=True).then_inc(ranked, 1)
            nc.tensor.matmul(tot_ps[:], ones[:], both[:], start=True, stop=True).then_inc(ranked, 1)

        @block.vector
        def _(dve):
            link = link_on(dve, chain)
            finish_stats(nc, dve, link, sh, var_ready, std_ready)
            dve.wait_ge(mods_in, 16)

            with dve.Fori(0, B) as b:
                for j in range(TPB):
                    tile = b * TPB + j
                    nc.vector.scalar_tensor_tensor(out=half[:, j % 2, :], in0=sh.x[:, tile, :], scalar=sh.mean[:, bass.ds(tile, 1)],
                                                   in1=sh.mods[:, 1, b, :], op0=ALU.subtract, op1=ALU.mult).then_inc(half_ready, 1)
                    dve.wait_ge(half_ready, b * TPB + j + 1)
                    dve.wait_ge(row_turned, b * TPB + j + 1)
                    dve.wait_ge(rows_copied, b * TPB + 1)
                    nc.vector.scalar_tensor_tensor(out=row8[:, j, :], in0=half[:, j % 2, :], scalar=sh.rstd[:, bass.ds(tile, 1)],
                                                   in1=sh.mods[:, 0, b, :], op0=ALU.mult, op1=ALU.add).then_inc(row_ready, 1)

            over = lambda a: a.rearrange("p (t o) -> p t o", o=1).broadcast_to([P, TILES, NE])
            dve.wait_ge(score_ready, 1)
            dve.wait_ge(consts_ready, 6)
            values = logits
            for k in range(2):
                link(nc.vector.tensor_reduce(top[:, k], values[:], AX_X, ALU.max))
                link(nc.vector.tensor_tensor(cand[:], values[:], over(top[:, k]), ALU.is_lt))
                link(nc.vector.scalar_tensor_tensor(out=cand[:], in0=cand[:], scalar=float(NE), in1=iota_e[:], op0=ALU.mult, op1=ALU.add))
                link(nc.vector.tensor_reduce(idx[:], cand[:], AX_X, ALU.min))
                link(nc.vector.tensor_tensor(mask[:, k], iota_e[:], over(idx[:]), ALU.is_equal))
                if k == 0:
                    link(nc.vector.scalar_tensor_tensor(out=scores[:], in0=mask[:, 0], scalar=-3e38, in1=values[:], op0=ALU.mult, op1=ALU.add))
                    values = scores
            nc.vector.tensor_tensor(both[:], mask[:, 0], mask[:, 1], ALU.add).then_inc(masks_ready, 1)
            if layer == 0:
                nc.vector.tensor_tensor(sh.weight[:, 1], top[:, 1], top[:, 0], ALU.subtract).then_inc(gap_ready, 1)
            dve.wait_ge(ranked, 2)
            link(nc.vector.tensor_copy(total[:], tot_ps[:].rearrange("p t e -> p e t")))
            flat = lambda a: a.rearrange("p e t -> p (e t)")
            link(nc.vector.tensor_tensor_scan(flat(before[:]), flat(run_on[:]), flat(total[:]), 0.0, ALU.mult, ALU.add))
            link(nc.vector.tensor_copy(count[:], before[:, :, TILES - 1]))
            link(nc.vector.tensor_tensor(before[:], before[:], total[:], ALU.subtract))
            link(nc.vector.tensor_tensor(rank[:], tri_ps[:], before[:].rearrange("p e t -> p t e"), ALU.add))
            if layer == 0:
                link(nc.vector.tensor_scalar(count_i[:], count[:], float(P - 1), None, ALU.add))
                link(nc.vector.tensor_scalar(count_i[:], count_i[:], 7, 7, ALU.arith_shift_right, ALU.logical_shift_left))
                link(nc.vector.tensor_copy(padded[:], count_i[:]))
                link(nc.vector.tensor_tensor_scan(ends[:], ones[:, 0:NE], padded[:], 0.0, ALU.mult, ALU.add))
                link(nc.vector.tensor_tensor(offs[:], ends[:], padded[:], ALU.subtract))
                link(nc.vector.tensor_scalar(owner[:], tiles_at[:], ends[:, 0:1], None, ALU.is_ge))
                for e in range(1, NE - 1):
                    link(nc.vector.scalar_tensor_tensor(out=owner[:], in0=tiles_at[:], scalar=ends[:, e:e + 1], in1=owner[:],
                                                        op0=ALU.is_ge, op1=ALU.add))
                link(nc.vector.tensor_copy(sh.owner_i[:], owner[:]))
            link(nc.vector.tensor_tensor(cand[:], rank[:], offs[:].rearrange("p (o e) -> p o e", o=1).broadcast_to([P, TILES, NE]), ALU.add))
            for k in range(2):
                link(nc.vector.tensor_tensor(scores[:], mask[:, k], cand[:], ALU.mult))
                link(nc.vector.tensor_reduce(slot[:, k], scores[:], AX_X, ALU.add))
                if layer == 1:
                    link(nc.vector.tensor_tensor(scores[:], mask[:, k], rank[:], ALU.mult))
                    link(nc.vector.tensor_reduce(valid[:, k], scores[:], AX_X, ALU.add))
            if layer == 1:
                link(nc.vector.tensor_scalar(valid[:], valid[:], float(CAP1), None, ALU.is_lt))
                link(nc.vector.scalar_tensor_tensor(out=slot[:], in0=slot[:], scalar=spare[:, 0:1], in1=valid[:], op0=ALU.subtract, op1=ALU.mult))
                link(nc.vector.tensor_scalar(slot[:], slot[:], spare[:, 0:1], None, ALU.add))
            nc.vector.tensor_copy(sh.slot_of[:], slot[:]).then_inc(slots_ready, 1)
            if layer == 0:
                dve.wait_ge(exp_ready, 1)
                link(nc.vector.tensor_scalar(wsum[:], sh.weight[:, 1], 1.0, None, ALU.add))
                link(nc.vector.reciprocal(sh.weight[:, 0], wsum[:]))
                link(nc.vector.tensor_tensor(sh.weight[:, 1], sh.weight[:, 1], sh.weight[:, 0], ALU.mult))
            else:
                link(nc.vector.tensor_tensor(wsum[:], top[:, 0], top[:, 1], ALU.add))
                link(nc.vector.tensor_scalar(wsum[:], wsum[:], 1e-6, None, ALU.add))
                link(nc.vector.reciprocal(wsum[:], wsum[:]))
                for k in range(2):
                    link(nc.vector.tensor_tensor(sh.weight[:, k], top[:, k], wsum[:], ALU.mult))
                    link(nc.vector.tensor_tensor(sh.weight[:, k], sh.weight[:, k], valid[:, k], ALU.mult))


def phase_experts0(nc, d, sh):
    U = 4
    with ExitStack() as ctx:
        sb = lambda name, shape: ctx.enter_context(nc.sbuf_tensor(f"e0_{name}", shape, F32))
        ps = lambda name, shape: ctx.enter_context(nc.psum_tensor(f"e0_{name}", shape, F32))
        sem = ctx.enter_context(Semaphores(nc, "e0_"))
        w13 = sb("w13", [P, EXPERTS0, 2, KE, H0])
        w2 = sb("w2", [P, EXPERTS0, MH0, E])
        xs = sb("xs", [P, U, E])
        xt = sb("xt", [P, 2, KE, P])
        act_h = sb("act_h", [P, 2, H0])
        prod = sb("prod", [P, 2, H0])
        pt = sb("pt", [P, 2, MH0, P])
        ys = sb("ys", [P, U, E])
        x_ps = ps("x_ps", [P, KE, P])
        h_ps = [ps(f"h_ps{i}", [P, H0]) for i in range(2)]
        g_ps = [ps(f"g_ps{i}", [P, H0]) for i in range(2)]
        p_ps = ps("p_ps", [P, MH0, P])
        y_ps = ps("y_ps", [P, E])
        w_in, x_in, y_out = sem("w_in"), [sem(f"x_in{i}") for i in range(U)], [sem(f"y_out{i}") for i in range(U)]
        x_turned, x_copied, h_done, silu_done, prod_done, p_turned, p_copied, y_done, y_copied = (
            sem(n) for n in "x_turned x_copied h_done silu_done prod_done p_turned p_copied y_done y_copied".split())
        block = ctx.enter_context(nc.Block())
        LOOPS = TILES0 // U
        assert TILES0 % U == 0

        def tiles(eng, body):
            for r in range(U):
                body(r, r, 0)
            with eng.Fori(1, LOOPS - 1) as q:
                for r in range(U):
                    body(q * U + r, r, q)
            for r in range(U):
                body(TILES0 - U + r, r, LOOPS - 1)

        exists = lambda j: not isinstance(j, int) or 0 <= j < TILES0
        early = lambda j, n: isinstance(j, int) and j < n

        @block.sync
        def _(sp):
            for e in range(EXPERTS0):
                for i, name in enumerate(("L0_ffn_W1", "L0_ffn_W3")):
                    sp.dma_start(w13[:, e, i], d[name][e].rearrange("(k p) f -> p k f", p=P)).then_inc(w_in, 16)
                sp.dma_start(w2[:, e], d["L0_ffn_W2"][e].rearrange("(m p) f -> p m f", p=P)).then_inc(w_in, 16)

            def load(j, r):
                if not early(j, U):
                    sp.wait_ge(x_turned, j - U + 1)
                sp.dma_start(xs[:, r], d["slots0"][bass.ds(j * P, P), :]).then_inc(x_in[r], 16)

            def store(j, r):
                sp.wait_ge(y_copied, j + 1)
                sp.dma_start(d["outs0"][bass.ds(j * P, P), :], ys[:, r]).then_inc(y_out[r], 16)

            def body(j, r, q):
                if exists(j + 2):
                    load(j + 2, (r + 2) % U)
                if exists(j - 2):
                    store(j - 2, (r - 2) % U)

            load(0, 0)
            load(1, 1)
            tiles(sp, body)
            store(TILES0 - 2, U - 2)
            store(TILES0 - 1, U - 1)
            for r in range(U):
                sp.wait_ge(y_out[r], 16 * LOOPS + 1)

        @block.tensor
        def _(pe):
            def turn_x(j, r, q):
                pe.wait_ge(x_in[r], q * 16 + 16)
                if not early(j, 1):
                    pe.wait_ge(x_copied, j)
                for k in range(KE):
                    last = nc.tensor.transpose(x_ps[:, k, :], xs[:, r, k * P:(k + 1) * P], sh.ident[:])
                last.then_inc(x_turned, 1)

            def hidden(j, r):
                e = nc.tensor.value_load(sh.owner_i[0:1, bass.ds(j, 1)], min_val=0, max_val=EXPERTS0 - 1)
                pe.wait_ge(x_copied, j + 1)
                if not early(j, 2):
                    pe.wait_ge(prod_done, j - 1)
                for i, out_ps in ((0, h_ps), (1, g_ps)):
                    for k in range(KE):
                        last = nc.tensor.matmul(out_ps[r % 2][:], xt[:, r % 2, k, :], w13[:, e, i, k, :],
                                                start=(k == 0), stop=(k == KE - 1))
                last.then_inc(h_done, 1)

            def turn_p(j, r):
                pe.wait_ge(prod_done, j + 1)
                if not early(j, 1):
                    pe.wait_ge(p_copied, j)
                for m in range(MH0):
                    last = nc.tensor.transpose(p_ps[:, m, :], prod[:, r % 2, m * P:(m + 1) * P], sh.ident[:])
                last.then_inc(p_turned, 1)

            def output(j, r):
                e = nc.tensor.value_load(sh.owner_i[0:1, bass.ds(j, 1)], min_val=0, max_val=EXPERTS0 - 1)
                pe.wait_ge(p_copied, j + 1)
                if not early(j, 1):
                    pe.wait_ge(y_copied, j)
                for m in range(MH0):
                    last = nc.tensor.matmul(y_ps[:], pt[:, r % 2, m, :], w2[:, e, m, :], start=(m == 0), stop=(m == MH0 - 1))
                last.then_inc(y_done, 1)

            def body(j, r, q):
                hidden(j, r)
                if exists(j - 1):
                    turn_p(j - 1, (r - 1) % U)
                if exists(j + 1):
                    turn_x(j + 1, (r + 1) % U, q + (r + 1) // U)
                if exists(j - 2):
                    output(j - 2, (r - 2) % U)

            pe.wait_ge(w_in, 48 * EXPERTS0)
            turn_x(0, 0, 0)
            tiles(pe, body)
            turn_p(TILES0 - 1, U - 1)
            output(TILES0 - 2, U - 2)
            output(TILES0 - 1, U - 1)

        @block.scalar
        def _(act):
            def copy_x(j, r):
                act.wait_ge(x_turned, j + 1)
                if not early(j, 2):
                    act.wait_ge(h_done, j - 1)
                nc.scalar.copy(xt[:, r % 2], x_ps[:]).then_inc(x_copied, 1)

            def silu(j, r):
                act.wait_ge(h_done, j + 1)
                if not early(j, 2):
                    act.wait_ge(prod_done, j - 1)
                nc.scalar.activation(act_h[:, r % 2], h_ps[r % 2][:], ACT.Silu).then_inc(silu_done, 1)

            def copy_y(j, r, q):
                act.wait_ge(y_done, j + 1)
                if not early(j, U):
                    act.wait_ge(y_out[r], q * 16 + 1)
                nc.scalar.copy(ys[:, r], y_ps[:]).then_inc(y_copied, 1)

            def body(j, r, q):
                silu(j, r)
                if exists(j + 1):
                    copy_x(j + 1, (r + 1) % U)
                if exists(j - 2):
                    copy_y(j - 2, (r - 2) % U, q - (1 if r < 2 else 0))

            for r in range(U):
                act.sem_inc(y_out[r], 1)
            copy_x(0, 0)
            tiles(act, body)
            copy_y(TILES0 - 2, U - 2, LOOPS - 1)
            copy_y(TILES0 - 1, U - 1, LOOPS - 1)

        @block.vector
        def _(dve):
            def copy_p(j, r):
                dve.wait_ge(p_turned, j + 1)
                if not early(j, 2):
                    dve.wait_ge(y_done, j - 1)
                nc.vector.tensor_copy(pt[:, r % 2], p_ps[:]).then_inc(p_copied, 1)

            def multiply(j, r):
                dve.wait_ge(silu_done, j + 1)
                if not early(j, 2):
                    dve.wait_ge(p_turned, j - 1)
                nc.vector.tensor_tensor(prod[:, r % 2], act_h[:, r % 2], g_ps[r % 2][:], ALU.mult).then_inc(prod_done, 1)

            def body(j, r, q):
                if exists(j - 1):
                    copy_p(j - 1, (r - 1) % U)
                multiply(j, r)

            tiles(dve, body)
            copy_p(TILES0 - 1, U - 1)


def phase_experts1(nc, d, sh):
    S1 = CAP1 // P
    HALF = CAP1 // 2
    with ExitStack() as ctx:
        sb = lambda name, shape: ctx.enter_context(nc.sbuf_tensor(f"e1_{name}", shape, F32))
        ps = lambda name, shape: ctx.enter_context(nc.psum_tensor(f"e1_{name}", shape, F32))
        sem = ctx.enter_context(Semaphores(nc, "e1_"))
        w1 = sb("w1", [P, 2, KE, F1])
        w2 = sb("w2", [P, 2, MF1, E])
        xs = sb("xs", [P, 2, S1, E])
        xt = sb("xt", [P, KE, CAP1])
        hid = sb("hid", [P, MF1, CAP1])
        ys = sb("ys", [P, 2, S1, E])
        x_ps = [ps(f"x_ps{i}", [P, KE, P]) for i in range(2)]
        h_ps = [ps(f"h_ps{i}", [P, HALF]) for i in range(4)]
        y_ps = [ps(f"y_ps{i}", [P, E]) for i in range(2)]
        w1_in, w2_in, x_in, y_out = ([sem(f"{n}{i}") for i in range(2)] for n in ("w1_in", "w2_in", "x_in", "y_out"))
        x_turned, x_copied, h_done, h_act, y_done, y_copied = (sem(n) for n in "x_turned x_copied h_done h_act y_done y_copied".split())
        block = ctx.enter_context(nc.Block())
        NH = 2 * MF1

        def experts(eng, body):
            for r in range(2):
                body(r, r, 0)
            with eng.Fori(1, EXPERTS1 // 2 - 1) as q:
                for r in range(2):
                    body(q * 2 + r, r, q)
            for r in range(2):
                body(EXPERTS1 - 2 + r, r, EXPERTS1 // 2 - 1)

        exists = lambda e: not isinstance(e, int) or e < EXPERTS1
        early = lambda e, n: isinstance(e, int) and e < n

        @block.sync
        def _(sp):
            def load(e, r, q):
                if not early(e, 2):
                    sp.wait_ge(x_turned, (e - 1) * S1)
                sp.dma_start(xs[:, r], d["slots1"][bass.ds(e * CAP1, CAP1), :].rearrange("(t p) f -> p t f", p=P)).then_inc(x_in[r], 16)
                if not early(e, 2):
                    sp.wait_ge(y_done, (e - 1) * S1)
                one = bass.ds(e, 1)
                sp.dma_start(w1[:, r], d["L1_ffn_w1"][one].rearrange("o (k p) f -> p (o k) f", p=P)).then_inc(w1_in[r], 16)
                sp.dma_start(w2[:, r], d["L1_ffn_w2"][one].rearrange("o (m p) f -> p (o m) f", p=P)).then_inc(w2_in[r], 16)

            def body(e, r, q):
                sp.wait_ge(y_copied, (e + 1) * S1)
                sp.dma_start(d["outs1"][bass.ds(e * CAP1, CAP1), :].rearrange("(t p) f -> p t f", p=P), ys[:, r]).then_inc(y_out[r], 16)
                if exists(e + 2):
                    load(e + 2, r, q + 1)

            load(0, 0, 0)
            load(1, 1, 0)
            experts(sp, body)
            for r in range(2):
                sp.wait_ge(y_out[r], 16 * (EXPERTS1 // 2))

        @block.tensor
        def _(pe):
            def turn_x(e, r, q):
                pe.wait_ge(x_in[r], q * 16 + 16)
                for t in range(S1):
                    if not early(e, 1) or t >= 2:
                        pe.wait_ge(x_copied, e * S1 + t - 1)
                    for k in range(KE):
                        last = nc.tensor.transpose(x_ps[(r + t) % 2][:, k, :], xs[:, r, t, k * P:(k + 1) * P], sh.ident[:])
                    last.then_inc(x_turned, 1)

            def hidden(e, r, q):
                pe.wait_ge(x_copied, (e + 1) * S1)
                pe.wait_ge(w1_in[r], q * 16 + 16)
                for n in range(NH):
                    m, part = n // 2, n % 2
                    if not early(e, 1) or n >= 4:
                        pe.wait_ge(h_act, e * NH + n - 3)
                    for k in range(KE):
                        last = nc.tensor.matmul(h_ps[n % 4][:], w1[:, r, k, m * P:(m + 1) * P],
                                                xt[:, k, part * HALF:(part + 1) * HALF], start=(k == 0), stop=(k == KE - 1))
                    last.then_inc(h_done, 1)

            def output(e, r, q):
                pe.wait_ge(h_act, (e + 1) * NH)
                pe.wait_ge(w2_in[r], q * 16 + 16)
                for t in range(S1):
                    if not early(e, 1) or t >= 2:
                        pe.wait_ge(y_copied, e * S1 + t - 1)
                    for m in range(MF1):
                        last = nc.tensor.matmul(y_ps[(r + t) % 2][:], hid[:, m, t * P:(t + 1) * P], w2[:, r, m, :],
                                                start=(m == 0), stop=(m == MF1 - 1))
                    last.then_inc(y_done, 1)

            def body(e, r, q):
                hidden(e, r, q)
                if exists(e + 1):
                    turn_x(e + 1, 1 - r, q + r)
                output(e, r, q)

            turn_x(0, 0, 0)
            experts(pe, body)

        @block.scalar
        def _(act):
            def body(e, r, q):
                for n in range(NH):
                    m, part = n // 2, n % 2
                    act.wait_ge(h_done, e * NH + n + 1)
                    if n == 0 and not early(e, 1):
                        act.wait_ge(y_done, e * S1)
                    nc.scalar.activation(hid[:, m, part * HALF:(part + 1) * HALF], h_ps[n % 4][:], ACT.Gelu).then_inc(h_act, 1)

            experts(act, body)

        @block.vector
        def _(dve):
            def copy_x(e, r):
                for t in range(S1):
                    dve.wait_ge(x_turned, e * S1 + t + 1)
                    if t == 0 and not early(e, 1):
                        dve.wait_ge(h_done, e * NH)
                    nc.vector.tensor_copy(xt[:, :, t * P:(t + 1) * P], x_ps[(r + t) % 2][:]).then_inc(x_copied, 1)

            def body(e, r, q):
                if exists(e + 1):
                    copy_x(e + 1, 1 - r)
                for t in range(S1):
                    dve.wait_ge(y_done, e * S1 + t + 1)
                    if t == 0 and not early(e, 2):
                        dve.wait_ge(y_out[r], q * 16)
                    nc.vector.tensor_copy(ys[:, r, t, :], y_ps[(r + t) % 2][:]).then_inc(y_copied, 1)

            copy_x(0, 0)
            experts(dve, body)


def phase_combine(nc, d, sh, layer, outs_name):
    R = 4
    with ExitStack() as ctx:
        sb = lambda name, shape: ctx.enter_context(nc.sbuf_tensor(f"cb{layer}_{name}", shape, F32))
        sem = ctx.enter_context(Semaphores(nc, f"cb{layer}_"))
        y = sb("y", [P, R, 2, E])
        tmp = sb("tmp", [P, 2, E])
        gathered = [sem(f"gathered{r}") for r in range(R)]
        x_ready, chain = sem("x_ready"), sem("chain")
        out_stored = sem("out_stored")
        block = ctx.enter_context(nc.Block())

        @block.gpsimd
        def _(pool):
            for i in range(TILES):
                if i >= R:
                    pool.wait_ge(x_ready, i - R + 1)
                for k in range(2):
                    nc.gpsimd.indirect_dma_start(out=y[:, i % R, k, :], out_offset=None, in_=d[outs_name],
                                                 in_offset=bass.IndirectOffsetOnAxis(ap=sh.slot_of[:, k, i:i + 1], axis=0)
                                                 ).then_inc(gathered[i % R], 16)

        @block.vector
        def _(dve):
            with dve.Fori(0, B) as b:
                for j in range(TPB):
                    tile, r, t = b * TPB + j, j % R, tmp[:, j % 2, :]
                    dve.wait_ge(gathered[r], b * (32 * TPB // R) + 32 * (j // R + 1))
                    nc.vector.tensor_scalar(t, y[:, r, 0, :], sh.weight[:, 0, bass.ds(tile, 1)], None, ALU.mult).then_inc(chain, 1)
                    dve.wait_ge(chain, tile * 3 + 1)
                    nc.vector.scalar_tensor_tensor(out=t, in0=y[:, r, 1, :], scalar=sh.weight[:, 1, bass.ds(tile, 1)], in1=t,
                                                   op0=ALU.mult, op1=ALU.add).then_inc(chain, 1)
                    dve.wait_ge(chain, tile * 3 + 2)
                    nc.vector.tensor_tensor(t, t, sh.mods[:, 2, b, :], ALU.mult).then_inc(chain, 1)
                    dve.wait_ge(chain, tile * 3 + 3)
                    nc.vector.tensor_tensor(sh.x[:, tile, :], sh.x[:, tile, :], t, ALU.add).then_inc(x_ready, 1)
                    dve.wait_ge(x_ready, tile + 1)
                    if layer == 0:
                        nc.vector.bn_stats(sh.stats[:, tile, :], sh.x[:, tile, :])

        if layer == 1:
            @block.sync
            def _(sp):
                out = token_tiles(d["out"])
                for b in range(B):
                    sp.wait_ge(x_ready, (b + 1) * TPB)
                    sp.dma_start(out[:, b * TPB:(b + 1) * TPB], sh.x[:, b * TPB:(b + 1) * TPB]).then_inc(out_stored, 16)
                sp.wait_ge(out_stored, 16 * B)


def phase_attention(nc, d, sh):
    SCALE = float(1.0 / np.sqrt(np.float32(DH)))
    N = HEADS * TPB
    QK = 2 * CPB
    with ExitStack() as ctx:
        sb = lambda name, shape: ctx.enter_context(nc.sbuf_tensor(f"at_{name}", shape, F32))
        ps = lambda name, shape: ctx.enter_context(nc.psum_tensor(f"at_{name}", shape, F32))
        sem = ctx.enter_context(Semaphores(nc, "at_"))
        w_qkv = sb("w_qkv", [P, KE, HEADS, 3, DH])
        w_o = sb("w_o", [P, HEADS, E])
        pos = sb("pos", [P, T])
        hidden_pos = sb("later", [P, P])
        h_b = sb("h_b", [P, CPB, KE, CH])
        v = sb("v", [P, TPB, HEADS, DH])
        qk = sb("qk", [P, 2, 2, T])
        probs = sb("probs", [P, 4, T])
        pt = sb("pt", [P, 2, TPB, P])
        attn = sb("attn", [P, HEADS, T])
        small = sb("small", [P, 4, 4])
        gated = sb("gated", [P, 2, E])
        s_ps = [ps(f"s_ps{i}", [P, T]) for i in range(2)]
        pt_ps = [ps(f"pt_ps{i}", [P, CT, P]) for i in range(2)]
        o_ps = ps("o_ps", [P, P])
        qk_ps = ps("qk_ps", [P, CH])
        names = ("w_in h_in later_set v_done v_copied qk_done qk_ready scored masked max_taken bias_ready exp_done inverted "
                 "normed turned0 turned1 copied0 copied1 pv_done attn_ready out_done out_added chain").split()
        S = {n: sem(n) for n in names}
        block = ctx.enter_context(nc.Block())

        @block.sync
        def _(sp):
            sp.dma_start(w_qkv[:], d["wqkvT"].rearrange("(k p) (h c f) -> p k h c f", p=P, h=HEADS, c=3)).then_inc(S["w_in"], 16)
            sp.dma_start(w_o[:], d["woT"].rearrange("(h p) e -> p h e", p=P)).then_inc(S["w_in"], 16)
            sp.dma_start(pos[:], d["posT"]).then_inc(S["w_in"], 16)
            with sp.Fori(0, B) as b:
                sp.wait_ge(S["qk_done"], b * (HEADS * QK) + 1)
                for th in range(CPB):
                    sp.dma_start(h_b[:, th], d["h_turned"][bass.ds(b * CPB + th, 1)].rearrange("o p k t -> (o p) k t")).then_inc(S["h_in"], 16)

        @block.gpsimd
        def _(pool):
            nc.gpsimd.memset(hidden_pos[:], 0.0).then_inc(S["later_set"], 1)
            pool.wait_ge(S["later_set"], 1)
            nc.gpsimd.affine_select(out=hidden_pos[:], in_=hidden_pos[:], compare_op=ALU.is_ge, fill=-3e38, base=0,
                                    pattern=[[-1, P]], channel_multiplier=1).then_inc(S["later_set"], 1)

        def bank(n):
            return s_ps[n // 2 % 2][:, (n % 2) * CH:(n % 2 + 1) * CH]

        @block.tensor
        def _(pe):
            for name in ("qk_done", "qk_ready", "out_added", "pv_done", "attn_ready", "copied0", "copied1"):
                pe.sem_inc(S[name], 1)
            pe.wait_ge(S["w_in"], 48)
            with pe.Fori(0, B) as b:
                def values(n):
                    t, part = n // 2, n % 2
                    if n >= 4:
                        pe.wait_ge(S["v_copied"], b * 16 + n - 3)
                    for k in range(KE):
                        last = nc.tensor.matmul(bank(n), h_b[:, t // CT, k, (t % CT) * P:(t % CT + 1) * P],
                                                w_qkv[:, k, part * 4:part * 4 + 4, 2, :], start=(k == 0), stop=(k == KE - 1))
                    last.then_inc(S["v_done"], 1)

                def project(h, i):
                    pe.wait_ge(S["qk_ready"], b * (HEADS * QK) + h * QK + i + 1)
                    for k in range(KE):
                        last = nc.tensor.matmul(qk_ps[:], w_qkv[:, k, h, i // 2, :], h_b[:, i % 2, k, :], start=(k == 0), stop=(k == KE - 1))
                    last.then_inc(S["qk_done"], 1)

                def score(n):
                    h, i = n // TPB, n % TPB
                    if i == 0:
                        pe.wait_ge(S["qk_ready"], b * (HEADS * QK) + (h + 1) * QK + 1)
                    if n >= 2:
                        pe.wait_ge(S["exp_done"], b * N + n - 1)
                    for part in range(i // CT + 1):
                        end = min((i + 1) * P, (part + 1) * CH)
                        last = nc.tensor.matmul(s_ps[n % 2][:, part * CH:end], qk[:, h % 2, 0, i * P:(i + 1) * P],
                                                qk[:, h % 2, 1, part * CH:end], start=True, stop=True)
                    last.then_inc(S["scored"], 1)

                def turn(n):
                    i = n % TPB
                    pe.wait_ge(S["normed"], b * N + n + 1)
                    for half in range(i // CT + 1):
                        pe.wait_ge(S[f"copied{half}"], (b * N + n + 1) if half == 0 else (b * (N // 2) + n // TPB * CT + i - CT + 1))
                        for j in range(half * CT, min(i + 1, (half + 1) * CT)):
                            last = nc.tensor.transpose(pt_ps[half][:, j % CT, :], probs[:, n % 4, j * P:(j + 1) * P], sh.ident[:])
                        last.then_inc(S[f"turned{half}"], 1)

                def weigh(n):
                    h, i = n // TPB, n % TPB
                    pe.wait_ge(S["copied0"], b * N + n + 2)
                    if i >= CT:
                        pe.wait_ge(S["copied1"], b * (N // 2) + h * CT + i - CT + 2)
                    pe.wait_ge(S["attn_ready"], b * N + n + 1)
                    for j in range(i + 1):
                        last = nc.tensor.matmul(o_ps[:], v[:, j, h, :], pt[:, n % 2, j, :], start=(j == 0), stop=(j == i))
                    last.then_inc(S["pv_done"], 1)

                def output(t):
                    if t >= 4:
                        pe.wait_ge(S["out_added"], b * TPB + t - 2)
                    for h in range(HEADS):
                        last = nc.tensor.matmul(bank(t)[:, 0:E], attn[:, h, t * P:(t + 1) * P], w_o[:, h, :],
                                                start=(h == 0), stop=(h == HEADS - 1))
                    last.then_inc(S["out_done"], 1)

                pe.wait_ge(S["h_in"], b * (16 * CPB) + 16 * CPB)
                pe.wait_ge(S["out_added"], b * TPB + 1)
                for n in range(2 * TPB):
                    values(n)
                for i in range(QK):
                    project(0, i)
                pe.wait_ge(S["v_copied"], b * 16 + 16)
                for n in range(N + 2):
                    if n >= 2:
                        turn(n - 2)
                    if n < N:
                        score(n)
                        if n % 2 == 1 and n // TPB + 1 < HEADS:
                            project(n // TPB + 1, n % TPB // 2)
                    if n >= 2:
                        weigh(n - 2)
                pe.wait_ge(S["attn_ready"], b * N + N + 1)
                for t in range(TPB):
                    output(t)

        @block.scalar
        def _(act):
            with act.Fori(0, B) as b:
                def exponential(n):
                    i = n % TPB
                    act.wait_ge(S["bias_ready"], b * N + n + 1)
                    if n >= 4:
                        act.wait_ge(S[f"turned{(n - 4) % TPB // CT}"],
                                    (b * N + n - 3) if (n - 4) % TPB < CT else (b * (N // 2) + (n - 4) // TPB * CT + (n - 4) % TPB - CT + 1))
                    nc.scalar.activation(probs[:, n % 4, 0:(i + 1) * P], s_ps[n % 2][:, 0:(i + 1) * P], ACT.Exp,
                                         bias=small[:, n % 4, 1:2], scale=SCALE, accum_out=small[:, n % 4, 2:3]).then_inc(S["exp_done"], 1)

                def copy_turned(n):
                    i = n % TPB
                    for half in range(i // CT + 1):
                        m = min(i + 1, (half + 1) * CT) - half * CT
                        act.wait_ge(S[f"turned{half}"], (b * N + n + 1) if half == 0 else (b * (N // 2) + n // TPB * CT + i - CT + 1))
                        if n >= 2 and half == 0:
                            act.wait_ge(S["pv_done"], b * N + n)
                        nc.scalar.copy(pt[:, n % 2, half * CT:half * CT + m, :], pt_ps[half][:, 0:m, :]).then_inc(S[f"copied{half}"], 1)

                act.wait_ge(S["pv_done"], b * N + 1)
                for n in range(2 * TPB):
                    act.wait_ge(S["v_done"], b * 16 + n + 1)
                    nc.scalar.copy(v[:, n // 2, (n % 2) * 4:(n % 2) * 4 + 4, :], bank(n)).then_inc(S["v_copied"], 1)
                for n in range(N + 2):
                    if n >= 2:
                        copy_turned(n - 2)
                    if n < N:
                        exponential(n)

        @block.vector
        def _(dve):
            dve.wait_ge(S["w_in"], 48)
            dve.wait_ge(S["later_set"], 2)
            with dve.Fori(0, B) as b:
                def add_pos(h, i):
                    dve.wait_ge(S["qk_done"], b * (HEADS * QK) + h * QK + i + 2)
                    if i == 0 and h >= 2:
                        dve.wait_ge(S["scored"], b * N + (h - 1) * TPB)
                    nc.vector.tensor_tensor(qk[:, h % 2, i // 2, (i % 2) * CH:(i % 2 + 1) * CH], qk_ps[:],
                                            pos[:, (i % 2) * CH:(i % 2 + 1) * CH], ALU.add).then_inc(S["qk_ready"], 1)

                def maximum(n):
                    i = n % TPB
                    diagonal = s_ps[n % 2][:, i * P:(i + 1) * P]
                    dve.wait_ge(S["scored"], b * N + n + 1)
                    nc.vector.tensor_tensor(diagonal, diagonal, hidden_pos[:], ALU.add).then_inc(S["masked"], 1)
                    dve.wait_ge(S["masked"], b * N + n + 1)
                    nc.vector.reduce_max(small[:, n % 4, 0:1], s_ps[n % 2][:, 0:(i + 1) * P], AX_X).then_inc(S["max_taken"], 1)
                    dve.wait_ge(S["max_taken"], b * N + n + 1)
                    nc.vector.tensor_scalar(small[:, n % 4, 1:2], small[:, n % 4, 0:1], -SCALE, None, ALU.mult).then_inc(S["bias_ready"], 1)

                def normalise(n):
                    i = n % TPB
                    dve.wait_ge(S["exp_done"], b * N + n + 1)
                    nc.vector.reciprocal(small[:, n % 4, 3:4], small[:, n % 4, 2:3]).then_inc(S["inverted"], 1)
                    dve.wait_ge(S["inverted"], b * N + n + 1)
                    row = probs[:, n % 4, 0:(i + 1) * P]
                    nc.vector.tensor_scalar(row, row, small[:, n % 4, 3:4], None, ALU.mult).then_inc(S["normed"], 1)

                def keep(n):
                    h, i = n // TPB, n % TPB
                    dve.wait_ge(S["pv_done"], b * N + n + 2)
                    nc.vector.tensor_copy(attn[:, h, i * P:(i + 1) * P], o_ps[:]).then_inc(S["attn_ready"], 1)

                for i in range(QK):
                    add_pos(0, i)
                for n in range(N + 3):
                    if n < N:
                        maximum(n)
                    if 1 <= n <= N:
                        normalise(n - 1)
                    if n < N and n % 2 == 1 and n // TPB + 1 < HEADS:
                        add_pos(n // TPB + 1, n % TPB // 2)
                    if n >= 3:
                        keep(n - 3)
                for t in range(TPB):
                    tile = b * TPB + t
                    dve.wait_ge(S["out_done"], tile + 1)
                    nc.vector.tensor_tensor(gated[:, t % 2, :], bank(t)[:, 0:E], sh.mods[:, 2, b, :], ALU.mult).then_inc(S["out_added"], 1)
                    dve.wait_ge(S["out_added"], tile + 2)
                    nc.vector.tensor_tensor(sh.x[:, tile, :], sh.x[:, tile, :], gated[:, t % 2, :], ALU.add).then_inc(S["chain"], 1)
                    dve.wait_ge(S["chain"], tile + 1)
                    nc.vector.bn_stats(sh.stats[:, tile, :], sh.x[:, tile, :])


def store_x(nc, d, sh):
    with ExitStack() as ctx:
        stored = ctx.enter_context(nc.semaphore("stored"))
        block = ctx.enter_context(nc.Block())

        @block.sync
        def _(sp):
            sp.dma_start(token_tiles(d["out"]), sh.x[:]).then_inc(stored, 16)
            sp.wait_ge(stored, 16)


def program(nc, d, stop=99):
    sh = Shared()
    with ExitStack() as ctx:
        sb = lambda name, shape, dt=F32: ctx.enter_context(nc.sbuf_tensor(name, shape, dt))
        sh.x = sb("x", [P, TILES, E])
        sh.mods = sb("mods", [P, 3, B, E])
        sh.ident = sb("ident", [P, P])
        sh.zeros = sb("zeros", [P, E])
        sh.stats = sb("stats", [P, TILES, 6])
        sh.mean, sh.var, sh.rstd, sh.dif = (sb(name, [P, TILES]) for name in ("mean", "var", "rstd", "dif"))
        sh.slot_of = sb("slot_of", [P, 2, TILES], U32)
        sh.weight = sb("weight", [P, 2, TILES])
        sh.owner_i = sb("owner_i", [P, TILES0], I32)
        with ExitStack() as layer:
            sl = lambda name, shape: layer.enter_context(nc.sbuf_tensor(name, shape, F32))
            sh.w_in = sl("w_in", [P, KE, 2 * DI])
            sh.w_out = sl("w_out", [P, MD, E])
            sh.w_x = sl("w_x", [P, MD, 1 + 2 * NS])
            sh.w_delta = sl("w_delta", [P, MD, P])
            sh.conv_w = sl("conv_w", [P, MD, DC])
            sh.vecs = sl("inner_vecs", [P, 4, MD])
            sh.a_neg = sl("a_neg", [P, MD, NS])
            phase_prepare(nc, d, sh)
            phase_norm_turn(nc, d, sh, 0)
            phase_mamba(nc, d, sh)
        if stop >= 2:
            phase_route(nc, d, sh, 0, "L0_ffn_Wr", "slots0")
            phase_experts0(nc, d, sh)
            phase_combine(nc, d, sh, 0, "outs0")
        if stop >= 3:
            phase_norm_turn(nc, d, sh, 1)
            phase_attention(nc, d, sh)
        if stop >= 4:
            phase_route(nc, d, sh, 1, "gate_wT", "slots1")
            phase_experts1(nc, d, sh)
            phase_combine(nc, d, sh, 1, "outs1")
        if stop < 4:
            store_x(nc, d, sh)


_PLAIN = ["L0_attn_x", "L0_attn_W_in", "L0_attn_conv_w", "L0_attn_W_x", "L0_attn_A_log", "L0_attn_W_out", "L0_wmod", "L1_wmod",
          "L0_ffn_Wr", "L0_ffn_W1", "L0_ffn_W2", "L0_ffn_W3", "L1_ffn_w1", "L1_ffn_w2"]
_SCRATCH = {
    "mod_rows": [2, 6, B, E],
    "h_turned": [B * CPB, P, KE, CH],
    "bc_rows": [B * CPB, 2 * NS, CH],
    "slots0": [SLOTS0, E],
    "outs0": [SLOTS0, E],
    "slots1": [SLOTS1, E],
    "outs1": [SLOTS1, E],
}


def lay_out(inputs):
    get = lambda n: np.asarray(inputs[n])
    arrays = {n: np.ascontiguousarray(get(n)) for n in _PLAIN}
    cs = np.stack([get("L0_c"), get("L1_c")])
    arrays["cT"] = np.ascontiguousarray(cs.reshape(2, B, KE, P).transpose(3, 0, 2, 1))
    vecs = np.stack([get("L0_attn_conv_b"), get("L0_attn_dt_w"), get("L0_attn_dt_b"), get("L0_attn_D")])
    arrays["vecs"] = np.ascontiguousarray(vecs.reshape(4, MD, P).transpose(2, 0, 1))
    arrays["wqkvT"] = np.ascontiguousarray(get("L1_attn_Wqkv").T)
    arrays["woT"] = np.ascontiguousarray(get("L1_attn_Wo").T)
    arrays["gate_wT"] = np.ascontiguousarray(get("L1_ffn_gate_w").T)
    arrays["posT"] = positions()
    return arrays


def positions():
    t = np.arange(T, dtype=np.float32)[:, None]
    div = np.exp(np.arange(0, DH, 2, dtype=np.float32) * np.float32(-np.log(10000.0) / DH))
    angle = t * div
    return np.ascontiguousarray(np.stack([np.sin(angle), np.cos(angle)], axis=-1).reshape(T, DH).T)


def declare(nc, arrays):
    d = {n: nc.dram_tensor(n, list(a.shape), F32, kind="ExternalInput").ap() for n, a in arrays.items()}
    for n, shape in _SCRATCH.items():
        d[n] = nc.dram_tensor(n, shape, F32).ap()
    d["out"] = nc.dram_tensor("out", [B, T, E], F32, kind="ExternalOutput").ap()
    return d


def kernel(**inputs):
    import concourse.bacc as bacc
    from concourse.bass_utils import run_bass_kernel_spmd

    nc = bacc.Bacc("TRN2", target_bir_lowering=False, num_devices=1)
    arrays = lay_out(inputs)
    program(nc, declare(nc, arrays))
    return run_bass_kernel_spmd(nc, [arrays], core_ids=[0]).results[0]["out"]
```

```python
from contextlib import ExitStack

import numpy as np

import concourse.bass as bass
from concourse import mybir

ALU = mybir.AluOpType
ACT = mybir.ActivationFunctionType
F32 = mybir.dt.float32
U32, I32 = mybir.dt.uint32, mybir.dt.int32
AX_X = mybir.AxisListType.X

P = 128
B, T, E = 4, 1024, 256
TILES = B * T // P
TPB = T // P
KE = E // P
EPS_LN = 1e-5

DI, NS, DC = 512, 16, 4
MD = DI // P
CH = 512
CPB = T // CH
CT = CH // P
G = 2
NG = NS // G
STEPS = NG * MD
RING, RING_A, RING_B = 4, 8, 2

EXPERTS0, H0 = 8, 384
MH0 = H0 // P
SLOTS0 = 2 * B * T + EXPERTS0 * P
TILES0 = SLOTS0 // P

HEADS, DH = 8, 128
EXPERTS1, F1 = 16, 512
MF1 = F1 // P
CAP1 = int(1.25 * B * T * 2 / EXPERTS1)
SLOTS1 = EXPERTS1 * CAP1 + P
FILL0, FILL1 = TILES0 // (B * CPB), EXPERTS1 * CAP1 // P // (B * CPB)


def token_tiles(ap):
    return ap.rearrange("b (j p) e -> p (b j) e", p=P)


class Shared:
    pass


class Semaphores:

    def __init__(self, nc, prefix):
        self.nc, self.prefix, self.taken = nc, prefix, []

    def __enter__(self):
        return self

    def __call__(self, name):
        self.taken.append(self.nc.alloc_semaphore(self.prefix + name))
        return self.taken[-1]

    def __exit__(self, *failure):
        if not any(failure):
            self.nc.clear_and_free_semaphores(self.taken)
            self.nc.all_engine_barrier()


def link_on(eng, sem):
    count = [0]

    def link(ins):
        count[0] += 1
        ins.then_inc(sem, 1)
        eng.wait_ge(sem, count[0])

    return link


def phase_prepare(nc, d, sh):
    with ExitStack() as ctx:
        sb = lambda name, shape: ctx.enter_context(nc.sbuf_tensor(name, shape, F32))
        sem = ctx.enter_context(Semaphores(nc, "prep_"))
        wmod = sb("wmod", [P, 2, KE, 6 * E])
        c_t = sb("c_t", [P, 2, KE, B])
        c_act = sb("c_act", [P, 2, KE, B])
        rows = sb("rows", [P, 2, 6, E])
        sign = sb("sign", [P, E])
        a_log = sb("a_log", [P, MD, NS])
        mod_ps = ctx.enter_context(nc.psum_tensor("mod_ps", [P, 2, 3, 512], F32))
        c_in, wmod_in, a_in, x_in = sem("c_in"), [sem("wmod0_in"), sem("wmod1_in")], sem("a_in"), [sem(f"x{b}_in") for b in range(B)]
        small_in, c_ready, mod_done, a_exp = sem("small_in"), sem("c_ready"), sem("mod_done"), sem("a_exp")
        rows_ready, rows_out, chain = sem("rows_ready"), sem("rows_out"), sem("chain")
        ident_set, wx_set = sem("ident_set"), sem("wx_set")
        block = ctx.enter_context(nc.Block())

        @block.sync
        def _(sp):
            sp.dma_start(c_t[:], d["cT"]).then_inc(c_in, 16)
            for l, name in enumerate(("L0_wmod", "L1_wmod")):
                sp.dma_start(wmod[:, l], d[name].rearrange("(k p) f -> p k f", p=P)).then_inc(wmod_in[l], 16)
            sp.dma_start(a_log[:], d["L0_attn_A_log"].rearrange("(m p) n -> p m n", p=P)).then_inc(a_in, 16)
            xt = token_tiles(d["L0_attn_x"])
            for b in range(B):
                sp.dma_start(sh.x[:, b * TPB:(b + 1) * TPB], xt[:, b * TPB:(b + 1) * TPB]).then_inc(x_in[b], 16)
            for dst, src in (
                (sh.w_in[:], d["L0_attn_W_in"].rearrange("(k p) f -> p k f", p=P)),
                (sh.w_out[:], d["L0_attn_W_out"].rearrange("(k p) f -> p k f", p=P)),
                (sh.w_x[:], d["L0_attn_W_x"].rearrange("(k p) f -> p k f", p=P)),
                (sh.conv_w[:], d["L0_attn_conv_w"].rearrange("(m p) j -> p m j", p=P)),
                (sh.vecs[:], d["vecs"]),
            ):
                sp.dma_start(dst, src).then_inc(small_in, 16)
            sp.wait_ge(rows_ready, 1)
            sp.dma_start(d["mod_rows"].rearrange("l j b e -> b l j e"), rows[0:B]).then_inc(rows_out, 16)
            sp.wait_ge(rows_out, 16)
            sp.wait_ge(small_in, 80)

        @block.gpsimd
        def _(pool):
            nc.gpsimd.memset(sh.zeros[:], 0.0)
            nc.gpsimd.memset(sh.ident[:], 0.0).then_inc(ident_set, 1)
            pool.wait_ge(ident_set, 1)
            nc.gpsimd.affine_select(out=sh.ident[:], in_=sh.ident[:], compare_op=ALU.not_equal, fill=1.0, base=0,
                                    pattern=[[-1, P]], channel_multiplier=1).then_inc(ident_set, 1)

        @block.scalar
        def _(act):
            act.wait_ge(c_in, 16)
            nc.scalar.activation(c_act[:], c_t[:], ACT.Silu).then_inc(c_ready, 1)
            act.wait_ge(a_in, 16)
            nc.scalar.activation(a_log[:], a_log[:], ACT.Exp).then_inc(a_exp, 1)

        @block.tensor
        def _(pe):
            pe.wait_ge(c_ready, 1)
            for l in range(2):
                pe.wait_ge(wmod_in[l], 16)
                for n in range(3):
                    for k in range(KE):
                        last = nc.tensor.matmul(mod_ps[0:B, l, n, :], c_act[:, l, k, :], wmod[:, l, k, n * 512:(n + 1) * 512],
                                                start=(k == 0), stop=(k == KE - 1))
                last.then_inc(mod_done, 1)

        @block.vector
        def _(dve):
            link = link_on(dve, chain)
            dve.wait_ge(a_exp, 1)
            nc.vector.tensor_scalar(sh.a_neg[:], a_log[:], -1.0, None, ALU.mult)
            for l in range(2):
                dve.wait_ge(mod_done, l + 1)
                for j in range(6):
                    src = mod_ps[0:B, l, j // 2, (j % 2) * E:(j % 2 + 1) * E]
                    dst = rows[0:B, l, j, :]
                    if j % 3 == 0:
                        last = nc.vector.tensor_copy(dst, src)
                    elif j % 3 == 1:
                        last = nc.vector.tensor_scalar(dst, src, 1.0, None, ALU.add)
                    else:
                        link(nc.vector.tensor_scalar(sign[0:B], src, 0.0, 2.0, ALU.is_ge, ALU.mult))
                        link(nc.vector.tensor_scalar(sign[0:B], sign[0:B], 1.0, None, ALU.subtract))
                        link(nc.vector.tensor_copy(dst, src))
                        link(nc.vector.scalar_tensor_tensor(out=dst, in0=dst, scalar=-1.0, in1=dst, op0=ALU.mult, op1=ALU.max))
                        link(nc.vector.tensor_scalar(dst, dst, 0.25, None, ALU.max))
                        link(nc.vector.tensor_tensor(dst, dst, sign[0:B], ALU.mult))
            dve.sem_inc(rows_ready, 1)
            for b in range(B):
                dve.wait_ge(x_in[b], 16)
                for i in range(b * TPB, (b + 1) * TPB):
                    nc.vector.bn_stats(sh.stats[:, i, :], sh.x[:, i, :])
            dve.wait_ge(small_in, 80)
            for k in range(MD):
                last = nc.vector.tensor_copy(sh.w_delta[:, k, :], sh.w_x[:, k, 0:1].broadcast_to([P, P]))
            last.then_inc(wx_set, 1)


def finish_stats(nc, dve, link, sh, std_ready, rstd_wait):
    s = sh.stats
    link(nc.vector.tensor_tensor(sh.mean[:], s[:, :, 1], s[:, :, 4], ALU.add))
    link(nc.vector.tensor_scalar(sh.mean[:], sh.mean[:], 0.5, None, ALU.mult))
    link(nc.vector.tensor_tensor(sh.dif[:], s[:, :, 1], s[:, :, 4], ALU.subtract))
    link(nc.vector.tensor_tensor(sh.dif[:], sh.dif[:], sh.dif[:], ALU.mult))
    link(nc.vector.tensor_tensor(sh.var[:], s[:, :, 2], s[:, :, 5], ALU.add))
    link(nc.vector.tensor_scalar(sh.dif[:], sh.dif[:], 0.25, EPS_LN, ALU.mult, ALU.add))
    nc.vector.scalar_tensor_tensor(out=sh.var[:], in0=sh.var[:], scalar=1.0 / E, in1=sh.dif[:],
                                   op0=ALU.mult, op1=ALU.add).then_inc(std_ready, 1)
    dve.wait_ge(rstd_wait, 1)
    link(nc.vector.reciprocal(sh.rstd[:], sh.var[:]))


def load_mods(sp, d, sh, layer, part, mods_in):
    sp.dma_start(sh.mods[:], d["mod_rows"][layer, 3 * part:3 * part + 3].partition_broadcast(P)).then_inc(mods_in, 16)


def norm_rows(nc, dve, sh, half, rows, half_ready, row_ready, rows_freed):
    ring = rows.shape[1]
    with dve.Fori(0, B) as b:
        def first_half(j):
            tile = b * TPB + j
            dve.wait_ge(row_ready, tile + 1)
            nc.vector.scalar_tensor_tensor(out=half[:, j % 4, :], in0=sh.x[:, tile, :], scalar=sh.mean[:, bass.ds(tile, 1)],
                                           in1=sh.mods[:, 1, b, :], op0=ALU.subtract, op1=ALU.mult).then_inc(half_ready, 1)

        def second_half(j):
            tile = b * TPB + j
            dve.wait_ge(half_ready, b * TPB + j + 1)
            rows_freed(b, j)
            nc.vector.scalar_tensor_tensor(out=rows[:, j % ring, :], in0=half[:, j % 4, :], scalar=sh.rstd[:, bass.ds(tile, 1)],
                                           in1=sh.mods[:, 0, b, :], op0=ALU.mult, op1=ALU.add).then_inc(row_ready, 1)

        first_half(0)
        for j in range(1, TPB):
            first_half(j)
            second_half(j - 1)
        second_half(TPB - 1)


def phase_norm_turn(nc, d, sh, layer):
    with ExitStack() as ctx:
        sb = lambda name, shape: ctx.enter_context(nc.sbuf_tensor(f"nt{layer}_{name}", shape, F32))
        sem = ctx.enter_context(Semaphores(nc, f"nt{layer}_"))
        half = sb("half", [P, 4, E])
        h_row = sb("h_row", [P, 4, E])
        h_chunk = sb("h_chunk", [P, CPB, KE, CH])
        turned = [ctx.enter_context(nc.psum_tensor(f"nt{layer}_turned{i}", [P, KE, P], F32)) for i in range(4)]
        mods_in, var_ready, std_ready, chain = sem("mods_in"), sem("var_ready"), sem("std_ready"), sem("chain")
        half_ready, row_ready, turn_done, turn_copied = sem("half_ready"), sem("row_ready"), sem("turn_done"), sem("turn_copied")
        stored = [sem(f"stored{i}") for i in range(CPB)]
        block = ctx.enter_context(nc.Block())

        @block.sync
        def _(sp):
            load_mods(sp, d, sh, layer, 0, mods_in)
            with sp.Fori(0, B) as b:
                for th in range(CPB):
                    sp.wait_ge(turn_copied, b * TPB + (th + 1) * CT + 4)
                    sp.dma_start(d["h_turned"][bass.ds(b * CPB + th, 1)].rearrange("o p k t -> (o p) k t"),
                                 h_chunk[:, th]).then_inc(stored[th], 16)
            for th in range(CPB):
                sp.wait_ge(stored[th], 16 * B + 1)

        @block.scalar
        def _(act):
            act.wait_ge(var_ready, 1)
            nc.scalar.activation(sh.var[:], sh.var[:], ACT.Sqrt).then_inc(std_ready, 1)
            with act.Fori(0, B) as b:
                for j in range(TPB):
                    if j % CT == 0:
                        act.wait_ge(stored[j // CT], b * 16 + 1)
                    act.wait_ge(turn_done, b * TPB + j + 5)
                    nc.scalar.copy(h_chunk[:, j // CT, :, (j % CT) * P:(j % CT + 1) * P], turned[j % 4][:]).then_inc(turn_copied, 1)

        @block.tensor
        def _(pe):
            pe.sem_inc(turn_done, 4)
            pe.sem_inc(turn_copied, 4)
            pe.sem_inc(row_ready, 4)
            for th in range(CPB):
                pe.sem_inc(stored[th], 1)
            with pe.Fori(0, B) as b:
                for j in range(TPB):
                    pe.wait_ge(row_ready, b * TPB + j + 5)
                    pe.wait_ge(turn_copied, b * TPB + j + 1)
                    for k in range(KE):
                        last = nc.tensor.transpose(turned[j % 4][:, k, :], h_row[:, j % 4, k * P:(k + 1) * P], sh.ident[:])
                    last.then_inc(turn_done, 1)

        @block.vector
        def _(dve):
            link = link_on(dve, chain)
            finish_stats(nc, dve, link, sh, var_ready, std_ready)
            dve.wait_ge(mods_in, 16)
            norm_rows(nc, dve, sh, half, h_row, half_ready, row_ready, lambda b, j: dve.wait_ge(turn_done, b * TPB + j + 1))


def phase_mamba(nc, d, sh):
    with ExitStack() as ctx:
        sb = lambda name, shape: ctx.enter_context(nc.sbuf_tensor(name, shape, F32))
        ps = lambda name, shape: ctx.enter_context(nc.psum_tensor(name, shape, F32))
        sem = ctx.enter_context(Semaphores(nc, "ss_"))
        x_main = sb("x_main", [P, 2, DC - 1 + CH])
        tail = sb("tail", [P, MD, DC - 1])
        x_conv = sb("x_conv", [P, 2, MD, CH])
        gate = sb("gate", [P, 2, MD, CH])
        delta = sb("delta", [P, 2, MD, CH])
        u = sb("u", [P, 2, MD, CH])
        h_in = sb("h_in", [P, 2, KE, CH])
        bc_sb = sb("bc_sb", [P, CH])
        b_all = sb("b_all", [P, RING_B, G, CH])
        c_all = sb("c_all", [P, RING_B, G, CH])
        da = sb("da", [P, RING_A, G, CH])
        dbx = sb("dbx", [P, RING, G, CH])
        state = sb("state", [P, STEPS, G])
        gated = sb("gated", [P, 2, E])
        y_ps = [ps(f"y_ps{m}", [P, CH]) for m in range(MD)]
        proj_ps = [ps(f"proj_ps{i}", [P, CH]) for i in range(2)]
        out_ps = [ps(f"out_ps{i}", [P, E]) for i in range(2)]

        PE_MAIN, PE_OUT, PE_BC, PE_Z = (0, 2, 4, 6), 11, 14, (18, 20, 22, 24)
        ACT_MAIN, ACT_SILU, ACT_BC, ACT_SOFT, ACT_Z = (6, 8, 10, 12), 17, 22, 25, (25, 27, 29, 31)
        DVE_CONV, DVE_OUT, DVE_DELTA = (7, 9, 11, 13), 13, 27
        POOL_GATE, POOL_U = 10, 31

        names = ("proj_done proj_copied conv_chain conv_done conv_act z_act bc_done delta_done bc_copied bc_stored raw_ready "
                 "soft_chain soft_ready delta_ready u_ready da_ready dbx_ready scanned states_kept hc_ready summed "
                 "y_taken y_gated out_done out_chain out_added tail_kept head_set filled").split()
        S = {n: sem(n) for n in names}
        bc_loaded = [sem(f"bc_loaded{i}") for i in range(RING_B)]
        h_loaded = [sem("h_loaded0"), sem("h_loaded1")]
        block = ctx.enter_context(nc.Block())

        def chunks(eng, body):
            for th in range(CPB):
                body(th, 0, th, th == 0, False)
            with eng.Fori(1, B - 1) as b:
                for th in range(CPB):
                    body(b * CPB + th, b, th, False, False)
            for th in range(CPB):
                body((B - 1) * CPB + th, B - 1, th, False, th == CPB - 1)

        zeros_over = lambda tiles: sh.zeros[:].rearrange("p (o e) -> p o e", o=1).broadcast_to([P, tiles, E])

        @block.sync
        def _(sp):
            def store_rows(c):
                sp.wait_ge(S["bc_copied"], c + 1)
                sp.dma_start(d["bc_rows"][bass.ds(c, 1)].rearrange("o n t -> (o n) t"), bc_sb[0:2 * NS, :]).then_inc(S["bc_stored"], 16)

            def load_group(c, g, first):
                if not (first and g < RING_B):
                    sp.wait_ge(S["dbx_ready"], c * STEPS + (g + 1 - RING_B) * MD)
                    sp.wait_ge(S["hc_ready"], c * STEPS + (g + 1 - RING_B) * MD)
                if g == 0:
                    sp.wait_ge(S["bc_stored"], c * 16 + 16)
                for dst, row in ((b_all, 0), (c_all, NS)):
                    src = d["bc_rows"][bass.ds(c, 1), row + g * G:row + (g + 1) * G, :].rearrange("o n t -> (o n) t")
                    sp.dma_start(dst[:, g % RING_B], src.partition_broadcast(P)).then_inc(bc_loaded[g % RING_B], 16)

            def load_h(c, b, p, first):
                if not first:
                    sp.wait_ge(S["proj_done"], c * 8 - 8)
                sp.dma_start(h_in[:, p], d["h_turned"][bass.ds(c, 1)].rearrange("o p k t -> (o p) k t")).then_inc(h_loaded[p], 16)

            def fill(c, g):
                rows, n, tiles = (d["slots0"], g, 3) if g < FILL0 // 3 else (d["slots1"], g - FILL0 // 3, 2)
                first_row = c * ((FILL0 if g < FILL0 // 3 else FILL1) * P) + n * tiles * P
                part = rows[bass.ds(first_row, tiles * P), :].rearrange("(a p) e -> p a e", p=P)
                sp.dma_start(part, zeros_over(tiles)).then_inc(S["filled"], 16)

            def body(c, b, th, first, last):
                for g in range(NG):
                    load_group(c, g, first)
                    fill(c, g)
                    if g == 4 and not (last or (isinstance(c, int) and c >= B * CPB - 2)):
                        load_h(c + 2, b + 1, th, False)
                if not last:
                    store_rows(c + 1)

            load_h(0, 0, 0, True)
            load_h(1, 0, 1, True)
            store_rows(0)
            for rows in (d["slots1"][FILL1 * P * B * CPB:], d["outs1"][EXPERTS1 * CAP1:]):
                sp.dma_start(rows.rearrange("(a p) e -> p a e", p=P), zeros_over(rows.shape[0] // P)).then_inc(S["filled"], 16)
            chunks(sp, body)
            sp.wait_ge(S["filled"], 16 * (NG * B * CPB + 2))

        @block.tensor
        def _(pe):
            def project(c, b, p, m, first):
                if m == 0:
                    pe.wait_ge(h_loaded[p], b * 16 + 16)
                if m in (MD, MD + 1):
                    pe.wait_ge(S["raw_ready" if m > MD else "bc_copied"], c + 1)
                elif not (first and m < 2):
                    pe.wait_ge(S["proj_copied"], c * 8 + m - 1)
                for k in range(KE):
                    mm = nc.tensor.matmul(proj_ps[m % 2][:], sh.w_in[:, k, m * P:(m + 1) * P], h_in[:, p, k, :],
                                          start=(k == 0), stop=(k == KE - 1))
                mm.then_inc(S["proj_done"], 1)

            def bc_product(c, p):
                pe.wait_ge(S["conv_act"], c + 1)
                pe.wait_ge(S["proj_copied"], c * 8 + 3)
                for k in range(MD):
                    mm = nc.tensor.matmul(proj_ps[0][0:2 * NS, :], sh.w_x[:, k, 1:1 + 2 * NS], x_conv[:, p, k, :],
                                          start=(k == 0), stop=(k == MD - 1))
                mm.then_inc(S["bc_done"], 1)

            def delta_product(c, p):
                pe.wait_ge(S["proj_copied"], c * 8 + 4)
                for k in range(MD):
                    mm = nc.tensor.matmul(proj_ps[1][:], sh.w_delta[:, k, :], x_conv[:, p, k, :],
                                          start=(k == 0), stop=(k == MD - 1))
                mm.then_inc(S["delta_done"], 1)

            def sum_states(c, s, first):
                g, m = s // MD, s % MD
                pe.wait_ge(S["hc_ready"], c * STEPS + s + 1)
                if g == 0 and not first:
                    pe.wait_ge(S["y_taken"], (c - 1) * MD + m + 1)
                for i in range(G):
                    mm = nc.tensor.matmul(y_ps[m][:], sh.ident[:], da[:, s % RING_A, i, :],
                                          start=(g == 0 and i == 0), stop=(g == NG - 1 and i == G - 1))
                mm.then_inc(S["summed"], 1)

            def out_product(c, p, j, first):
                pe.wait_ge(S["y_gated"], (c + 1) * MD)
                if not (first and j < 2):
                    pe.wait_ge(S["out_added"], c * CT + j - 1)
                for k in range(MD):
                    mm = nc.tensor.matmul(out_ps[j % 2][:], u[:, p, k, j * P:(j + 1) * P], sh.w_out[:, k, :],
                                          start=(k == 0), stop=(k == MD - 1))
                mm.then_inc(S["out_done"], 1)

            def body(c, b, th, first, last):
                for s in range(STEPS):
                    sum_states(c, s, first)
                    if not last:
                        if s in PE_MAIN:
                            project(c + 1, b + th, 1 - th, PE_MAIN.index(s), False)
                        if s == PE_BC:
                            bc_product(c + 1, 1 - th)
                        if s == PE_BC + 1:
                            delta_product(c + 1, 1 - th)
                        if s in PE_Z:
                            project(c + 1, b + th, 1 - th, MD + PE_Z.index(s), False)
                    if not first and PE_OUT <= s < PE_OUT + CT:
                        out_product(c - 1, 1 - th, s - PE_OUT, isinstance(c, int) and c == 1)

            for m in range(MD):
                project(0, 0, 0, m, True)
            bc_product(0, 0)
            delta_product(0, 0)
            for m in range(MD, 2 * MD):
                project(0, 0, 0, m, True)
            chunks(pe, body)
            for j in range(CT):
                out_product(B * CPB - 1, 1, j, False)

        @block.scalar
        def _(act):
            def copy_out(c, p, m):
                act.wait_ge(S["proj_done"], c * 8 + m + 1)
                if m < MD:
                    dst = x_main[:, m % 2, DC - 1:]
                    if m >= 2 or not (isinstance(c, int) and c == 0):
                        act.wait_ge(S["tail_kept"], (c * MD + m - 1))
                else:
                    dst = gate[:, p, m - MD, :]
                if m < MD:
                    nc.scalar.activation(delta[:, p, m, :], proj_ps[m % 2][:], ACT.Identity, bias=sh.vecs[:, 0, m:m + 1],
                                         scale=sh.conv_w[:, m, DC - 1:DC])
                nc.scalar.copy(dst, proj_ps[m % 2][:]).then_inc(S["proj_copied"], 1)

            def silu_conv(c, p):
                act.wait_ge(S["conv_done"], (c + 1) * MD)
                nc.scalar.activation(x_conv[:, p], delta[:, p], ACT.Silu).then_inc(S["conv_act"], 1)

            def silu_z(c, p):
                act.wait_ge(S["proj_copied"], c * 8 + 8)
                nc.scalar.activation(gate[:, p], gate[:, p], ACT.Silu).then_inc(S["z_act"], 1)

            def copy_bc(c, first):
                act.wait_ge(S["bc_done"], c + 1)
                if not first:
                    act.wait_ge(S["bc_stored"], c * 16)
                nc.scalar.copy(bc_sb[0:2 * NS, :], proj_ps[0][0:2 * NS, :]).then_inc(S["bc_copied"], 1)

            def softplus(c, p, first):
                act.wait_ge(S["delta_done"], c + 1)
                if not first:
                    act.wait_ge(S["out_done"], (c - 1) * CT)
                for m in range(MD):
                    for dst, fun in ((delta, ACT.Relu), (u, ACT.Abs)):
                        ins = nc.scalar.activation(dst[:, p, m, :], proj_ps[1][:], fun, bias=sh.vecs[:, 2, m:m + 1],
                                                   scale=sh.vecs[:, 1, m:m + 1])
                ins.then_inc(S["raw_ready"], 1)
                act.wait_ge(S["raw_ready"], c + 1)
                nc.scalar.activation(u[:, p], u[:, p], ACT.Exp, scale=-1.0).then_inc(S["soft_chain"], 1)
                act.wait_ge(S["soft_chain"], c + 1)
                nc.scalar.activation(u[:, p], u[:, p], ACT.Ln, bias=1.0).then_inc(S["soft_ready"], 1)

            def decays(c, p, s, first):
                g, m = s // MD, s % MD
                if s == 0:
                    act.wait_ge(S["delta_ready"], c + 1)
                if not (first and s < RING_A):
                    act.wait_ge(S["summed"], c * STEPS + s + 1 - RING_A)
                for i in range(G):
                    ex = nc.scalar.activation(da[:, s % RING_A, i, :], delta[:, p, m, :], ACT.Exp,
                                              scale=sh.a_neg[:, m, g * G + i:g * G + i + 1])
                ex.then_inc(S["da_ready"], 1)

            def body(c, b, th, first, last):
                for s in range(STEPS):
                    decays(c, th, s, first)
                    if s == ACT_SILU:
                        silu_z(c, th)
                        if not last:
                            silu_conv(c + 1, 1 - th)
                    if not last:
                        if s in ACT_MAIN:
                            copy_out(c + 1, 1 - th, ACT_MAIN.index(s))
                        if s == ACT_BC:
                            copy_bc(c + 1, False)
                        if s == ACT_SOFT:
                            softplus(c + 1, 1 - th, first)
                        if s in ACT_Z:
                            if s == ACT_Z[0] and not first:
                                act.wait_ge(S["y_gated"], c * MD)
                            copy_out(c + 1, 1 - th, MD + ACT_Z.index(s))

            for m in range(MD):
                copy_out(0, 0, m)
            silu_conv(0, 0)
            copy_bc(0, True)
            softplus(0, 0, True)
            for m in range(MD, 2 * MD):
                copy_out(0, 0, m)
            chunks(act, body)

        @block.gpsimd
        def _(pool):
            def products(c, p, s, first):
                g, m = s // MD, s % MD
                if s == 0:
                    pool.wait_ge(S["u_ready"], c + 1)
                if m == 0:
                    pool.wait_ge(bc_loaded[g % RING_B], c * (32 * NG // RING_B) + 32 * (g // RING_B + 1))
                if not (first and s < RING):
                    pool.wait_ge(S["scanned"], c * STEPS + s + 1 - RING)
                nc.gpsimd.tensor_tensor(dbx[:, s % RING], u[:, p, m:m + 1, :].broadcast_to([P, G, CH]), b_all[:, g % RING_B],
                                        ALU.mult).then_inc(S["dbx_ready"], 1)

            def multiply_u(c, p):
                pool.wait_ge(S["delta_ready"], c + 1)
                nc.gpsimd.tensor_tensor(u[:, p], delta[:, p], x_conv[:, p], ALU.mult).then_inc(S["u_ready"], 1)

            def gate_y(c, p, m):
                pool.wait_ge(S["y_taken"], c * MD + m + 1)
                if m == 0:
                    pool.wait_ge(S["z_act"], c + 1)
                nc.gpsimd.tensor_tensor(u[:, p, m, :], u[:, p, m, :], gate[:, p, m, :], ALU.mult).then_inc(S["y_gated"], 1)

            def body(c, b, th, first, last):
                for s in range(STEPS):
                    products(c, th, s, first)
                    if not first and POOL_GATE <= s < POOL_GATE + MD:
                        gate_y(c - 1, 1 - th, s - POOL_GATE)
                    if not last and s == POOL_U:
                        multiply_u(c + 1, 1 - th)

            multiply_u(0, 0)
            chunks(pool, body)
            for m in range(MD):
                gate_y(B * CPB - 1, 1, m)

        @block.vector
        def _(dve):
            def convolve(c, p, m, fresh):
                dve.wait_ge(S["proj_copied"], c * 8 + m + 1)
                if not fresh:
                    dve.wait_ge(S["tail_kept"], (c - 1) * MD + m + 1)
                acc, xm = delta[:, p, m, :], x_main[:, m % 2, :]
                if fresh:
                    nc.vector.memset(xm[:, 0:DC - 1], 0.0).then_inc(S["head_set"], 1)
                else:
                    nc.vector.tensor_copy(xm[:, 0:DC - 1], tail[:, m, :]).then_inc(S["head_set"], 1)
                dve.wait_ge(S["head_set"], c * MD + m + 1)
                for j in range(DC - 1):
                    if j:
                        dve.wait_ge(S["conv_chain"], (c * MD + m) * (DC - 2) + j)
                    ins = nc.vector.scalar_tensor_tensor(out=acc, in0=xm[:, j:j + CH], scalar=sh.conv_w[:, m, j:j + 1],
                                                         in1=acc, op0=ALU.mult, op1=ALU.add)
                    ins.then_inc(S["conv_chain"] if j < DC - 2 else S["conv_done"], 1)
                nc.vector.tensor_copy(tail[:, m, :], xm[:, CH:]).then_inc(S["tail_kept"], 1)

            def finish_delta(c, p):
                dve.wait_ge(S["soft_ready"], c + 1)
                nc.vector.tensor_tensor(delta[:, p], delta[:, p], u[:, p], ALU.add).then_inc(S["delta_ready"], 1)

            def scans(c, b, th, s):
                g, m = s // MD, s % MD
                dve.wait_ge(S["da_ready"], c * STEPS + s + 1)
                dve.wait_ge(S["dbx_ready"], c * STEPS + s + 1)
                if th == 1:
                    dve.wait_ge(S["states_kept"], b * STEPS + s + 1)
                for i in range(G):
                    h = da[:, s % RING_A, i, :]
                    ins = nc.vector.tensor_tensor_scan(h, h, dbx[:, s % RING, i, :], 0.0 if th == 0 else state[:, s, i:i + 1],
                                                       ALU.mult, ALU.add)
                ins.then_inc(S["scanned"], 1)

            def outputs(c, b, th, s):
                g, m = s // MD, s % MD
                dve.wait_ge(S["scanned"], c * STEPS + s + 1)
                if th == 0:
                    nc.vector.tensor_copy(state[:, s, :], da[:, s % RING_A, :, CH - 1]).then_inc(S["states_kept"], 1)
                    dve.wait_ge(S["states_kept"], b * STEPS + s + 1)
                if m == 0:
                    dve.wait_ge(bc_loaded[g % RING_B], c * (32 * NG // RING_B) + 32 * (g // RING_B + 1))
                nc.vector.tensor_tensor(da[:, s % RING_A], da[:, s % RING_A], c_all[:, g % RING_B], ALU.mult).then_inc(S["hc_ready"], 1)

            def take_y(c, p, m):
                dve.wait_ge(S["summed"], (c + 1) * STEPS - MD + m + 1)
                nc.vector.scalar_tensor_tensor(out=u[:, p, m, :], in0=x_conv[:, p, m, :], scalar=sh.vecs[:, 3, m:m + 1],
                                               in1=y_ps[m][:], op0=ALU.mult, op1=ALU.add).then_inc(S["y_taken"], 1)

            def add_out(c, b, th, j):
                tile = c * CT + j
                dve.wait_ge(S["out_done"], c * CT + j + 1)
                nc.vector.tensor_tensor(gated[:, j % 2, :], out_ps[j % 2][:], sh.mods[:, 2, b, :], ALU.mult).then_inc(S["out_added"], 1)
                dve.wait_ge(S["out_added"], c * CT + j + 1)
                nc.vector.tensor_tensor(sh.x[:, tile, :], sh.x[:, tile, :], gated[:, j % 2, :], ALU.add).then_inc(S["out_chain"], 1)
                dve.wait_ge(S["out_chain"], c * CT + j + 1)
                nc.vector.bn_stats(sh.stats[:, tile, :], sh.x[:, tile, :])

            def body(c, b, th, first, last):
                for s in range(STEPS):
                    scans(c, b, th, s)
                    outputs(c, b, th, s)
                    if not last:
                        if s in DVE_CONV:
                            convolve(c + 1, 1 - th, DVE_CONV.index(s), th == CPB - 1)
                        if s == DVE_DELTA:
                            finish_delta(c + 1, 1 - th)
                    if not first:
                        if s < MD:
                            take_y(c - 1, 1 - th, s)
                        if DVE_OUT <= s < DVE_OUT + CT:
                            add_out(c - 1, b if th == 1 else b - 1, 1 - th, s - DVE_OUT)

            for m in range(MD):
                convolve(0, 0, m, True)
            finish_delta(0, 0)
            chunks(dve, body)
            for m in range(MD):
                take_y(B * CPB - 1, 1, m)
            for j in range(CT):
                add_out(B * CPB - 1, B - 1, 1, j)


def phase_route(nc, d, sh, layer, gate_name, slots_name):
    NE = (EXPERTS0, EXPERTS1)[layer]
    RT = 4
    with ExitStack() as ctx:
        sb = lambda name, shape, dt=F32: ctx.enter_context(nc.sbuf_tensor(f"rt{layer}_{name}", shape, dt))
        ps = lambda name, shape: ctx.enter_context(nc.psum_tensor(f"rt{layer}_{name}", shape, F32))
        sem = ctx.enter_context(Semaphores(nc, f"rt{layer}_"))
        gate_w = sb("gate_w", [P, KE, NE])
        half = sb("half", [P, 4, E])
        row8 = sb("row8", [P, TPB, E])
        h_rows = sb("h_rows", [P, TILES, E])
        h_tr = sb("h_tr", [P, RT, KE, P])
        logits = sb("logits", [P, TILES, NE])
        scores = sb("scores", [P, TILES, NE])
        cand = sb("cand", [P, TILES, NE])
        rank = sb("rank", [P, TILES, NE])
        mask = sb("mask", [P, 2, TILES, NE])
        both = sb("both", [P, TILES, NE])
        iota_e = sb("iota_e", [P, TILES, NE])
        top = sb("top", [P, 2, TILES])
        idx = sb("idx", [P, TILES])
        tri = sb("tri", [P, P])
        ones = sb("ones", [P, P])
        run_on = sb("run_on", [P, NE, TILES])
        total = sb("total", [P, NE, TILES])
        before = sb("before", [P, NE, TILES])
        count = sb("count", [P, NE])
        count_i = sb("count_i", [P, NE], I32)
        padded = sb("padded", [P, NE])
        ends = sb("ends", [P, NE])
        offs = sb("offs", [P, NE])
        slot = sb("slot", [P, 2, TILES])
        valid = sb("valid", [P, 2, TILES])
        spare = sb("spare", [P, 1])
        wsum = sb("wsum", [P, TILES])
        tiles_at = sb("tiles_at", [P, TILES0])
        owner = sb("owner", [P, TILES0])
        turned = [ps(f"turned{i}", [P, KE, P]) for i in range(RT)]
        logit_ps = ps("logit_ps", [P, TPB, NE])
        tri_ps, tot_ps = ps("tri_ps", [P, TILES, NE]), ps("tot_ps", [P, TILES, NE])
        (mods_in, gate_in, var_ready, std_ready, chain, half_ready, row_ready, row_turned, turn_copied, logits_done,
         logits_copied, consts_ready, score_ready, masks_ready, ranked, gap_ready, exp_ready, slots_ready, scattered, pool_chain) = (
            sem(n) for n in ("mods_in gate_in var_ready std_ready chain half_ready row_ready row_turned turn_copied logits_done "
                             "logits_copied consts_ready score_ready masks_ready ranked gap_ready exp_ready "
                             "slots_ready scattered pool_chain").split())
        rows_copied = [sem(f"rows_copied{th}") for th in range(CPB)]
        block = ctx.enter_context(nc.Block())

        @block.sync
        def _(sp):
            load_mods(sp, d, sh, layer, 1, mods_in)
            sp.dma_start(gate_w[:], d[gate_name].rearrange("(k p) n -> p k n", p=P)).then_inc(gate_in, 16)
            with sp.Fori(0, B) as b:
                for th in range(CPB):
                    sp.wait_ge(row_ready, b * TPB + (th + 1) * CT + 4)
                    sp.dma_start(h_rows[:, bass.ds(b * TPB + th * CT, CT), :], row8[:, th * CT:(th + 1) * CT, :]).then_inc(rows_copied[th], 16)
            if layer == 0:
                for e in range(EXPERTS0):
                    for i, name in enumerate(("L0_ffn_W1", "L0_ffn_W3")):
                        sp.dma_start(sh.w13[:, e, i], d[name][e].rearrange("(k p) f -> p k f", p=P)).then_inc(sh.e0_w_in, 16)
                    sp.dma_start(sh.w2_0[:, e], d["L0_ffn_W2"][e].rearrange("(m p) f -> p m f", p=P)).then_inc(sh.e0_w_in, 16)

        @block.gpsimd
        def _(pool):
            nc.gpsimd.memset(tri[:], 1.0).then_inc(pool_chain, 1)
            nc.gpsimd.memset(ones[:], 1.0).then_inc(pool_chain, 1)
            pool.wait_ge(pool_chain, 2)
            nc.gpsimd.affine_select(out=tri[:], in_=tri[:], compare_op=ALU.is_gt, fill=0.0, base=0, pattern=[[1, P]],
                                    channel_multiplier=-1).then_inc(consts_ready, 1)
            nc.gpsimd.iota(iota_e[:], pattern=[[0, TILES], [1, NE]], base=0, channel_multiplier=0,
                           allow_small_or_imprecise_dtypes=True).then_inc(consts_ready, 1)
            nc.gpsimd.memset(run_on[:], 1.0).then_inc(pool_chain, 1)
            pool.wait_ge(pool_chain, 3)
            nc.gpsimd.memset(run_on[:, :, 0:1], 0.0).then_inc(consts_ready, 1)
            nc.gpsimd.iota(offs[:], pattern=[[CAP1, NE]], base=0, channel_multiplier=0,
                           allow_small_or_imprecise_dtypes=True).then_inc(consts_ready, 1)
            nc.gpsimd.iota(spare[:], pattern=[[0, 1]], base=EXPERTS1 * CAP1, channel_multiplier=1,
                           allow_small_or_imprecise_dtypes=True).then_inc(consts_ready, 1)
            nc.gpsimd.iota(tiles_at[:], pattern=[[P, TILES0]], base=0, channel_multiplier=0,
                           allow_small_or_imprecise_dtypes=True).then_inc(consts_ready, 1)
            pool.wait_ge(slots_ready, 1)
            for th in range(CPB):
                pool.wait_ge(rows_copied[th], 16 * B + 1)
            for i in range(TILES):
                for k in range(2):
                    nc.gpsimd.indirect_dma_start(out=d[slots_name], out_offset=bass.IndirectOffsetOnAxis(ap=sh.slot_of[:, k, i:i + 1], axis=0),
                                                 in_=h_rows[:, i, :], in_offset=None).then_inc(scattered, 16)
            pool.wait_ge(scattered, 2 * TILES * 16)

        @block.scalar
        def _(act):
            act.wait_ge(var_ready, 1)
            nc.scalar.activation(sh.var[:], sh.var[:], ACT.Sqrt).then_inc(std_ready, 1)
            with act.Fori(0, B) as b:
                for j in range(TPB):
                    act.wait_ge(row_turned, b * TPB + j + 1 + TPB)
                    act.wait_ge(logits_done, b * TPB + j + 1)
                    nc.scalar.copy(h_tr[:, j % RT], turned[j % RT][:]).then_inc(turn_copied, 1)
                act.wait_ge(logits_done, b * TPB + TPB + RT)
                nc.scalar.copy(logits[:, bass.ds(b * TPB, TPB), :], logit_ps[:]).then_inc(logits_copied, 1)
            act.wait_ge(logits_copied, B + 1)
            if layer == 1:
                nc.scalar.activation(logits[:], logits[:], ACT.Sigmoid).then_inc(score_ready, 1)
            else:
                act.sem_inc(score_ready, 1)
                act.wait_ge(gap_ready, 1)
                nc.scalar.activation(sh.weight[:, 1], sh.weight[:, 1], ACT.Exp).then_inc(exp_ready, 1)

        @block.tensor
        def _(pe):
            pe.sem_inc(row_turned, TPB)
            pe.sem_inc(logits_done, RT)
            pe.sem_inc(turn_copied, RT)
            pe.sem_inc(row_ready, 4)
            pe.sem_inc(logits_copied, 1)
            for th in range(CPB):
                pe.sem_inc(rows_copied[th], 1)
            pe.wait_ge(gate_in, 16)

            with pe.Fori(0, B) as b:
                def turn(j):
                    pe.wait_ge(row_ready, b * TPB + j + 5)
                    pe.wait_ge(turn_copied, b * TPB + j + 1)
                    for k in range(KE):
                        last = nc.tensor.transpose(turned[j % RT][:, k, :], row8[:, j, k * P:(k + 1) * P], sh.ident[:])
                    last.then_inc(row_turned, 1)

                def product(j):
                    pe.wait_ge(turn_copied, b * TPB + j + RT + 1)
                    if j == 0:
                        pe.wait_ge(logits_copied, b + 1)
                    for k in range(KE):
                        last = nc.tensor.matmul(logit_ps[:, j, :], h_tr[:, j % RT, k, :], gate_w[:, k, :],
                                                start=(k == 0), stop=(k == KE - 1))
                    last.then_inc(logits_done, 1)

                for j in range(TPB + 2):
                    if j < TPB:
                        turn(j)
                    if j >= 2:
                        product(j - 2)
            pe.wait_ge(masks_ready, 1)
            pe.wait_ge(consts_ready, 1)
            nc.tensor.matmul(tri_ps[:], tri[:], both[:], start=True, stop=True).then_inc(ranked, 1)
            nc.tensor.matmul(tot_ps[:], ones[:], both[:], start=True, stop=True).then_inc(ranked, 1)

        @block.vector
        def _(dve):
            link = link_on(dve, chain)
            finish_stats(nc, dve, link, sh, var_ready, std_ready)
            dve.wait_ge(mods_in, 16)

            def row_free(b, j):
                dve.wait_ge(row_turned, b * TPB + j + 1)
                if j % CT == 0:
                    dve.wait_ge(rows_copied[j // CT], b * 16 + 1)

            norm_rows(nc, dve, sh, half, row8, half_ready, row_ready, row_free)

            over = lambda a: a.rearrange("p (t o) -> p t o", o=1).broadcast_to([P, TILES, NE])
            dve.wait_ge(score_ready, 1)
            dve.wait_ge(consts_ready, 6)
            values = logits
            for k in range(2):
                link(nc.vector.tensor_reduce(top[:, k], values[:], AX_X, ALU.max))
                link(nc.vector.tensor_tensor(cand[:], values[:], over(top[:, k]), ALU.is_lt))
                link(nc.vector.scalar_tensor_tensor(out=cand[:], in0=cand[:], scalar=float(NE), in1=iota_e[:], op0=ALU.mult, op1=ALU.add))
                link(nc.vector.tensor_reduce(idx[:], cand[:], AX_X, ALU.min))
                link(nc.vector.tensor_tensor(mask[:, k], iota_e[:], over(idx[:]), ALU.is_equal))
                if k == 0:
                    link(nc.vector.scalar_tensor_tensor(out=scores[:], in0=mask[:, 0], scalar=-3e38, in1=values[:], op0=ALU.mult, op1=ALU.add))
                    values = scores
            nc.vector.tensor_tensor(both[:], mask[:, 0], mask[:, 1], ALU.add).then_inc(masks_ready, 1)
            if layer == 0:
                nc.vector.tensor_tensor(sh.weight[:, 1], top[:, 1], top[:, 0], ALU.subtract).then_inc(gap_ready, 1)
            dve.wait_ge(ranked, 2)
            link(nc.vector.tensor_copy(total[:], tot_ps[:].rearrange("p t e -> p e t")))
            flat = lambda a: a.rearrange("p e t -> p (e t)")
            link(nc.vector.tensor_tensor_scan(flat(before[:]), flat(run_on[:]), flat(total[:]), 0.0, ALU.mult, ALU.add))
            link(nc.vector.tensor_copy(count[:], before[:, :, TILES - 1]))
            link(nc.vector.tensor_tensor(before[:], before[:], total[:], ALU.subtract))
            link(nc.vector.tensor_tensor(rank[:], tri_ps[:], before[:].rearrange("p e t -> p t e"), ALU.add))
            if layer == 0:
                link(nc.vector.tensor_scalar(count_i[:], count[:], float(P - 1), None, ALU.add))
                link(nc.vector.tensor_scalar(count_i[:], count_i[:], 7, 7, ALU.arith_shift_right, ALU.logical_shift_left))
                link(nc.vector.tensor_copy(padded[:], count_i[:]))
                link(nc.vector.tensor_tensor_scan(ends[:], ones[:, 0:NE], padded[:], 0.0, ALU.mult, ALU.add))
                link(nc.vector.tensor_tensor(offs[:], ends[:], padded[:], ALU.subtract))
                link(nc.vector.tensor_scalar(owner[:], tiles_at[:], ends[:, 0:1], None, ALU.is_ge))
                for e in range(1, NE - 1):
                    link(nc.vector.scalar_tensor_tensor(out=owner[:], in0=tiles_at[:], scalar=ends[:, e:e + 1], in1=owner[:],
                                                        op0=ALU.is_ge, op1=ALU.add))
                link(nc.vector.tensor_copy(sh.owner_i[:], owner[:]))
            link(nc.vector.tensor_tensor(cand[:], rank[:], offs[:].rearrange("p (o e) -> p o e", o=1).broadcast_to([P, TILES, NE]), ALU.add))
            for k in range(2):
                link(nc.vector.tensor_tensor(scores[:], mask[:, k], cand[:], ALU.mult))
                link(nc.vector.tensor_reduce(slot[:, k], scores[:], AX_X, ALU.add))
                if layer == 1:
                    link(nc.vector.tensor_tensor(scores[:], mask[:, k], rank[:], ALU.mult))
                    link(nc.vector.tensor_reduce(valid[:, k], scores[:], AX_X, ALU.add))
            if layer == 1:
                link(nc.vector.tensor_scalar(valid[:], valid[:], float(CAP1), None, ALU.is_lt))
                link(nc.vector.scalar_tensor_tensor(out=slot[:], in0=slot[:], scalar=spare[:, 0:1], in1=valid[:], op0=ALU.subtract, op1=ALU.mult))
                link(nc.vector.tensor_scalar(slot[:], slot[:], spare[:, 0:1], None, ALU.add))
            nc.vector.tensor_copy(sh.slot_of[:], slot[:]).then_inc(slots_ready, 1)
            if layer == 0:
                dve.wait_ge(exp_ready, 1)
                link(nc.vector.tensor_scalar(wsum[:], sh.weight[:, 1], 1.0, None, ALU.add))
                link(nc.vector.reciprocal(sh.weight[:, 0], wsum[:]))
                link(nc.vector.tensor_tensor(sh.weight[:, 1], sh.weight[:, 1], sh.weight[:, 0], ALU.mult))
            else:
                link(nc.vector.tensor_tensor(wsum[:], top[:, 0], top[:, 1], ALU.add))
                link(nc.vector.tensor_scalar(wsum[:], wsum[:], 1e-6, None, ALU.add))
                link(nc.vector.reciprocal(wsum[:], wsum[:]))
                for k in range(2):
                    link(nc.vector.tensor_tensor(sh.weight[:, k], top[:, k], wsum[:], ALU.mult))
                    link(nc.vector.tensor_tensor(sh.weight[:, k], sh.weight[:, k], valid[:, k], ALU.mult))


def phase_experts0(nc, d, sh):
    U = 4
    with ExitStack() as ctx:
        sb = lambda name, shape: ctx.enter_context(nc.sbuf_tensor(f"e0_{name}", shape, F32))
        ps = lambda name, shape: ctx.enter_context(nc.psum_tensor(f"e0_{name}", shape, F32))
        sem = ctx.enter_context(Semaphores(nc, "e0_"))
        w13, w2 = sh.w13, sh.w2_0
        xs = sb("xs", [P, U, E])
        xt = sb("xt", [P, 2, KE, P])
        act_h = sb("act_h", [P, 2, H0])
        prod = sb("prod", [P, 2, H0])
        pt = sb("pt", [P, 2, MH0, P])
        ys = sb("ys", [P, U, E])
        x_ps = ps("x_ps", [P, KE, P])
        h_ps = [ps(f"h_ps{i}", [P, H0]) for i in range(2)]
        g_ps = [ps(f"g_ps{i}", [P, H0]) for i in range(2)]
        p_ps = ps("p_ps", [P, MH0, P])
        y_ps = ps("y_ps", [P, E])
        x_in, y_out = [sem(f"x_in{i}") for i in range(U)], [sem(f"y_out{i}") for i in range(U)]
        x_turned, x_copied, h_done, silu_done, prod_done, p_turned, p_copied, y_done, y_copied = (
            sem(n) for n in "x_turned x_copied h_done silu_done prod_done p_turned p_copied y_done y_copied".split())
        block = ctx.enter_context(nc.Block())
        LOOPS = TILES0 // U
        assert TILES0 % U == 0

        def tiles(eng, body):
            for r in range(U):
                body(r, r, 0)
            with eng.Fori(1, LOOPS - 1) as q:
                for r in range(U):
                    body(q * U + r, r, q)
            for r in range(U):
                body(TILES0 - U + r, r, LOOPS - 1)

        exists = lambda j: not isinstance(j, int) or 0 <= j < TILES0
        early = lambda j, n: isinstance(j, int) and j < n

        @block.sync
        def _(sp):
            sp.dma_start(sh.w_qkv[:], d["wqkvT"].rearrange("(k p) (h c f) -> p k h c f", p=P, h=HEADS, c=3)).then_inc(sh.att_w_in, 16)

            def load(j, r):
                if not early(j, U):
                    sp.wait_ge(x_turned, j - U + 1)
                sp.dma_start(xs[:, r], d["slots0"][bass.ds(j * P, P), :]).then_inc(x_in[r], 16)

            def store(j, r):
                sp.wait_ge(y_copied, j + 1)
                sp.dma_start(d["outs0"][bass.ds(j * P, P), :], ys[:, r]).then_inc(y_out[r], 16)

            def body(j, r, q):
                if exists(j + 2):
                    load(j + 2, (r + 2) % U)
                if exists(j - 2):
                    store(j - 2, (r - 2) % U)

            load(0, 0)
            load(1, 1)
            tiles(sp, body)
            store(TILES0 - 2, U - 2)
            store(TILES0 - 1, U - 1)
            for r in range(U):
                sp.wait_ge(y_out[r], 16 * LOOPS + 1)

        @block.tensor
        def _(pe):
            def turn_x(j, r, q):
                pe.wait_ge(x_in[r], q * 16 + 16)
                if not early(j, 1):
                    pe.wait_ge(x_copied, j)
                for k in range(KE):
                    last = nc.tensor.transpose(x_ps[:, k, :], xs[:, r, k * P:(k + 1) * P], sh.ident[:])
                last.then_inc(x_turned, 1)

            def hidden(j, r):
                e = nc.tensor.value_load(sh.owner_i[0:1, bass.ds(j, 1)], min_val=0, max_val=EXPERTS0 - 1)
                pe.wait_ge(x_copied, j + 1)
                if not early(j, 2):
                    pe.wait_ge(prod_done, j - 1)
                for i, out_ps in ((0, h_ps), (1, g_ps)):
                    for k in range(KE):
                        last = nc.tensor.matmul(out_ps[r % 2][:], xt[:, r % 2, k, :], w13[:, e, i, k, :],
                                                start=(k == 0), stop=(k == KE - 1))
                last.then_inc(h_done, 1)

            def turn_p(j, r):
                pe.wait_ge(prod_done, j + 1)
                if not early(j, 1):
                    pe.wait_ge(p_copied, j)
                for m in range(MH0):
                    last = nc.tensor.transpose(p_ps[:, m, :], prod[:, r % 2, m * P:(m + 1) * P], sh.ident[:])
                last.then_inc(p_turned, 1)

            def output(j, r):
                e = nc.tensor.value_load(sh.owner_i[0:1, bass.ds(j, 1)], min_val=0, max_val=EXPERTS0 - 1)
                pe.wait_ge(p_copied, j + 1)
                if not early(j, 1):
                    pe.wait_ge(y_copied, j)
                for m in range(MH0):
                    last = nc.tensor.matmul(y_ps[:], pt[:, r % 2, m, :], w2[:, e, m, :], start=(m == 0), stop=(m == MH0 - 1))
                last.then_inc(y_done, 1)

            def body(j, r, q):
                hidden(j, r)
                if exists(j - 1):
                    turn_p(j - 1, (r - 1) % U)
                if exists(j + 1):
                    turn_x(j + 1, (r + 1) % U, q + (r + 1) // U)
                if exists(j - 2):
                    output(j - 2, (r - 2) % U)

            pe.wait_ge(sh.e0_w_in, 48 * EXPERTS0)
            turn_x(0, 0, 0)
            tiles(pe, body)
            turn_p(TILES0 - 1, U - 1)
            output(TILES0 - 2, U - 2)
            output(TILES0 - 1, U - 1)

        @block.scalar
        def _(act):
            def copy_x(j, r):
                act.wait_ge(x_turned, j + 1)
                if not early(j, 2):
                    act.wait_ge(h_done, j - 1)
                nc.scalar.copy(xt[:, r % 2], x_ps[:]).then_inc(x_copied, 1)

            def silu(j, r):
                act.wait_ge(h_done, j + 1)
                if not early(j, 2):
                    act.wait_ge(prod_done, j - 1)
                nc.scalar.activation(act_h[:, r % 2], h_ps[r % 2][:], ACT.Silu).then_inc(silu_done, 1)

            def copy_y(j, r, q):
                act.wait_ge(y_done, j + 1)
                if not early(j, U):
                    act.wait_ge(y_out[r], q * 16 + 1)
                nc.scalar.copy(ys[:, r], y_ps[:]).then_inc(y_copied, 1)

            def body(j, r, q):
                silu(j, r)
                if exists(j + 1):
                    copy_x(j + 1, (r + 1) % U)
                if exists(j - 2):
                    copy_y(j - 2, (r - 2) % U, q - (1 if r < 2 else 0))

            for r in range(U):
                act.sem_inc(y_out[r], 1)
            copy_x(0, 0)
            tiles(act, body)
            copy_y(TILES0 - 2, U - 2, LOOPS - 1)
            copy_y(TILES0 - 1, U - 1, LOOPS - 1)

        @block.vector
        def _(dve):
            def copy_p(j, r):
                dve.wait_ge(p_turned, j + 1)
                if not early(j, 2):
                    dve.wait_ge(y_done, j - 1)
                nc.vector.tensor_copy(pt[:, r % 2], p_ps[:]).then_inc(p_copied, 1)

            def multiply(j, r):
                dve.wait_ge(silu_done, j + 1)
                if not early(j, 2):
                    dve.wait_ge(p_turned, j - 1)
                nc.vector.tensor_tensor(prod[:, r % 2], act_h[:, r % 2], g_ps[r % 2][:], ALU.mult).then_inc(prod_done, 1)

            def body(j, r, q):
                if exists(j - 1):
                    copy_p(j - 1, (r - 1) % U)
                multiply(j, r)

            tiles(dve, body)
            copy_p(TILES0 - 1, U - 1)


def phase_experts1(nc, d, sh):
    S1 = CAP1 // P
    HALF = CAP1 // 2
    with ExitStack() as ctx:
        sb = lambda name, shape: ctx.enter_context(nc.sbuf_tensor(f"e1_{name}", shape, F32))
        ps = lambda name, shape: ctx.enter_context(nc.psum_tensor(f"e1_{name}", shape, F32))
        sem = ctx.enter_context(Semaphores(nc, "e1_"))
        w1 = sb("w1", [P, 2, KE, F1])
        w2 = sb("w2", [P, 2, MF1, E])
        xs = sb("xs", [P, 2, S1, E])
        xt = sb("xt", [P, KE, CAP1])
        hid = sb("hid", [P, MF1, CAP1])
        ys = sb("ys", [P, 2, S1, E])
        x_ps = [ps(f"x_ps{i}", [P, KE, P]) for i in range(2)]
        h_ps = [ps(f"h_ps{i}", [P, HALF]) for i in range(4)]
        y_ps = [ps(f"y_ps{i}", [P, E]) for i in range(2)]
        w1_in, w2_in, x_in, y_out = ([sem(f"{n}{i}") for i in range(2)] for n in ("w1_in", "w2_in", "x_in", "y_out"))
        x_turned, x_copied, h_done, h_act, y_done, y_copied = (sem(n) for n in "x_turned x_copied h_done h_act y_done y_copied".split())
        block = ctx.enter_context(nc.Block())
        NH = 2 * MF1

        def experts(eng, body):
            for r in range(2):
                body(r, r, 0)
            with eng.Fori(1, EXPERTS1 // 2 - 1) as q:
                for r in range(2):
                    body(q * 2 + r, r, q)
            for r in range(2):
                body(EXPERTS1 - 2 + r, r, EXPERTS1 // 2 - 1)

        exists = lambda e: not isinstance(e, int) or e < EXPERTS1
        early = lambda e, n: isinstance(e, int) and e < n

        @block.sync
        def _(sp):
            def load(e, r, q):
                if not early(e, 2):
                    sp.wait_ge(x_turned, (e - 1) * S1)
                sp.dma_start(xs[:, r], d["slots1"][bass.ds(e * CAP1, CAP1), :].rearrange("(t p) f -> p t f", p=P)).then_inc(x_in[r], 16)
                if not early(e, 2):
                    sp.wait_ge(y_done, (e - 1) * S1)
                one = bass.ds(e, 1)
                sp.dma_start(w1[:, r], d["L1_ffn_w1"][one].rearrange("o (k p) f -> p (o k) f", p=P)).then_inc(w1_in[r], 16)
                sp.dma_start(w2[:, r], d["L1_ffn_w2"][one].rearrange("o (m p) f -> p (o m) f", p=P)).then_inc(w2_in[r], 16)

            def body(e, r, q):
                sp.wait_ge(y_copied, (e + 1) * S1)
                sp.dma_start(d["outs1"][bass.ds(e * CAP1, CAP1), :].rearrange("(t p) f -> p t f", p=P), ys[:, r]).then_inc(y_out[r], 16)
                if exists(e + 2):
                    load(e + 2, r, q + 1)

            load(0, 0, 0)
            load(1, 1, 0)
            experts(sp, body)
            for r in range(2):
                sp.wait_ge(y_out[r], 16 * (EXPERTS1 // 2))

        @block.tensor
        def _(pe):
            def turn_x(e, r, q):
                pe.wait_ge(x_in[r], q * 16 + 16)
                for t in range(S1):
                    if not early(e, 1) or t >= 2:
                        pe.wait_ge(x_copied, e * S1 + t - 1)
                    for k in range(KE):
                        last = nc.tensor.transpose(x_ps[(r + t) % 2][:, k, :], xs[:, r, t, k * P:(k + 1) * P], sh.ident[:])
                    last.then_inc(x_turned, 1)

            def hidden(e, r, q):
                pe.wait_ge(x_copied, (e + 1) * S1)
                pe.wait_ge(w1_in[r], q * 16 + 16)
                for n in range(NH):
                    m, part = n // 2, n % 2
                    if not early(e, 1) or n >= 4:
                        pe.wait_ge(h_act, e * NH + n - 3)
                    for k in range(KE):
                        last = nc.tensor.matmul(h_ps[n % 4][:], w1[:, r, k, m * P:(m + 1) * P],
                                                xt[:, k, part * HALF:(part + 1) * HALF], start=(k == 0), stop=(k == KE - 1))
                    last.then_inc(h_done, 1)

            def output(e, r, q):
                pe.wait_ge(h_act, (e + 1) * NH)
                pe.wait_ge(w2_in[r], q * 16 + 16)
                for t in range(S1):
                    if not early(e, 1) or t >= 2:
                        pe.wait_ge(y_copied, e * S1 + t - 1)
                    for m in range(MF1):
                        last = nc.tensor.matmul(y_ps[(r + t) % 2][:], hid[:, m, t * P:(t + 1) * P], w2[:, r, m, :],
                                                start=(m == 0), stop=(m == MF1 - 1))
                    last.then_inc(y_done, 1)

            def body(e, r, q):
                hidden(e, r, q)
                if exists(e + 1):
                    turn_x(e + 1, 1 - r, q + r)
                output(e, r, q)

            turn_x(0, 0, 0)
            experts(pe, body)

        @block.scalar
        def _(act):
            def body(e, r, q):
                for n in range(NH):
                    m, part = n // 2, n % 2
                    act.wait_ge(h_done, e * NH + n + 1)
                    if n == 0 and not early(e, 1):
                        act.wait_ge(y_done, e * S1)
                    nc.scalar.activation(hid[:, m, part * HALF:(part + 1) * HALF], h_ps[n % 4][:], ACT.Gelu).then_inc(h_act, 1)

            experts(act, body)

        @block.vector
        def _(dve):
            def copy_x(e, r):
                for t in range(S1):
                    dve.wait_ge(x_turned, e * S1 + t + 1)
                    if t == 0 and not early(e, 1):
                        dve.wait_ge(h_done, e * NH)
                    nc.vector.tensor_copy(xt[:, :, t * P:(t + 1) * P], x_ps[(r + t) % 2][:]).then_inc(x_copied, 1)

            def body(e, r, q):
                if exists(e + 1):
                    copy_x(e + 1, 1 - r)
                for t in range(S1):
                    dve.wait_ge(y_done, e * S1 + t + 1)
                    if t == 0 and not early(e, 2):
                        dve.wait_ge(y_out[r], q * 16)
                    nc.vector.tensor_copy(ys[:, r, t, :], y_ps[(r + t) % 2][:]).then_inc(y_copied, 1)

            copy_x(0, 0)
            experts(dve, body)


def phase_combine(nc, d, sh, layer, outs_name):
    R = 4
    with ExitStack() as ctx:
        sb = lambda name, shape: ctx.enter_context(nc.sbuf_tensor(f"cb{layer}_{name}", shape, F32))
        sem = ctx.enter_context(Semaphores(nc, f"cb{layer}_"))
        y = sb("y", [P, R, 2, E])
        tmp = sb("tmp", [P, 2, E])
        gathered = [sem(f"gathered{r}") for r in range(R)]
        x_ready, chain = sem("x_ready"), sem("chain")
        out_stored = sem("out_stored")
        block = ctx.enter_context(nc.Block())

        @block.gpsimd
        def _(pool):
            for i in range(TILES):
                if i >= R:
                    pool.wait_ge(x_ready, i - R + 1)
                for k in range(2):
                    nc.gpsimd.indirect_dma_start(out=y[:, i % R, k, :], out_offset=None, in_=d[outs_name],
                                                 in_offset=bass.IndirectOffsetOnAxis(ap=sh.slot_of[:, k, i:i + 1], axis=0)
                                                 ).then_inc(gathered[i % R], 16)

        @block.vector
        def _(dve):
            with dve.Fori(0, B) as b:
                for j in range(TPB):
                    tile, r, t = b * TPB + j, j % R, tmp[:, j % 2, :]
                    dve.wait_ge(gathered[r], b * (32 * TPB // R) + 32 * (j // R + 1))
                    nc.vector.tensor_scalar(t, y[:, r, 0, :], sh.weight[:, 0, bass.ds(tile, 1)], None, ALU.mult).then_inc(chain, 1)
                    dve.wait_ge(chain, tile * 3 + 1)
                    nc.vector.scalar_tensor_tensor(out=t, in0=y[:, r, 1, :], scalar=sh.weight[:, 1, bass.ds(tile, 1)], in1=t,
                                                   op0=ALU.mult, op1=ALU.add).then_inc(chain, 1)
                    dve.wait_ge(chain, tile * 3 + 2)
                    nc.vector.tensor_tensor(t, t, sh.mods[:, 2, b, :], ALU.mult).then_inc(chain, 1)
                    dve.wait_ge(chain, tile * 3 + 3)
                    nc.vector.tensor_tensor(sh.x[:, tile, :], sh.x[:, tile, :], t, ALU.add).then_inc(x_ready, 1)
                    dve.wait_ge(x_ready, tile + 1)
                    if layer == 0:
                        nc.vector.bn_stats(sh.stats[:, tile, :], sh.x[:, tile, :])

        if layer == 1:
            @block.sync
            def _(sp):
                out = token_tiles(d["out"])
                for b in range(B):
                    sp.wait_ge(x_ready, (b + 1) * TPB)
                    sp.dma_start(out[:, b * TPB:(b + 1) * TPB], sh.x[:, b * TPB:(b + 1) * TPB]).then_inc(out_stored, 16)
                sp.wait_ge(out_stored, 16 * B)


def phase_attention(nc, d, sh):
    R = 2
    SCALE = float(1.0 / np.sqrt(np.float32(DH)))
    N = HEADS * TPB
    PROJECT = (1, 2, 3, 5, 6, 7)
    PIECES = 3 * CPB
    with ExitStack() as ctx:
        sb = lambda name, shape: ctx.enter_context(nc.sbuf_tensor(f"at_{name}", shape, F32))
        ps = lambda name, shape: ctx.enter_context(nc.psum_tensor(f"at_{name}", shape, F32))
        sem = ctx.enter_context(Semaphores(nc, "at_"))
        w_qkv = sh.w_qkv
        w_o = sb("w_o", [P, HEADS, E])
        pos = sb("pos", [P, T])
        gate0 = sb("gate0", [P, B, E])
        y = sb("y", [P, R, 2, E])
        tmp = sb("tmp", [P, 2, E])
        rows = sb("rows", [P, 4, E])
        hidden_pos = sb("later", [P, P])
        h_b = sb("h_b", [P, CPB, KE, CH])
        v = sb("v", [P, 2, TPB, DH])
        qk = sb("qk", [P, 2, 2, T])
        probs = sb("probs", [P, 3, T])
        pt = sb("pt", [P, 2, TPB, P])
        attn = sb("attn", [P, HEADS, T])
        small = sb("small", [P, 4, 4])
        gated = sb("gated", [P, 2, E])
        s_ps = [ps(f"s_ps{i}", [P, T]) for i in range(2)]
        pt_ps = [ps(f"pt_ps{i}", [P, CT, P]) for i in range(2)]
        o_ps = ps("o_ps", [P, P])
        qk_ps = ps("qk_ps", [P, CH])
        gathered = [sem(f"gathered{r}") for r in range(R)]
        names = ("mods_in pos_in w_o_in combine_chain combined stats_in stats_chain var_ready std_ready rstd_ready half_ready row_ready row_turned "
                 "h_copied later_set qk_done qk_ready scored masked max_taken bias_ready exp_done inverted "
                 "normed turned0 turned1 copied0 copied1 pv_done attn_ready out_done out_added chain").split()
        S = {n: sem(n) for n in names}
        block = ctx.enter_context(nc.Block())

        ADD = tuple(4 + 5 * j for j in range(TPB))
        VAR, ROOT, INVERT = ADD[-1] + 2, ADD[-1] + 4, ADD[-1] + 6
        NORM, TURN, COPY = N - 11, N - 8, N - 7

        def batches(eng, body):
            with eng.Fori(0, B - 1) as b:
                body(b, False)
            body(B - 1, True)

        @block.sync
        def _(sp):
            load_mods(sp, d, sh, 1, 0, S["mods_in"])
            sp.dma_start(gate0[:], d["mod_rows"][0, 5].partition_broadcast(P)).then_inc(S["mods_in"], 16)
            sp.dma_start(pos[:], d["posT"]).then_inc(S["pos_in"], 16)
            sp.dma_start(w_o[:], d["woT"].rearrange("(h p) e -> p h e", p=P)).then_inc(S["w_o_in"], 16)

        @block.gpsimd
        def _(pool):
            def fetch(i):
                if i >= R:
                    pool.wait_ge(S["combined"], i - R + 1)
                for k in range(2):
                    nc.gpsimd.indirect_dma_start(out=y[:, i % R, k, :], out_offset=None, in_=d["outs0"],
                                                 in_offset=bass.IndirectOffsetOnAxis(ap=sh.slot_of[:, k, i:i + 1], axis=0)
                                                 ).then_inc(gathered[i % R], 16)

            for i in range(TPB):
                fetch(i)
            nc.gpsimd.memset(hidden_pos[:], 0.0).then_inc(S["later_set"], 1)
            pool.wait_ge(S["later_set"], 1)
            nc.gpsimd.affine_select(out=hidden_pos[:], in_=hidden_pos[:], compare_op=ALU.is_ge, fill=-3e38, base=0,
                                    pattern=[[-1, P]], channel_multiplier=1).then_inc(S["later_set"], 1)
            for i in range(TPB, TILES):
                fetch(i)

        def bank(n):
            return s_ps[n // 2 % 2][:, (n % 2) * CH:(n % 2 + 1) * CH]

        def piece_bank(h, i):
            return qk_ps[:] if h else bank(i)

        @block.tensor
        def _(pe):
            for name in ("qk_done", "qk_ready", "out_added", "pv_done", "attn_ready", "copied0", "copied1", "h_copied"):
                pe.sem_inc(S[name], 1)
            pe.sem_inc(S["row_turned"], 4)
            pe.wait_ge(sh.att_w_in, 16)
            pe.wait_ge(S["w_o_in"], 16)

            def turn_rows(nb, j):
                pe.wait_ge(S["row_ready"], nb * TPB + j + 1)
                pe.wait_ge(S["h_copied"], nb * TPB + j + 1)
                if j == 0:
                    pe.wait_ge(S["qk_ready"], nb * (HEADS * PIECES) + 1)
                for k in range(KE):
                    last = nc.tensor.transpose(qk_ps[:, k * P:(k + 1) * P], rows[:, j % 4, k * P:(k + 1) * P], sh.ident[:])
                last.then_inc(S["row_turned"], 1)

            for j in range(TPB):
                turn_rows(0, j)

            def batch(b, last_batch):
                def project(h, i):
                    out = piece_bank(h, i)
                    """Piece i of head h: queries (0, 1) and keys (2, 3), turned, and values (4, 5) by tiles of tokens."""
                    if h > 0:
                        pe.wait_ge(S["qk_ready"], b * (HEADS * PIECES) + h * PIECES + i + 1)
                    elif i >= 4:
                        pe.wait_ge(S["qk_ready"], b * (HEADS * PIECES) + i - 2)
                    if i < 4:
                        for k in range(KE):
                            last = nc.tensor.matmul(out, w_qkv[:, k, h, i // 2, :], h_b[:, i % 2, k, :], start=(k == 0), stop=(k == KE - 1))
                    else:
                        for t in range(CT):
                            at = slice(t * P, (t + 1) * P)
                            for k in range(KE):
                                last = nc.tensor.matmul(out[:, at], h_b[:, i % 2, k, at], w_qkv[:, k, h, 2, :], start=(k == 0), stop=(k == KE - 1))
                    last.then_inc(S["qk_done"], 1)

                def score(n):
                    h, i = n // TPB, n % TPB
                    if i == 0:
                        pe.wait_ge(S["qk_ready"], b * (HEADS * PIECES) + h * PIECES + (4 if h else PIECES) + 1)
                    if n >= 2:
                        pe.wait_ge(S["exp_done"], b * N + n - 1)
                    for part in range(i // CT + 1):
                        end = min((i + 1) * P, (part + 1) * CH)
                        last = nc.tensor.matmul(s_ps[n % 2][:, part * CH:end], qk[:, h % 2, 0, i * P:(i + 1) * P],
                                                qk[:, h % 2, 1, part * CH:end], start=True, stop=True)
                    last.then_inc(S["scored"], 1)

                def turn(n):
                    i = n % TPB
                    pe.wait_ge(S["normed"], b * N + n + 1)
                    for half in range(i // CT + 1):
                        pe.wait_ge(S[f"copied{half}"], (b * N + n + 1) if half == 0 else (b * (N // 2) + n // TPB * CT + i - CT + 1))
                        for j in range(half * CT, min(i + 1, (half + 1) * CT)):
                            last = nc.tensor.transpose(pt_ps[half][:, j % CT, :], probs[:, n % 3, j * P:(j + 1) * P], sh.ident[:])
                        last.then_inc(S[f"turned{half}"], 1)

                def weigh(n):
                    h, i = n // TPB, n % TPB
                    pe.wait_ge(S["copied0"], b * N + n + 2)
                    if i >= CT:
                        pe.wait_ge(S["copied1"], b * (N // 2) + h * CT + i - CT + 2)
                    pe.wait_ge(S["attn_ready"], b * N + n + 1)
                    if i == 0:
                        pe.wait_ge(S["qk_ready"], b * (HEADS * PIECES) + (h + 1) * PIECES + 1)
                    for j in range(i + 1):
                        last = nc.tensor.matmul(o_ps[:], v[:, h % 2, j, :], pt[:, n % 2, j, :], start=(j == 0), stop=(j == i))
                    last.then_inc(S["pv_done"], 1)

                def output(t):
                    if t >= 4:
                        pe.wait_ge(S["out_added"], b * TPB + t - 2)
                    for h in range(HEADS):
                        last = nc.tensor.matmul(bank(t)[:, 0:E], attn[:, h, t * P:(t + 1) * P], w_o[:, h, :],
                                                start=(h == 0), stop=(h == HEADS - 1))
                    last.then_inc(S["out_done"], 1)

                pe.wait_ge(S["h_copied"], b * TPB + TPB + 1)
                pe.wait_ge(S["out_added"], b * TPB + 1)
                for i in range(PIECES):
                    project(0, i)
                for n in range(N + 3):
                    if n < N:
                        score(n)
                    if n < N and n % TPB in PROJECT and n // TPB + 1 < HEADS:
                        project(n // TPB + 1, PROJECT.index(n % TPB))
                    if 2 <= n < N + 2:
                        turn(n - 2)
                    if not last_batch and TURN <= n < TURN + TPB:
                        turn_rows(b + 1, n - TURN)
                    if n >= 3:
                        weigh(n - 3)
                pe.wait_ge(S["attn_ready"], b * N + N + 1)
                for t in range(TPB):
                    output(t)

            batches(pe, batch)

        @block.scalar
        def _(act):
            def root(nb):
                act.wait_ge(S["var_ready"], nb + 1)
                of_batch = bass.ds(nb * TPB, TPB)
                nc.scalar.activation(sh.var[:, of_batch], sh.var[:, of_batch], ACT.Sqrt).then_inc(S["std_ready"], 1)

            def copy_rows(nb, j):
                act.wait_ge(S["row_turned"], nb * TPB + j + 5)
                if j == 0:
                    act.wait_ge(S["qk_done"], nb * (HEADS * PIECES) + 1)
                nc.scalar.copy(h_b[:, j // CT, :, (j % CT) * P:(j % CT + 1) * P],
                               qk_ps[:, 0:KE * P].rearrange("p (k t) -> p k t", k=KE)).then_inc(S["h_copied"], 1)

            root(0)
            for j in range(TPB):
                copy_rows(0, j)

            def batch(b, last_batch):
                def exponential(n):
                    i = n % TPB
                    act.wait_ge(S["bias_ready"], b * N + n + 1)
                    if n >= 3:
                        act.wait_ge(S[f"turned{(n - 3) % TPB // CT}"],
                                    (b * N + n - 2) if (n - 3) % TPB < CT else (b * (N // 2) + (n - 3) // TPB * CT + (n - 3) % TPB - CT + 1))
                    nc.scalar.activation(probs[:, n % 3, 0:(i + 1) * P], s_ps[n % 2][:, 0:(i + 1) * P], ACT.Exp,
                                         bias=small[:, n % 4, 1:2], scale=SCALE, accum_out=small[:, n % 4, 2:3]).then_inc(S["exp_done"], 1)

                def copy_turned(n):
                    i = n % TPB
                    for half in range(i // CT + 1):
                        m = min(i + 1, (half + 1) * CT) - half * CT
                        act.wait_ge(S[f"turned{half}"], (b * N + n + 1) if half == 0 else (b * (N // 2) + n // TPB * CT + i - CT + 1))
                        if n >= 2 and half == 0:
                            act.wait_ge(S["pv_done"], b * N + n)
                        nc.scalar.copy(pt[:, n % 2, half * CT:half * CT + m, :], pt_ps[half][:, 0:m, :]).then_inc(S[f"copied{half}"], 1)

                for n in range(N + 2):
                    if n >= 2:
                        copy_turned(n - 2)
                    if not last_batch and COPY <= n < COPY + TPB:
                        copy_rows(b + 1, n - COPY)
                    if n < N:
                        exponential(n)
                    if not last_batch and n == ROOT:
                        root(b + 1)

            batches(act, batch)

        @block.vector
        def _(dve):
            STATS_OPS = 6

            def combine(nb, j):
                tile, r, t = nb * TPB + j, j % R, tmp[:, j % 2, :]
                dve.wait_ge(gathered[r], nb * (32 * TPB // R) + 32 * (j // R + 1))
                nc.vector.tensor_scalar(t, y[:, r, 0, :], sh.weight[:, 0, bass.ds(tile, 1)], None, ALU.mult).then_inc(S["combine_chain"], 1)
                dve.wait_ge(S["combine_chain"], tile * 3 + 1)
                nc.vector.scalar_tensor_tensor(out=t, in0=y[:, r, 1, :], scalar=sh.weight[:, 1, bass.ds(tile, 1)], in1=t,
                                               op0=ALU.mult, op1=ALU.add).then_inc(S["combine_chain"], 1)
                dve.wait_ge(S["combine_chain"], tile * 3 + 2)
                nc.vector.tensor_tensor(t, t, gate0[:, nb, :], ALU.mult).then_inc(S["combine_chain"], 1)
                dve.wait_ge(S["combine_chain"], tile * 3 + 3)
                nc.vector.tensor_tensor(sh.x[:, tile, :], sh.x[:, tile, :], t, ALU.add).then_inc(S["combined"], 1)
                dve.wait_ge(S["combined"], tile + 1)
                nc.vector.bn_stats(sh.stats[:, tile, :], sh.x[:, tile, :]).then_inc(S["stats_in"], 1)

            def variance(nb):
                at = bass.ds(nb * TPB, TPB)
                stat = lambda i: sh.stats[:, at, i]
                mean, dif, var = sh.mean[:, at], sh.dif[:, at], sh.var[:, at]
                count = [0]

                def link(ins):
                    count[0] += 1
                    ins.then_inc(S["stats_chain"], 1)
                    dve.wait_ge(S["stats_chain"], nb * STATS_OPS + count[0])

                dve.wait_ge(S["stats_in"], nb * TPB + TPB)
                link(nc.vector.tensor_tensor(mean, stat(1), stat(4), ALU.add))
                link(nc.vector.tensor_scalar(mean, mean, 0.5, None, ALU.mult))
                link(nc.vector.tensor_tensor(dif, stat(1), stat(4), ALU.subtract))
                link(nc.vector.tensor_tensor(dif, dif, dif, ALU.mult))
                link(nc.vector.tensor_tensor(var, stat(2), stat(5), ALU.add))
                link(nc.vector.tensor_scalar(dif, dif, 0.25, EPS_LN, ALU.mult, ALU.add))
                nc.vector.scalar_tensor_tensor(out=var, in0=var, scalar=1.0 / E, in1=dif, op0=ALU.mult, op1=ALU.add).then_inc(S["var_ready"], 1)

            def invert(nb):
                at = bass.ds(nb * TPB, TPB)
                dve.wait_ge(S["std_ready"], nb + 1)
                nc.vector.reciprocal(sh.rstd[:, at], sh.var[:, at]).then_inc(S["rstd_ready"], 1)

            def normalise_rows(nb, j):
                tile = nb * TPB + j
                if j == 0:
                    dve.wait_ge(S["rstd_ready"], nb + 1)
                dve.wait_ge(S["row_turned"], tile + 1)
                nc.vector.scalar_tensor_tensor(out=rows[:, j % 4, :], in0=sh.x[:, tile, :], scalar=sh.mean[:, bass.ds(tile, 1)],
                                               in1=sh.mods[:, 1, nb, :], op0=ALU.subtract, op1=ALU.mult).then_inc(S["half_ready"], 1)
                dve.wait_ge(S["half_ready"], tile + 1)
                nc.vector.scalar_tensor_tensor(out=rows[:, j % 4, :], in0=rows[:, j % 4, :], scalar=sh.rstd[:, bass.ds(tile, 1)],
                                               in1=sh.mods[:, 0, nb, :], op0=ALU.mult, op1=ALU.add).then_inc(S["row_ready"], 1)

            dve.wait_ge(S["mods_in"], 32)
            for j in range(TPB):
                combine(0, j)
            variance(0)
            invert(0)
            for j in range(TPB):
                normalise_rows(0, j)
            dve.wait_ge(S["pos_in"], 16)
            dve.wait_ge(S["later_set"], 2)

            def batch(b, last_batch):
                def take_piece(h, i):
                    dve.wait_ge(S["qk_done"], b * (HEADS * PIECES) + h * PIECES + i + 2)
                    if i == 0 and h >= 2:
                        dve.wait_ge(S["scored"], b * N + (h - 1) * TPB)
                    if i < 4:
                        nc.vector.tensor_tensor(qk[:, h % 2, i // 2, (i % 2) * CH:(i % 2 + 1) * CH], piece_bank(h, i),
                                                pos[:, (i % 2) * CH:(i % 2 + 1) * CH], ALU.add).then_inc(S["qk_ready"], 1)
                    else:
                        dve.wait_ge(S["pv_done"], b * N + max(h - 1, 0) * TPB + 1)
                        nc.vector.tensor_copy(v[:, h % 2, (i % 2) * CT:(i % 2 + 1) * CT, :],
                                              piece_bank(h, i).rearrange("p (t f) -> p t f", t=CT)).then_inc(S["qk_ready"], 1)

                def maximum(n):
                    i = n % TPB
                    diagonal = s_ps[n % 2][:, i * P:(i + 1) * P]
                    dve.wait_ge(S["scored"], b * N + n + 1)
                    nc.vector.tensor_tensor(diagonal, diagonal, hidden_pos[:], ALU.add).then_inc(S["masked"], 1)
                    dve.wait_ge(S["masked"], b * N + n + 1)
                    nc.vector.reduce_max(small[:, n % 4, 0:1], s_ps[n % 2][:, 0:(i + 1) * P], AX_X).then_inc(S["max_taken"], 1)
                    dve.wait_ge(S["max_taken"], b * N + n + 1)
                    nc.vector.tensor_scalar(small[:, n % 4, 1:2], small[:, n % 4, 0:1], -SCALE, None, ALU.mult).then_inc(S["bias_ready"], 1)

                def normalise(n):
                    i = n % TPB
                    dve.wait_ge(S["exp_done"], b * N + n + 1)
                    nc.vector.reciprocal(small[:, n % 4, 3:4], small[:, n % 4, 2:3]).then_inc(S["inverted"], 1)
                    dve.wait_ge(S["inverted"], b * N + n + 1)
                    row = probs[:, n % 3, 0:(i + 1) * P]
                    nc.vector.tensor_scalar(row, row, small[:, n % 4, 3:4], None, ALU.mult).then_inc(S["normed"], 1)

                def keep(n):
                    h, i = n // TPB, n % TPB
                    dve.wait_ge(S["pv_done"], b * N + n + 2)
                    nc.vector.tensor_copy(attn[:, h, i * P:(i + 1) * P], o_ps[:]).then_inc(S["attn_ready"], 1)

                for i in range(PIECES):
                    take_piece(0, i)
                for n in range(N + 4):
                    if n >= 4:
                        keep(n - 4)
                    if not last_batch:
                        if n in ADD:
                            combine(b + 1, ADD.index(n))
                        if n == VAR:
                            variance(b + 1)
                        if n == INVERT:
                            invert(b + 1)
                        if NORM <= n < NORM + TPB:
                            normalise_rows(b + 1, n - NORM)
                    if n < N:
                        maximum(n)
                    if 1 <= n <= N:
                        normalise(n - 1)
                    if n < N and n % TPB in PROJECT and n // TPB + 1 < HEADS:
                        take_piece(n // TPB + 1, PROJECT.index(n % TPB))
                for t in range(TPB):
                    tile = b * TPB + t
                    dve.wait_ge(S["out_done"], tile + 1)
                    nc.vector.tensor_tensor(gated[:, t % 2, :], bank(t)[:, 0:E], sh.mods[:, 2, b, :], ALU.mult).then_inc(S["out_added"], 1)
                    dve.wait_ge(S["out_added"], tile + 2)
                    nc.vector.tensor_tensor(sh.x[:, tile, :], sh.x[:, tile, :], gated[:, t % 2, :], ALU.add).then_inc(S["chain"], 1)
                    dve.wait_ge(S["chain"], tile + 1)
                    nc.vector.bn_stats(sh.stats[:, tile, :], sh.x[:, tile, :])

            batches(dve, batch)


def dev_fill(nc, d, sh):
    with ExitStack() as ctx:
        filled = ctx.enter_context(nc.semaphore("filled"))
        block = ctx.enter_context(nc.Block())

        @block.sync
        def _(sp):
            n = 0
            for name, tiles, first in (("slots0", TILES0, 0), ("slots1", EXPERTS1 * CAP1 // P, 0), ("outs1", 1, EXPERTS1 * CAP1 // P)):
                for t in range(tiles):
                    sp.dma_start(d[name][(first + t) * P:(first + t + 1) * P], sh.zeros[:]).then_inc(filled, 16)
                    n += 16
            sp.wait_ge(filled, n)


def store_x(nc, d, sh):
    with ExitStack() as ctx:
        stored = ctx.enter_context(nc.semaphore("stored"))
        block = ctx.enter_context(nc.Block())

        @block.sync
        def _(sp):
            sp.dma_start(token_tiles(d["out"]), sh.x[:]).then_inc(stored, 16)
            sp.wait_ge(stored, 16)


def program(nc, d, stop=99, start=0):
    sh = Shared()
    with ExitStack() as ctx:
        sb = lambda name, shape, dt=F32: ctx.enter_context(nc.sbuf_tensor(name, shape, dt))
        sh.x = sb("x", [P, TILES, E])
        sh.mods = sb("mods", [P, 3, B, E])
        sh.ident = sb("ident", [P, P])
        sh.zeros = sb("zeros", [P, E])
        sh.stats = sb("stats", [P, TILES, 6])
        sh.mean, sh.var, sh.rstd, sh.dif = (sb(name, [P, TILES]) for name in ("mean", "var", "rstd", "dif"))
        sh.slot_of = sb("slot_of", [P, 2, TILES], U32)
        sh.weight = sb("weight", [P, 2, TILES])
        sh.owner_i = sb("owner_i", [P, TILES0], I32)
        with ExitStack() as layer:
            sl = lambda name, shape: layer.enter_context(nc.sbuf_tensor(name, shape, F32))
            sh.w_in = sl("w_in", [P, KE, 2 * DI])
            sh.w_out = sl("w_out", [P, MD, E])
            sh.w_x = sl("w_x", [P, MD, 1 + 2 * NS])
            sh.w_delta = sl("w_delta", [P, MD, P])
            sh.conv_w = sl("conv_w", [P, MD, DC])
            sh.vecs = sl("inner_vecs", [P, 4, MD])
            sh.a_neg = sl("a_neg", [P, MD, NS])
            phase_prepare(nc, d, sh)
            if start >= 1:
                dev_fill(nc, d, sh)
            if start < 1:
                phase_norm_turn(nc, d, sh, 0)
                phase_mamba(nc, d, sh)
        if stop >= 3:
          with ExitStack() as attention_weights:
            aw = lambda name, shape: attention_weights.enter_context(nc.sbuf_tensor(name, shape, F32))
            sh.w_qkv = aw("w_qkv", [P, KE, HEADS, 3, DH])
            sh.att_w_in = attention_weights.enter_context(Semaphores(nc, "aw_"))("loaded")
            with ExitStack() as expert_weights:
                ew = lambda name, shape: expert_weights.enter_context(nc.sbuf_tensor(name, shape, F32))
                sh.w13 = ew("w13", [P, EXPERTS0, 2, KE, H0])
                sh.w2_0 = ew("w2_0", [P, EXPERTS0, MH0, E])
                sh.e0_w_in = expert_weights.enter_context(Semaphores(nc, "ew_"))("loaded")
                phase_route(nc, d, sh, 0, "L0_ffn_Wr", "slots0")
                phase_experts0(nc, d, sh)
            phase_attention(nc, d, sh)
        if stop >= 4:
            phase_route(nc, d, sh, 1, "gate_wT", "slots1")
            phase_experts1(nc, d, sh)
            phase_combine(nc, d, sh, 1, "outs1")
        if stop < 4:
            store_x(nc, d, sh)


_PLAIN = ["L0_attn_x", "L0_attn_W_in", "L0_attn_conv_w", "L0_attn_W_x", "L0_attn_A_log", "L0_attn_W_out", "L0_wmod", "L1_wmod",
          "L0_ffn_Wr", "L0_ffn_W1", "L0_ffn_W2", "L0_ffn_W3", "L1_ffn_w1", "L1_ffn_w2"]
_SCRATCH = {
    "mod_rows": [2, 6, B, E],
    "h_turned": [B * CPB, P, KE, CH],
    "bc_rows": [B * CPB, 2 * NS, CH],
    "slots0": [SLOTS0, E],
    "outs0": [SLOTS0, E],
    "slots1": [SLOTS1, E],
    "outs1": [SLOTS1, E],
}


def lay_out(inputs):
    get = lambda n: np.asarray(inputs[n])
    arrays = {n: np.ascontiguousarray(get(n)) for n in _PLAIN}
    cs = np.stack([get("L0_c"), get("L1_c")])
    arrays["cT"] = np.ascontiguousarray(cs.reshape(2, B, KE, P).transpose(3, 0, 2, 1))
    vecs = np.stack([get("L0_attn_conv_b"), get("L0_attn_dt_w"), get("L0_attn_dt_b"), get("L0_attn_D")])
    arrays["vecs"] = np.ascontiguousarray(vecs.reshape(4, MD, P).transpose(2, 0, 1))
    arrays["wqkvT"] = np.ascontiguousarray(get("L1_attn_Wqkv").T)
    arrays["woT"] = np.ascontiguousarray(get("L1_attn_Wo").T)
    arrays["gate_wT"] = np.ascontiguousarray(get("L1_ffn_gate_w").T)
    arrays["posT"] = positions()
    return arrays


def positions():
    t = np.arange(T, dtype=np.float32)[:, None]
    div = np.exp(np.arange(0, DH, 2, dtype=np.float32) * np.float32(-np.log(10000.0) / DH))
    angle = t * div
    return np.ascontiguousarray(np.stack([np.sin(angle), np.cos(angle)], axis=-1).reshape(T, DH).T)


def declare(nc, arrays):
    d = {n: nc.dram_tensor(n, list(a.shape), F32, kind="ExternalInput").ap() for n, a in arrays.items()}
    for n, shape in _SCRATCH.items():
        d[n] = nc.dram_tensor(n, shape, F32).ap()
    d["out"] = nc.dram_tensor("out", [B, T, E], F32, kind="ExternalOutput").ap()
    return d


def kernel(**inputs):
    import concourse.bacc as bacc
    from concourse.bass_utils import run_bass_kernel_spmd

    nc = bacc.Bacc("TRN2", target_bir_lowering=False, num_devices=1)
    arrays = lay_out(inputs)
    program(nc, declare(nc, arrays))
    return run_bass_kernel_spmd(nc, [arrays], core_ids=[0]).results[0]["out"]
```

```python
from contextlib import ExitStack

import numpy as np

import concourse.bass as bass
from concourse import mybir

ALU = mybir.AluOpType
ACT = mybir.ActivationFunctionType
F32 = mybir.dt.float32
U32, I32 = mybir.dt.uint32, mybir.dt.int32
AX_X = mybir.AxisListType.X

P = 128
B, T, E = 4, 1024, 256
TILES = B * T // P
TPB = T // P
KE = E // P
EPS_LN = 1e-5

DI, NS, DC = 512, 16, 4
MD = DI // P
CH = 512
CPB = T // CH
CT = CH // P
G = 2
NG = NS // G
STEPS = NG * MD
RING, RING_A, RING_B = 4, 8, 2

EXPERTS0, H0 = 8, 384
MH0 = H0 // P
SLOTS0 = 2 * B * T + EXPERTS0 * P
TILES0 = SLOTS0 // P

HEADS, DH = 8, 128
EXPERTS1, F1 = 16, 512
MF1 = F1 // P
CAP1 = int(1.25 * B * T * 2 / EXPERTS1)
SLOTS1 = EXPERTS1 * CAP1 + P
FILL0, FILL1 = TILES0 // (B * CPB), EXPERTS1 * CAP1 // P // (B * CPB)


def token_tiles(ap):
    return ap.rearrange("b (j p) e -> p (b j) e", p=P)


class Shared:
    pass


class Semaphores:

    def __init__(self, nc, prefix):
        self.nc, self.prefix, self.taken = nc, prefix, []

    def __enter__(self):
        return self

    def __call__(self, name):
        self.taken.append(self.nc.alloc_semaphore(self.prefix + name))
        return self.taken[-1]

    def __exit__(self, *failure):
        if not any(failure):
            self.nc.clear_and_free_semaphores(self.taken)
            self.nc.all_engine_barrier()


def link_on(eng, sem):
    count = [0]

    def link(ins):
        count[0] += 1
        ins.then_inc(sem, 1)
        eng.wait_ge(sem, count[0])

    return link


def phase_prepare(nc, d, sh):
    with ExitStack() as ctx:
        sb = lambda name, shape: ctx.enter_context(nc.sbuf_tensor(name, shape, F32))
        sem = ctx.enter_context(Semaphores(nc, "prep_"))
        wmod = sb("wmod", [P, 2, KE, 6 * E])
        c_t = sb("c_t", [P, 2, KE, B])
        c_act = sb("c_act", [P, 2, KE, B])
        rows = sb("rows", [P, 2, 6, E])
        sign = sb("sign", [P, E])
        a_log = sb("a_log", [P, MD, NS])
        mod_ps = ctx.enter_context(nc.psum_tensor("mod_ps", [P, 2, 3, 512], F32))
        c_in, wmod_in, a_in, x_in = sem("c_in"), [sem("wmod0_in"), sem("wmod1_in")], sem("a_in"), [sem(f"x{b}_in") for b in range(B)]
        small_in, c_ready, mod_done, a_exp = sem("small_in"), sem("c_ready"), sem("mod_done"), sem("a_exp")
        rows_ready, rows_out, chain = sem("rows_ready"), sem("rows_out"), sem("chain")
        ident_set, wx_set = sem("ident_set"), sem("wx_set")
        block = ctx.enter_context(nc.Block())

        @block.sync
        def _(sp):
            sp.dma_start(c_t[:], d["cT"]).then_inc(c_in, 16)
            for l, name in enumerate(("L0_wmod", "L1_wmod")):
                sp.dma_start(wmod[:, l], d[name].rearrange("(k p) f -> p k f", p=P)).then_inc(wmod_in[l], 16)
            sp.dma_start(a_log[:], d["L0_attn_A_log"].rearrange("(m p) n -> p m n", p=P)).then_inc(a_in, 16)
            xt = token_tiles(d["L0_attn_x"])
            for b in range(B):
                sp.dma_start(sh.x[:, b * TPB:(b + 1) * TPB], xt[:, b * TPB:(b + 1) * TPB]).then_inc(x_in[b], 16)
            for dst, src in (
                (sh.w_in[:], d["L0_attn_W_in"].rearrange("(k p) f -> p k f", p=P)),
                (sh.w_out[:], d["L0_attn_W_out"].rearrange("(k p) f -> p k f", p=P)),
                (sh.w_x[:], d["L0_attn_W_x"].rearrange("(k p) f -> p k f", p=P)),
                (sh.conv_w[:], d["L0_attn_conv_w"].rearrange("(m p) j -> p m j", p=P)),
                (sh.vecs[:], d["vecs"]),
            ):
                sp.dma_start(dst, src).then_inc(small_in, 16)
            sp.wait_ge(rows_ready, 1)
            sp.dma_start(d["mod_rows"].rearrange("l j b e -> b l j e"), rows[0:B]).then_inc(rows_out, 16)
            sp.wait_ge(rows_out, 16)
            sp.wait_ge(small_in, 80)

        @block.gpsimd
        def _(pool):
            nc.gpsimd.memset(sh.zeros[:], 0.0)
            nc.gpsimd.memset(sh.ident[:], 0.0).then_inc(ident_set, 1)
            pool.wait_ge(ident_set, 1)
            nc.gpsimd.affine_select(out=sh.ident[:], in_=sh.ident[:], compare_op=ALU.not_equal, fill=1.0, base=0,
                                    pattern=[[-1, P]], channel_multiplier=1).then_inc(ident_set, 1)

        @block.scalar
        def _(act):
            act.wait_ge(c_in, 16)
            nc.scalar.activation(c_act[:], c_t[:], ACT.Silu).then_inc(c_ready, 1)
            act.wait_ge(a_in, 16)
            nc.scalar.activation(a_log[:], a_log[:], ACT.Exp).then_inc(a_exp, 1)

        @block.tensor
        def _(pe):
            pe.wait_ge(c_ready, 1)
            for l in range(2):
                pe.wait_ge(wmod_in[l], 16)
                for n in range(3):
                    for k in range(KE):
                        last = nc.tensor.matmul(mod_ps[0:B, l, n, :], c_act[:, l, k, :], wmod[:, l, k, n * 512:(n + 1) * 512],
                                                start=(k == 0), stop=(k == KE - 1))
                last.then_inc(mod_done, 1)

        @block.vector
        def _(dve):
            link = link_on(dve, chain)
            dve.wait_ge(a_exp, 1)
            nc.vector.tensor_scalar(sh.a_neg[:], a_log[:], -1.0, None, ALU.mult)
            for l in range(2):
                dve.wait_ge(mod_done, l + 1)
                for j in range(6):
                    src = mod_ps[0:B, l, j // 2, (j % 2) * E:(j % 2 + 1) * E]
                    dst = rows[0:B, l, j, :]
                    if j % 3 == 0:
                        last = nc.vector.tensor_copy(dst, src)
                    elif j % 3 == 1:
                        last = nc.vector.tensor_scalar(dst, src, 1.0, None, ALU.add)
                    else:
                        link(nc.vector.tensor_scalar(sign[0:B], src, 0.0, 2.0, ALU.is_ge, ALU.mult))
                        link(nc.vector.tensor_scalar(sign[0:B], sign[0:B], 1.0, None, ALU.subtract))
                        link(nc.vector.tensor_copy(dst, src))
                        link(nc.vector.scalar_tensor_tensor(out=dst, in0=dst, scalar=-1.0, in1=dst, op0=ALU.mult, op1=ALU.max))
                        link(nc.vector.tensor_scalar(dst, dst, 0.25, None, ALU.max))
                        link(nc.vector.tensor_tensor(dst, dst, sign[0:B], ALU.mult))
            dve.sem_inc(rows_ready, 1)
            for b in range(B):
                dve.wait_ge(x_in[b], 16)
                for i in range(b * TPB, (b + 1) * TPB):
                    nc.vector.bn_stats(sh.stats[:, i, :], sh.x[:, i, :])
            dve.wait_ge(small_in, 80)
            for k in range(MD):
                last = nc.vector.tensor_copy(sh.w_delta[:, k, :], sh.w_x[:, k, 0:1].broadcast_to([P, P]))
            last.then_inc(wx_set, 1)


def finish_stats(nc, dve, link, sh, std_ready, rstd_wait):
    s = sh.stats
    link(nc.vector.tensor_tensor(sh.mean[:], s[:, :, 1], s[:, :, 4], ALU.add))
    link(nc.vector.tensor_scalar(sh.mean[:], sh.mean[:], 0.5, None, ALU.mult))
    link(nc.vector.tensor_tensor(sh.dif[:], s[:, :, 1], s[:, :, 4], ALU.subtract))
    link(nc.vector.tensor_tensor(sh.dif[:], sh.dif[:], sh.dif[:], ALU.mult))
    link(nc.vector.tensor_tensor(sh.var[:], s[:, :, 2], s[:, :, 5], ALU.add))
    link(nc.vector.tensor_scalar(sh.dif[:], sh.dif[:], 0.25, EPS_LN, ALU.mult, ALU.add))
    nc.vector.scalar_tensor_tensor(out=sh.var[:], in0=sh.var[:], scalar=1.0 / E, in1=sh.dif[:],
                                   op0=ALU.mult, op1=ALU.add).then_inc(std_ready, 1)
    dve.wait_ge(rstd_wait, 1)
    link(nc.vector.reciprocal(sh.rstd[:], sh.var[:]))


def load_mods(sp, d, sh, layer, part, mods_in):
    sp.dma_start(sh.mods[:], d["mod_rows"][layer, 3 * part:3 * part + 3].partition_broadcast(P)).then_inc(mods_in, 16)


def norm_rows(nc, dve, sh, half, rows, half_ready, row_ready, rows_freed):
    ring = rows.shape[1]
    with dve.Fori(0, B) as b:
        def first_half(j):
            tile = b * TPB + j
            dve.wait_ge(row_ready, tile + 1)
            nc.vector.scalar_tensor_tensor(out=half[:, j % 4, :], in0=sh.x[:, tile, :], scalar=sh.mean[:, bass.ds(tile, 1)],
                                           in1=sh.mods[:, 1, b, :], op0=ALU.subtract, op1=ALU.mult).then_inc(half_ready, 1)

        def second_half(j):
            tile = b * TPB + j
            dve.wait_ge(half_ready, b * TPB + j + 1)
            rows_freed(b, j)
            nc.vector.scalar_tensor_tensor(out=rows[:, j % ring, :], in0=half[:, j % 4, :], scalar=sh.rstd[:, bass.ds(tile, 1)],
                                           in1=sh.mods[:, 0, b, :], op0=ALU.mult, op1=ALU.add).then_inc(row_ready, 1)

        first_half(0)
        for j in range(1, TPB):
            first_half(j)
            second_half(j - 1)
        second_half(TPB - 1)


def phase_norm_turn(nc, d, sh):
    with ExitStack() as ctx:
        sb = lambda name, shape: ctx.enter_context(nc.sbuf_tensor(f"nt_{name}", shape, F32))
        sem = ctx.enter_context(Semaphores(nc, "nt_"))
        half = sb("half", [P, 4, E])
        h_row = sb("h_row", [P, 4, E])
        h_chunk = sb("h_chunk", [P, CPB, KE, CH])
        turned = [ctx.enter_context(nc.psum_tensor(f"nt_turned{i}", [P, KE, P], F32)) for i in range(4)]
        mods_in, var_ready, std_ready, chain = sem("mods_in"), sem("var_ready"), sem("std_ready"), sem("chain")
        half_ready, row_ready, turn_done, turn_copied = sem("half_ready"), sem("row_ready"), sem("turn_done"), sem("turn_copied")
        stored = [sem(f"stored{i}") for i in range(CPB)]
        block = ctx.enter_context(nc.Block())

        @block.sync
        def _(sp):
            load_mods(sp, d, sh, 0, 0, mods_in)
            with sp.Fori(0, B) as b:
                for th in range(CPB):
                    sp.wait_ge(turn_copied, b * TPB + (th + 1) * CT + 4)
                    sp.dma_start(d["h_turned"][bass.ds(b * CPB + th, 1)].rearrange("o p k t -> (o p) k t"),
                                 h_chunk[:, th]).then_inc(stored[th], 16)
            for th in range(CPB):
                sp.wait_ge(stored[th], 16 * B + 1)

        @block.scalar
        def _(act):
            act.wait_ge(var_ready, 1)
            nc.scalar.activation(sh.var[:], sh.var[:], ACT.Sqrt).then_inc(std_ready, 1)
            with act.Fori(0, B) as b:
                for j in range(TPB):
                    if j % CT == 0:
                        act.wait_ge(stored[j // CT], b * 16 + 1)
                    act.wait_ge(turn_done, b * TPB + j + 5)
                    nc.scalar.copy(h_chunk[:, j // CT, :, (j % CT) * P:(j % CT + 1) * P], turned[j % 4][:]).then_inc(turn_copied, 1)

        @block.tensor
        def _(pe):
            pe.sem_inc(turn_done, 4)
            pe.sem_inc(turn_copied, 4)
            pe.sem_inc(row_ready, 4)
            for th in range(CPB):
                pe.sem_inc(stored[th], 1)
            with pe.Fori(0, B) as b:
                for j in range(TPB):
                    pe.wait_ge(row_ready, b * TPB + j + 5)
                    pe.wait_ge(turn_copied, b * TPB + j + 1)
                    for k in range(KE):
                        last = nc.tensor.transpose(turned[j % 4][:, k, :], h_row[:, j % 4, k * P:(k + 1) * P], sh.ident[:])
                    last.then_inc(turn_done, 1)

        @block.vector
        def _(dve):
            link = link_on(dve, chain)
            finish_stats(nc, dve, link, sh, var_ready, std_ready)
            dve.wait_ge(mods_in, 16)
            norm_rows(nc, dve, sh, half, h_row, half_ready, row_ready, lambda b, j: dve.wait_ge(turn_done, b * TPB + j + 1))


def phase_mamba(nc, d, sh):
    with ExitStack() as ctx:
        sb = lambda name, shape: ctx.enter_context(nc.sbuf_tensor(name, shape, F32))
        ps = lambda name, shape: ctx.enter_context(nc.psum_tensor(name, shape, F32))
        sem = ctx.enter_context(Semaphores(nc, "ss_"))
        x_main = sb("x_main", [P, 2, DC - 1 + CH])
        tail = sb("tail", [P, MD, DC - 1])
        x_conv = sb("x_conv", [P, 2, MD, CH])
        gate = sb("gate", [P, 2, MD, CH])
        delta = sb("delta", [P, 2, MD, CH])
        u = sb("u", [P, 2, MD, CH])
        h_in = sb("h_in", [P, 2, KE, CH])
        bc_sb = sb("bc_sb", [P, CH])
        b_all = sb("b_all", [P, RING_B, G, CH])
        c_all = sb("c_all", [P, RING_B, G, CH])
        da = sb("da", [P, RING_A, G, CH])
        dbx = sb("dbx", [P, RING, G, CH])
        state = sb("state", [P, STEPS, G])
        gated = sb("gated", [P, E])
        d_diag = sb("d_diag", [P, MD, P])
        y_ps = [ps(f"y_ps{m}", [P, CH]) for m in range(MD)]
        proj_ps = [ps(f"proj_ps{i}", [P, CH]) for i in range(2)]
        out_ps = [ps(f"out_ps{i}", [P, E]) for i in range(2)]

        PE_MAIN, PE_OUT, PE_BC, PE_Z = (1, 3, 5, 7), 11, 14, (18, 20, 22, 24)
        ACT_MAIN, ACT_SILU, ACT_BC, ACT_SOFT, ACT_Z = (8, 10, 12, 14), 17, 21, 27, (25, 27, 29, 31)
        DVE_CONV, DVE_OUT, DVE_DELTA = (6, 9, 12, 15), 15, 27
        ACT_Y, POOL_GATE, POOL_U = 2, 7, 31

        names = ("proj_done proj_copied conv_chain conv_done conv_act z_act bc_done delta_done bc_copied bc_stored raw_ready "
                 "soft_chain soft_ready delta_ready u_ready da_ready dbx_ready scanned states_kept hc_ready summed "
                 "y_taken y_gated diag_set out_done out_chain out_added tail_kept head_set filled").split()
        S = {n: sem(n) for n in names}
        bc_loaded = [sem(f"bc_loaded{i}") for i in range(RING_B)]
        h_loaded = [sem("h_loaded0"), sem("h_loaded1")]
        block = ctx.enter_context(nc.Block())

        def chunks(eng, body):
            for th in range(CPB):
                body(th, 0, th, th == 0, False)
            with eng.Fori(1, B - 1) as b:
                for th in range(CPB):
                    body(b * CPB + th, b, th, False, False)
            for th in range(CPB):
                body((B - 1) * CPB + th, B - 1, th, False, th == CPB - 1)

        zeros_over = lambda tiles: sh.zeros[:].rearrange("p (o e) -> p o e", o=1).broadcast_to([P, tiles, E])

        @block.sync
        def _(sp):
            def store_rows(c):
                sp.wait_ge(S["bc_copied"], c + 1)
                sp.dma_start(d["bc_rows"][bass.ds(c, 1)].rearrange("o n t -> (o n) t"), bc_sb[0:2 * NS, :]).then_inc(S["bc_stored"], 16)

            def load_group(c, g, first):
                if not (first and g < RING_B):
                    sp.wait_ge(S["dbx_ready"], c * STEPS + (g + 1 - RING_B) * MD)
                    sp.wait_ge(S["hc_ready"], c * STEPS + (g + 1 - RING_B) * MD)
                if g == 0:
                    sp.wait_ge(S["bc_stored"], c * 16 + 16)
                for dst, row in ((b_all, 0), (c_all, NS)):
                    src = d["bc_rows"][bass.ds(c, 1), row + g * G:row + (g + 1) * G, :].rearrange("o n t -> (o n) t")
                    sp.dma_start(dst[:, g % RING_B], src.partition_broadcast(P)).then_inc(bc_loaded[g % RING_B], 16)

            def load_h(c, b, p, first):
                if not first:
                    sp.wait_ge(S["proj_done"], c * 8 - 8)
                sp.dma_start(h_in[:, p], d["h_turned"][bass.ds(c, 1)].rearrange("o p k t -> (o p) k t")).then_inc(h_loaded[p], 16)

            def fill(c, g):
                rows, n, tiles = (d["slots0"], g, 3) if g < FILL0 // 3 else (d["slots1"], g - FILL0 // 3, 2)
                first_row = c * ((FILL0 if g < FILL0 // 3 else FILL1) * P) + n * tiles * P
                part = rows[bass.ds(first_row, tiles * P), :].rearrange("(a p) e -> p a e", p=P)
                sp.dma_start(part, zeros_over(tiles)).then_inc(S["filled"], 16)

            def body(c, b, th, first, last):
                for g in range(NG):
                    load_group(c, g, first)
                    fill(c, g)
                    if g == 4 and not (last or (isinstance(c, int) and c >= B * CPB - 2)):
                        load_h(c + 2, b + 1, th, False)
                if not last:
                    store_rows(c + 1)

            load_h(0, 0, 0, True)
            load_h(1, 0, 1, True)
            store_rows(0)
            for rows in (d["slots1"][FILL1 * P * B * CPB:], d["outs1"][EXPERTS1 * CAP1:]):
                sp.dma_start(rows.rearrange("(a p) e -> p a e", p=P), zeros_over(rows.shape[0] // P)).then_inc(S["filled"], 16)
            chunks(sp, body)
            sp.wait_ge(S["filled"], 16 * (NG * B * CPB + 2))

        @block.tensor
        def _(pe):
            def project(c, b, p, m, first):
                if m == 0:
                    pe.wait_ge(h_loaded[p], b * 16 + 16)
                if m in (MD, MD + 1):
                    pe.wait_ge(S["raw_ready" if m > MD else "bc_copied"], c + 1)
                elif not (first and m < 2):
                    pe.wait_ge(S["proj_copied"], c * 8 + m - 1)
                for k in range(KE):
                    mm = nc.tensor.matmul(proj_ps[m % 2][:], sh.w_in[:, k, m * P:(m + 1) * P], h_in[:, p, k, :],
                                          start=(k == 0), stop=(k == KE - 1))
                mm.then_inc(S["proj_done"], 1)

            def bc_product(c, p):
                pe.wait_ge(S["conv_act"], c + 1)
                pe.wait_ge(S["proj_copied"], c * 8 + 3)
                for k in range(MD):
                    mm = nc.tensor.matmul(proj_ps[0][0:2 * NS, :], sh.w_x[:, k, 1:1 + 2 * NS], x_conv[:, p, k, :],
                                          start=(k == 0), stop=(k == MD - 1))
                mm.then_inc(S["bc_done"], 1)

            def delta_product(c, p):
                pe.wait_ge(S["proj_copied"], c * 8 + 4)
                for k in range(MD):
                    mm = nc.tensor.matmul(proj_ps[1][:], sh.w_delta[:, k, :], x_conv[:, p, k, :],
                                          start=(k == 0), stop=(k == MD - 1))
                mm.then_inc(S["delta_done"], 1)

            def sum_states(c, p, s, first):
                g, m = s // MD, s % MD
                pe.wait_ge(S["hc_ready"], c * STEPS + s + 1)
                if g == 0:
                    if not first:
                        pe.wait_ge(S["y_taken"], (c - 1) * MD + m + 1)
                    nc.tensor.matmul(y_ps[m][:], d_diag[:, m, :], x_conv[:, p, m, :], start=True, stop=False)
                for i in range(G):
                    mm = nc.tensor.matmul(y_ps[m][:], sh.ident[:], da[:, s % RING_A, i, :],
                                          start=False, stop=(g == NG - 1 and i == G - 1))
                mm.then_inc(S["summed"], 1)

            def out_product(c, p, j, first):
                pe.wait_ge(S["y_gated"], (c + 1) * MD)
                if not (first and j < 2):
                    pe.wait_ge(S["out_added"], c * CT + j - 1)
                for k in range(MD):
                    mm = nc.tensor.matmul(out_ps[j % 2][:], u[:, p, k, j * P:(j + 1) * P], sh.w_out[:, k, :],
                                          start=(k == 0), stop=(k == MD - 1))
                mm.then_inc(S["out_done"], 1)

            def body(c, b, th, first, last):
                for s in range(STEPS):
                    sum_states(c, th, s, first)
                    if not last:
                        if s in PE_MAIN:
                            project(c + 1, b + th, 1 - th, PE_MAIN.index(s), False)
                        if s == PE_BC:
                            bc_product(c + 1, 1 - th)
                        if s == PE_BC + 1:
                            delta_product(c + 1, 1 - th)
                        if s in PE_Z:
                            project(c + 1, b + th, 1 - th, MD + PE_Z.index(s), False)
                    if not first and PE_OUT <= s < PE_OUT + CT:
                        out_product(c - 1, 1 - th, s - PE_OUT, isinstance(c, int) and c == 1)

            pe.wait_ge(S["diag_set"], MD)
            for m in range(MD):
                project(0, 0, 0, m, True)
            bc_product(0, 0)
            delta_product(0, 0)
            for m in range(MD, 2 * MD):
                project(0, 0, 0, m, True)
            chunks(pe, body)
            for j in range(CT):
                out_product(B * CPB - 1, 1, j, False)

        @block.scalar
        def _(act):
            def copy_out(c, p, m):
                act.wait_ge(S["proj_done"], c * 8 + m + 1)
                if m < MD:
                    dst = x_main[:, m % 2, DC - 1:]
                    if m >= 2 or not (isinstance(c, int) and c == 0):
                        act.wait_ge(S["tail_kept"], (c * MD + m - 1))
                else:
                    dst = gate[:, p, m - MD, :]
                if m < MD:
                    nc.scalar.activation(delta[:, p, m, :], proj_ps[m % 2][:], ACT.Identity, bias=sh.vecs[:, 0, m:m + 1],
                                         scale=sh.conv_w[:, m, DC - 1:DC])
                nc.scalar.copy(dst, proj_ps[m % 2][:]).then_inc(S["proj_copied"], 1)

            def silu_conv(c, p):
                act.wait_ge(S["conv_done"], (c + 1) * MD)
                nc.scalar.activation(x_conv[:, p], delta[:, p], ACT.Silu).then_inc(S["conv_act"], 1)

            def silu_z(c, p):
                act.wait_ge(S["proj_copied"], c * 8 + 8)
                nc.scalar.activation(gate[:, p], gate[:, p], ACT.Silu).then_inc(S["z_act"], 1)

            def copy_bc(c, first):
                act.wait_ge(S["bc_done"], c + 1)
                if not first:
                    act.wait_ge(S["bc_stored"], c * 16)
                nc.scalar.copy(bc_sb[0:2 * NS, :], proj_ps[0][0:2 * NS, :]).then_inc(S["bc_copied"], 1)

            def softplus(c, p, first):
                act.wait_ge(S["delta_done"], c + 1)
                if not first:
                    act.wait_ge(S["out_done"], (c - 1) * CT)
                for m in range(MD):
                    for dst, fun in ((delta, ACT.Relu), (u, ACT.Abs)):
                        ins = nc.scalar.activation(dst[:, p, m, :], proj_ps[1][:], fun, bias=sh.vecs[:, 2, m:m + 1],
                                                   scale=sh.vecs[:, 1, m:m + 1])
                ins.then_inc(S["raw_ready"], 1)
                act.wait_ge(S["raw_ready"], c + 1)
                nc.scalar.activation(u[:, p], u[:, p], ACT.Exp, scale=-1.0).then_inc(S["soft_chain"], 1)
                act.wait_ge(S["soft_chain"], c + 1)
                nc.scalar.activation(u[:, p], u[:, p], ACT.Ln, bias=1.0).then_inc(S["soft_ready"], 1)

            def decays(c, p, s, first):
                g, m = s // MD, s % MD
                if s == 0:
                    act.wait_ge(S["delta_ready"], c + 1)
                if not (first and s < RING_A):
                    act.wait_ge(S["summed"], c * STEPS + s + 1 - RING_A)
                for i in range(G):
                    ex = nc.scalar.activation(da[:, s % RING_A, i, :], delta[:, p, m, :], ACT.Exp,
                                              scale=sh.a_neg[:, m, g * G + i:g * G + i + 1])
                ex.then_inc(S["da_ready"], 1)

            def take_y(c, p, m):
                act.wait_ge(S["summed"], (c + 1) * STEPS - MD + m + 1)
                if m == 0:
                    act.wait_ge(S["dbx_ready"], (c + 1) * STEPS)
                nc.scalar.copy(u[:, p, m, :], y_ps[m][:]).then_inc(S["y_taken"], 1)

            def body(c, b, th, first, last):
                for s in range(STEPS):
                    decays(c, th, s, first)
                    if not first and ACT_Y <= s < ACT_Y + MD:
                        take_y(c - 1, 1 - th, s - ACT_Y)
                    if s == ACT_SILU:
                        silu_z(c, th)
                        if not last:
                            silu_conv(c + 1, 1 - th)
                    if not last:
                        if s in ACT_MAIN:
                            copy_out(c + 1, 1 - th, ACT_MAIN.index(s))
                        if s == ACT_BC:
                            copy_bc(c + 1, False)
                        if s == ACT_SOFT:
                            softplus(c + 1, 1 - th, first)
                        if s in ACT_Z:
                            if s == ACT_Z[0] and not first:
                                act.wait_ge(S["y_gated"], c * MD)
                            copy_out(c + 1, 1 - th, MD + ACT_Z.index(s))

            for m in range(MD):
                copy_out(0, 0, m)
            silu_conv(0, 0)
            copy_bc(0, True)
            softplus(0, 0, True)
            for m in range(MD, 2 * MD):
                copy_out(0, 0, m)
            chunks(act, body)
            for m in range(MD):
                take_y(B * CPB - 1, 1, m)

        @block.gpsimd
        def _(pool):
            def products(c, p, s, first):
                g, m = s // MD, s % MD
                if s == 0:
                    pool.wait_ge(S["u_ready"], c + 1)
                if m == 0:
                    pool.wait_ge(bc_loaded[g % RING_B], c * (32 * NG // RING_B) + 32 * (g // RING_B + 1))
                if not (first and s < RING):
                    pool.wait_ge(S["scanned"], c * STEPS + s + 1 - RING)
                nc.gpsimd.tensor_tensor(dbx[:, s % RING], u[:, p, m:m + 1, :].broadcast_to([P, G, CH]), b_all[:, g % RING_B],
                                        ALU.mult).then_inc(S["dbx_ready"], 1)

            def multiply_u(c, p):
                pool.wait_ge(S["delta_ready"], c + 1)
                nc.gpsimd.tensor_tensor(u[:, p], delta[:, p], x_conv[:, p], ALU.mult).then_inc(S["u_ready"], 1)

            def gate_y(c, p, m):
                pool.wait_ge(S["y_taken"], c * MD + m + 1)
                if m == 0:
                    pool.wait_ge(S["z_act"], c + 1)
                nc.gpsimd.tensor_tensor(u[:, p, m, :], u[:, p, m, :], gate[:, p, m, :], ALU.mult).then_inc(S["y_gated"], 1)

            def body(c, b, th, first, last):
                for s in range(STEPS):
                    products(c, th, s, first)
                    if not first and POOL_GATE <= s < POOL_GATE + MD:
                        gate_y(c - 1, 1 - th, s - POOL_GATE)
                    if not last and s == POOL_U:
                        multiply_u(c + 1, 1 - th)

            multiply_u(0, 0)
            chunks(pool, body)
            for m in range(MD):
                gate_y(B * CPB - 1, 1, m)

        @block.vector
        def _(dve):
            def convolve(c, p, m, fresh):
                dve.wait_ge(S["proj_copied"], c * 8 + m + 1)
                if not fresh:
                    dve.wait_ge(S["tail_kept"], (c - 1) * MD + m + 1)
                acc, xm = delta[:, p, m, :], x_main[:, m % 2, :]
                if fresh:
                    nc.vector.memset(xm[:, 0:DC - 1], 0.0).then_inc(S["head_set"], 1)
                else:
                    nc.vector.tensor_copy(xm[:, 0:DC - 1], tail[:, m, :]).then_inc(S["head_set"], 1)
                dve.wait_ge(S["head_set"], c * MD + m + 1)
                for j in range(DC - 1):
                    if j:
                        dve.wait_ge(S["conv_chain"], (c * MD + m) * (DC - 2) + j)
                    ins = nc.vector.scalar_tensor_tensor(out=acc, in0=xm[:, j:j + CH], scalar=sh.conv_w[:, m, j:j + 1],
                                                         in1=acc, op0=ALU.mult, op1=ALU.add)
                    ins.then_inc(S["conv_chain"] if j < DC - 2 else S["conv_done"], 1)
                nc.vector.tensor_copy(tail[:, m, :], xm[:, CH:]).then_inc(S["tail_kept"], 1)

            def finish_delta(c, p):
                dve.wait_ge(S["soft_ready"], c + 1)
                nc.vector.tensor_tensor(delta[:, p], delta[:, p], u[:, p], ALU.add).then_inc(S["delta_ready"], 1)

            def scans(c, b, th, s):
                g, m = s // MD, s % MD
                dve.wait_ge(S["da_ready"], c * STEPS + s + 1)
                dve.wait_ge(S["dbx_ready"], c * STEPS + s + 1)
                if th == 1:
                    dve.wait_ge(S["states_kept"], b * STEPS + s + 1)
                for i in range(G):
                    h = da[:, s % RING_A, i, :]
                    ins = nc.vector.tensor_tensor_scan(h, h, dbx[:, s % RING, i, :], 0.0 if th == 0 else state[:, s, i:i + 1],
                                                       ALU.mult, ALU.add)
                ins.then_inc(S["scanned"], 1)

            def keep_states(c, s):
                dve.wait_ge(S["scanned"], c * STEPS + s + 1)
                nc.vector.tensor_copy(state[:, s, :], da[:, s % RING_A, :, CH - 1]).then_inc(S["states_kept"], 1)

            def outputs(c, b, th, s):
                g, m = s // MD, s % MD
                if th == 0:
                    dve.wait_ge(S["states_kept"], b * STEPS + s + 1)
                else:
                    dve.wait_ge(S["scanned"], c * STEPS + s + 1)
                if m == 0:
                    dve.wait_ge(bc_loaded[g % RING_B], c * (32 * NG // RING_B) + 32 * (g // RING_B + 1))
                nc.vector.tensor_tensor(da[:, s % RING_A], da[:, s % RING_A], c_all[:, g % RING_B], ALU.mult).then_inc(S["hc_ready"], 1)

            def add_out(c, b, th, j):
                tile = c * CT + j
                dve.wait_ge(S["out_done"], c * CT + j + 1)
                nc.vector.tensor_tensor(gated[:], out_ps[j % 2][:], sh.mods[:, 2, b, :], ALU.mult).then_inc(S["out_added"], 1)
                dve.wait_ge(S["out_added"], c * CT + j + 1)
                nc.vector.tensor_tensor(sh.x[:, tile, :], sh.x[:, tile, :], gated[:], ALU.add).then_inc(S["out_chain"], 1)
                dve.wait_ge(S["out_chain"], c * CT + j + 1)
                nc.vector.bn_stats(sh.stats[:, tile, :], sh.x[:, tile, :])

            def body(c, b, th, first, last):
                for s in range(STEPS):
                    scans(c, b, th, s)
                    if s:
                        outputs(c, b, th, s - 1)
                    if th == 0:
                        keep_states(c, s)
                    if not last:
                        if s in DVE_CONV:
                            convolve(c + 1, 1 - th, DVE_CONV.index(s), th == CPB - 1)
                        if s == DVE_DELTA:
                            finish_delta(c + 1, 1 - th)
                    if not first:
                        if DVE_OUT <= s < DVE_OUT + CT:
                            add_out(c - 1, b if th == 1 else b - 1, 1 - th, s - DVE_OUT)
                outputs(c, b, th, STEPS - 1)

            for m in range(MD):
                nc.vector.tensor_scalar(d_diag[:, m, :], sh.ident[:], sh.vecs[:, 3, m:m + 1], None, ALU.mult).then_inc(S["diag_set"], 1)
            for m in range(MD):
                convolve(0, 0, m, True)
            finish_delta(0, 0)
            chunks(dve, body)
            for j in range(CT):
                add_out(B * CPB - 1, B - 1, 1, j)


def phase_route(nc, d, sh):
    NE = EXPERTS0
    RT = 4
    with ExitStack() as ctx:
        sb = lambda name, shape, dt=F32: ctx.enter_context(nc.sbuf_tensor(f"rt_{name}", shape, dt))
        ps = lambda name, shape: ctx.enter_context(nc.psum_tensor(f"rt_{name}", shape, F32))
        sem = ctx.enter_context(Semaphores(nc, "rt_"))
        gate_w = sb("gate_w", [P, KE, NE])
        half = sb("half", [P, 4, E])
        row8 = sb("row8", [P, TPB, E])
        h_rows = sb("h_rows", [P, TILES, E])
        h_tr = sb("h_tr", [P, RT, KE, P])
        logits = sb("logits", [P, TILES, NE])
        scores = sb("scores", [P, TILES, NE])
        cand = sb("cand", [P, TILES, NE])
        rank = sb("rank", [P, TILES, NE])
        mask = sb("mask", [P, 2, TILES, NE])
        both = sb("both", [P, TILES, NE])
        iota_e = sb("iota_e", [P, TILES, NE])
        top = sb("top", [P, 2, TILES])
        idx = sb("idx", [P, TILES])
        tri = sb("tri", [P, P])
        ones = sb("ones", [P, P])
        run_on = sb("run_on", [P, NE, TILES])
        total = sb("total", [P, NE, TILES])
        before = sb("before", [P, NE, TILES])
        count = sb("count", [P, NE])
        count_i = sb("count_i", [P, NE], I32)
        padded = sb("padded", [P, NE])
        ends = sb("ends", [P, NE])
        offs = sb("offs", [P, NE])
        slot = sb("slot", [P, 2, TILES])
        wsum = sb("wsum", [P, TILES])
        tiles_at = sb("tiles_at", [P, TILES0])
        owner = sb("owner", [P, TILES0])
        turned = [ps(f"turned{i}", [P, KE, P]) for i in range(RT)]
        logit_ps = ps("logit_ps", [P, TPB, NE])
        tri_ps, tot_ps = ps("tri_ps", [P, TILES, NE]), ps("tot_ps", [P, TILES, NE])
        (mods_in, gate_in, var_ready, std_ready, chain, half_ready, row_ready, row_turned, turn_copied, logits_done,
         logits_copied, consts_ready, score_ready, masks_ready, ranked, gap_ready, exp_ready, slots_ready, scattered, pool_chain) = (
            sem(n) for n in ("mods_in gate_in var_ready std_ready chain half_ready row_ready row_turned turn_copied logits_done "
                             "logits_copied consts_ready score_ready masks_ready ranked gap_ready exp_ready "
                             "slots_ready scattered pool_chain").split())
        rows_copied = [sem(f"rows_copied{th}") for th in range(CPB)]
        block = ctx.enter_context(nc.Block())

        @block.sync
        def _(sp):
            load_mods(sp, d, sh, 0, 1, mods_in)
            sp.dma_start(gate_w[:], d["L0_ffn_Wr"].rearrange("(k p) n -> p k n", p=P)).then_inc(gate_in, 16)
            with sp.Fori(0, B) as b:
                for th in range(CPB):
                    sp.wait_ge(row_ready, b * TPB + (th + 1) * CT + 4)
                    sp.dma_start(h_rows[:, bass.ds(b * TPB + th * CT, CT), :], row8[:, th * CT:(th + 1) * CT, :]).then_inc(rows_copied[th], 16)
            for e in range(EXPERTS0):
                for i, name in enumerate(("L0_ffn_W1", "L0_ffn_W3")):
                    sp.dma_start(sh.w13[:, e, i], d[name][e].rearrange("(k p) f -> p k f", p=P)).then_inc(sh.e0_w_in, 16)
                sp.dma_start(sh.w2_0[:, e], d["L0_ffn_W2"][e].rearrange("(m p) f -> p m f", p=P)).then_inc(sh.e0_w_in, 16)

        @block.gpsimd
        def _(pool):
            nc.gpsimd.memset(tri[:], 1.0).then_inc(pool_chain, 1)
            nc.gpsimd.memset(ones[:], 1.0).then_inc(pool_chain, 1)
            pool.wait_ge(pool_chain, 2)
            nc.gpsimd.affine_select(out=tri[:], in_=tri[:], compare_op=ALU.is_gt, fill=0.0, base=0, pattern=[[1, P]],
                                    channel_multiplier=-1).then_inc(consts_ready, 1)
            nc.gpsimd.iota(iota_e[:], pattern=[[0, TILES], [1, NE]], base=0, channel_multiplier=0,
                           allow_small_or_imprecise_dtypes=True).then_inc(consts_ready, 1)
            nc.gpsimd.memset(run_on[:], 1.0).then_inc(pool_chain, 1)
            pool.wait_ge(pool_chain, 3)
            nc.gpsimd.memset(run_on[:, :, 0:1], 0.0).then_inc(consts_ready, 1)
            nc.gpsimd.iota(tiles_at[:], pattern=[[P, TILES0]], base=0, channel_multiplier=0,
                           allow_small_or_imprecise_dtypes=True).then_inc(consts_ready, 1)
            pool.wait_ge(slots_ready, 1)
            for th in range(CPB):
                pool.wait_ge(rows_copied[th], 16 * B + 1)
            for i in range(TILES):
                for k in range(2):
                    nc.gpsimd.indirect_dma_start(out=d["slots0"], out_offset=bass.IndirectOffsetOnAxis(ap=sh.slot_of[:, k, i:i + 1], axis=0),
                                                 in_=h_rows[:, i, :], in_offset=None).then_inc(scattered, 16)
            pool.wait_ge(scattered, 2 * TILES * 16)

        @block.scalar
        def _(act):
            act.wait_ge(var_ready, 1)
            nc.scalar.activation(sh.var[:], sh.var[:], ACT.Sqrt).then_inc(std_ready, 1)
            with act.Fori(0, B) as b:
                for j in range(TPB):
                    act.wait_ge(row_turned, b * TPB + j + 1 + TPB)
                    act.wait_ge(logits_done, b * TPB + j + 1)
                    nc.scalar.copy(h_tr[:, j % RT], turned[j % RT][:]).then_inc(turn_copied, 1)
                act.wait_ge(logits_done, b * TPB + TPB + RT)
                nc.scalar.copy(logits[:, bass.ds(b * TPB, TPB), :], logit_ps[:]).then_inc(logits_copied, 1)
            act.wait_ge(logits_copied, B + 1)
            act.sem_inc(score_ready, 1)
            act.wait_ge(gap_ready, 1)
            nc.scalar.activation(sh.weight[:, 1], sh.weight[:, 1], ACT.Exp).then_inc(exp_ready, 1)

        @block.tensor
        def _(pe):
            pe.sem_inc(row_turned, TPB)
            pe.sem_inc(logits_done, RT)
            pe.sem_inc(turn_copied, RT)
            pe.sem_inc(row_ready, 4)
            pe.sem_inc(logits_copied, 1)
            for th in range(CPB):
                pe.sem_inc(rows_copied[th], 1)
            pe.wait_ge(gate_in, 16)

            with pe.Fori(0, B) as b:
                def turn(j):
                    pe.wait_ge(row_ready, b * TPB + j + 5)
                    pe.wait_ge(turn_copied, b * TPB + j + 1)
                    for k in range(KE):
                        last = nc.tensor.transpose(turned[j % RT][:, k, :], row8[:, j, k * P:(k + 1) * P], sh.ident[:])
                    last.then_inc(row_turned, 1)

                def product(j):
                    pe.wait_ge(turn_copied, b * TPB + j + RT + 1)
                    if j == 0:
                        pe.wait_ge(logits_copied, b + 1)
                    for k in range(KE):
                        last = nc.tensor.matmul(logit_ps[:, j, :], h_tr[:, j % RT, k, :], gate_w[:, k, :],
                                                start=(k == 0), stop=(k == KE - 1))
                    last.then_inc(logits_done, 1)

                for j in range(TPB + 2):
                    if j < TPB:
                        turn(j)
                    if j >= 2:
                        product(j - 2)
            pe.wait_ge(masks_ready, 1)
            pe.wait_ge(consts_ready, 1)
            nc.tensor.matmul(tri_ps[:], tri[:], both[:], start=True, stop=True).then_inc(ranked, 1)
            nc.tensor.matmul(tot_ps[:], ones[:], both[:], start=True, stop=True).then_inc(ranked, 1)

        @block.vector
        def _(dve):
            link = link_on(dve, chain)
            finish_stats(nc, dve, link, sh, var_ready, std_ready)
            dve.wait_ge(mods_in, 16)

            def row_free(b, j):
                dve.wait_ge(row_turned, b * TPB + j + 1)
                if j % CT == 0:
                    dve.wait_ge(rows_copied[j // CT], b * 16 + 1)

            norm_rows(nc, dve, sh, half, row8, half_ready, row_ready, row_free)

            over = lambda a: a.rearrange("p (t o) -> p t o", o=1).broadcast_to([P, TILES, NE])
            dve.wait_ge(score_ready, 1)
            dve.wait_ge(consts_ready, 4)
            values = logits
            for k in range(2):
                link(nc.vector.tensor_reduce(top[:, k], values[:], AX_X, ALU.max))
                link(nc.vector.tensor_tensor(cand[:], values[:], over(top[:, k]), ALU.is_lt))
                link(nc.vector.scalar_tensor_tensor(out=cand[:], in0=cand[:], scalar=float(NE), in1=iota_e[:], op0=ALU.mult, op1=ALU.add))
                link(nc.vector.tensor_reduce(idx[:], cand[:], AX_X, ALU.min))
                link(nc.vector.tensor_tensor(mask[:, k], iota_e[:], over(idx[:]), ALU.is_equal))
                if k == 0:
                    link(nc.vector.scalar_tensor_tensor(out=scores[:], in0=mask[:, 0], scalar=-3e38, in1=values[:], op0=ALU.mult, op1=ALU.add))
                    values = scores
            nc.vector.tensor_tensor(both[:], mask[:, 0], mask[:, 1], ALU.add).then_inc(masks_ready, 1)
            nc.vector.tensor_tensor(sh.weight[:, 1], top[:, 1], top[:, 0], ALU.subtract).then_inc(gap_ready, 1)
            dve.wait_ge(ranked, 2)
            link(nc.vector.tensor_copy(total[:], tot_ps[:].rearrange("p t e -> p e t")))
            flat = lambda a: a.rearrange("p e t -> p (e t)")
            link(nc.vector.tensor_tensor_scan(flat(before[:]), flat(run_on[:]), flat(total[:]), 0.0, ALU.mult, ALU.add))
            link(nc.vector.tensor_copy(count[:], before[:, :, TILES - 1]))
            link(nc.vector.tensor_tensor(before[:], before[:], total[:], ALU.subtract))
            link(nc.vector.tensor_tensor(rank[:], tri_ps[:], before[:].rearrange("p e t -> p t e"), ALU.add))
            link(nc.vector.tensor_scalar(count_i[:], count[:], float(P - 1), None, ALU.add))
            link(nc.vector.tensor_scalar(count_i[:], count_i[:], 7, 7, ALU.arith_shift_right, ALU.logical_shift_left))
            link(nc.vector.tensor_copy(padded[:], count_i[:]))
            link(nc.vector.tensor_tensor_scan(ends[:], ones[:, 0:NE], padded[:], 0.0, ALU.mult, ALU.add))
            link(nc.vector.tensor_tensor(offs[:], ends[:], padded[:], ALU.subtract))
            link(nc.vector.tensor_scalar(owner[:], tiles_at[:], ends[:, 0:1], None, ALU.is_ge))
            for e in range(1, NE - 1):
                link(nc.vector.scalar_tensor_tensor(out=owner[:], in0=tiles_at[:], scalar=ends[:, e:e + 1], in1=owner[:],
                                                    op0=ALU.is_ge, op1=ALU.add))
            link(nc.vector.tensor_copy(sh.owner_i[:], owner[:]))
            link(nc.vector.tensor_tensor(cand[:], rank[:], offs[:].rearrange("p (o e) -> p o e", o=1).broadcast_to([P, TILES, NE]), ALU.add))
            for k in range(2):
                link(nc.vector.tensor_tensor(scores[:], mask[:, k], cand[:], ALU.mult))
                link(nc.vector.tensor_reduce(slot[:, k], scores[:], AX_X, ALU.add))
            nc.vector.tensor_copy(sh.slot_of[:], slot[:]).then_inc(slots_ready, 1)
            dve.wait_ge(exp_ready, 1)
            link(nc.vector.tensor_scalar(wsum[:], sh.weight[:, 1], 1.0, None, ALU.add))
            link(nc.vector.reciprocal(sh.weight[:, 0], wsum[:]))
            link(nc.vector.tensor_tensor(sh.weight[:, 1], sh.weight[:, 1], sh.weight[:, 0], ALU.mult))


def phase_experts0(nc, d, sh):
    U = 4
    with ExitStack() as ctx:
        sb = lambda name, shape: ctx.enter_context(nc.sbuf_tensor(f"e0_{name}", shape, F32))
        ps = lambda name, shape: ctx.enter_context(nc.psum_tensor(f"e0_{name}", shape, F32))
        sem = ctx.enter_context(Semaphores(nc, "e0_"))
        w13, w2 = sh.w13, sh.w2_0
        xs = sb("xs", [P, U, E])
        xt = sb("xt", [P, 2, KE, P])
        act_h = sb("act_h", [P, 2, H0])
        prod = sb("prod", [P, 2, H0])
        pt = sb("pt", [P, 2, MH0, P])
        ys = sb("ys", [P, U, E])
        x_ps = ps("x_ps", [P, KE, P])
        h_ps = [ps(f"h_ps{i}", [P, H0]) for i in range(2)]
        g_ps = [ps(f"g_ps{i}", [P, H0]) for i in range(2)]
        p_ps = ps("p_ps", [P, MH0, P])
        y_ps = ps("y_ps", [P, E])
        x_in, y_out = [sem(f"x_in{i}") for i in range(U)], [sem(f"y_out{i}") for i in range(U)]
        x_turned, x_copied, h_done, silu_done, prod_done, p_turned, p_copied, y_done, y_copied = (
            sem(n) for n in "x_turned x_copied h_done silu_done prod_done p_turned p_copied y_done y_copied".split())
        block = ctx.enter_context(nc.Block())
        LOOPS = TILES0 // U
        assert TILES0 % U == 0

        def tiles(eng, body):
            for r in range(U):
                body(r, r, 0)
            with eng.Fori(1, LOOPS - 1) as q:
                for r in range(U):
                    body(q * U + r, r, q)
            for r in range(U):
                body(TILES0 - U + r, r, LOOPS - 1)

        exists = lambda j: not isinstance(j, int) or 0 <= j < TILES0
        early = lambda j, n: isinstance(j, int) and j < n

        @block.sync
        def _(sp):
            sp.dma_start(sh.w_qkv[:], d["wqkvT"].rearrange("(k p) (h c f) -> p k h c f", p=P, h=HEADS, c=3)).then_inc(sh.att_w_in, 16)

            def load(j, r):
                if not early(j, U):
                    sp.wait_ge(x_turned, j - U + 1)
                sp.dma_start(xs[:, r], d["slots0"][bass.ds(j * P, P), :]).then_inc(x_in[r], 16)

            def store(j, r):
                sp.wait_ge(y_copied, j + 1)
                sp.dma_start(d["outs0"][bass.ds(j * P, P), :], ys[:, r]).then_inc(y_out[r], 16)

            def body(j, r, q):
                if exists(j + 2):
                    load(j + 2, (r + 2) % U)
                if exists(j - 2):
                    store(j - 2, (r - 2) % U)

            load(0, 0)
            load(1, 1)
            tiles(sp, body)
            store(TILES0 - 2, U - 2)
            store(TILES0 - 1, U - 1)
            for r in range(U):
                sp.wait_ge(y_out[r], 16 * LOOPS + 1)

        @block.tensor
        def _(pe):
            def turn_x(j, r, q):
                pe.wait_ge(x_in[r], q * 16 + 16)
                if not early(j, 1):
                    pe.wait_ge(x_copied, j)
                for k in range(KE):
                    last = nc.tensor.transpose(x_ps[:, k, :], xs[:, r, k * P:(k + 1) * P], sh.ident[:])
                last.then_inc(x_turned, 1)

            def hidden(j, r):
                e = nc.tensor.value_load(sh.owner_i[0:1, bass.ds(j, 1)], min_val=0, max_val=EXPERTS0 - 1)
                pe.wait_ge(x_copied, j + 1)
                if not early(j, 2):
                    pe.wait_ge(prod_done, j - 1)
                for i, out_ps in ((0, h_ps), (1, g_ps)):
                    for k in range(KE):
                        last = nc.tensor.matmul(out_ps[r % 2][:], xt[:, r % 2, k, :], w13[:, e, i, k, :],
                                                start=(k == 0), stop=(k == KE - 1))
                last.then_inc(h_done, 1)

            def turn_p(j, r):
                pe.wait_ge(prod_done, j + 1)
                if not early(j, 1):
                    pe.wait_ge(p_copied, j)
                for m in range(MH0):
                    last = nc.tensor.transpose(p_ps[:, m, :], prod[:, r % 2, m * P:(m + 1) * P], sh.ident[:])
                last.then_inc(p_turned, 1)

            def output(j, r):
                e = nc.tensor.value_load(sh.owner_i[0:1, bass.ds(j, 1)], min_val=0, max_val=EXPERTS0 - 1)
                pe.wait_ge(p_copied, j + 1)
                if not early(j, 1):
                    pe.wait_ge(y_copied, j)
                for m in range(MH0):
                    last = nc.tensor.matmul(y_ps[:], pt[:, r % 2, m, :], w2[:, e, m, :], start=(m == 0), stop=(m == MH0 - 1))
                last.then_inc(y_done, 1)

            def body(j, r, q):
                hidden(j, r)
                if exists(j - 1):
                    turn_p(j - 1, (r - 1) % U)
                if exists(j + 1):
                    turn_x(j + 1, (r + 1) % U, q + (r + 1) // U)
                if exists(j - 2):
                    output(j - 2, (r - 2) % U)

            pe.wait_ge(sh.e0_w_in, 48 * EXPERTS0)
            turn_x(0, 0, 0)
            tiles(pe, body)
            turn_p(TILES0 - 1, U - 1)
            output(TILES0 - 2, U - 2)
            output(TILES0 - 1, U - 1)

        @block.scalar
        def _(act):
            def copy_x(j, r):
                act.wait_ge(x_turned, j + 1)
                if not early(j, 2):
                    act.wait_ge(h_done, j - 1)
                nc.scalar.copy(xt[:, r % 2], x_ps[:]).then_inc(x_copied, 1)

            def silu(j, r):
                act.wait_ge(h_done, j + 1)
                if not early(j, 2):
                    act.wait_ge(prod_done, j - 1)
                nc.scalar.activation(act_h[:, r % 2], h_ps[r % 2][:], ACT.Silu).then_inc(silu_done, 1)

            def copy_y(j, r, q):
                act.wait_ge(y_done, j + 1)
                if not early(j, U):
                    act.wait_ge(y_out[r], q * 16 + 1)
                nc.scalar.copy(ys[:, r], y_ps[:]).then_inc(y_copied, 1)

            def body(j, r, q):
                silu(j, r)
                if exists(j + 1):
                    copy_x(j + 1, (r + 1) % U)
                if exists(j - 2):
                    copy_y(j - 2, (r - 2) % U, q - (1 if r < 2 else 0))

            for r in range(U):
                act.sem_inc(y_out[r], 1)
            copy_x(0, 0)
            tiles(act, body)
            copy_y(TILES0 - 2, U - 2, LOOPS - 1)
            copy_y(TILES0 - 1, U - 1, LOOPS - 1)

        @block.vector
        def _(dve):
            def copy_p(j, r):
                dve.wait_ge(p_turned, j + 1)
                if not early(j, 2):
                    dve.wait_ge(y_done, j - 1)
                nc.vector.tensor_copy(pt[:, r % 2], p_ps[:]).then_inc(p_copied, 1)

            def multiply(j, r):
                dve.wait_ge(silu_done, j + 1)
                if not early(j, 2):
                    dve.wait_ge(p_turned, j - 1)
                nc.vector.tensor_tensor(prod[:, r % 2], act_h[:, r % 2], g_ps[r % 2][:], ALU.mult).then_inc(prod_done, 1)

            def body(j, r, q):
                if exists(j - 1):
                    copy_p(j - 1, (r - 1) % U)
                multiply(j, r)

            tiles(dve, body)
            copy_p(TILES0 - 1, U - 1)


def phase_experts1(nc, d, sh):
    S1 = CAP1 // P
    HALF = CAP1 // 2
    with ExitStack() as ctx:
        sb = lambda name, shape: ctx.enter_context(nc.sbuf_tensor(f"e1_{name}", shape, F32))
        ps = lambda name, shape: ctx.enter_context(nc.psum_tensor(f"e1_{name}", shape, F32))
        sem = ctx.enter_context(Semaphores(nc, "e1_"))
        w1 = sb("w1", [P, 2, KE, F1])
        w2 = sb("w2", [P, 2, MF1, E])
        xs = sb("xs", [P, 2, S1, E])
        xt = sb("xt", [P, KE, CAP1])
        hid = sb("hid", [P, MF1, CAP1])
        ys = sb("ys", [P, 2, S1, E])
        x_ps = [ps(f"x_ps{i}", [P, KE, P]) for i in range(2)]
        h_ps = [ps(f"h_ps{i}", [P, HALF]) for i in range(4)]
        y_ps = [ps(f"y_ps{i}", [P, E]) for i in range(2)]
        w1_in, w2_in, x_in, y_out = ([sem(f"{n}{i}") for i in range(2)] for n in ("w1_in", "w2_in", "x_in", "y_out"))
        mods_in = sem("mods_in")
        x_turned, x_copied, h_done, h_act, y_done, y_copied = (sem(n) for n in "x_turned x_copied h_done h_act y_done y_copied".split())
        block = ctx.enter_context(nc.Block())
        NH = 2 * MF1

        def experts(eng, body):
            for r in range(2):
                body(r, r, 0)
            with eng.Fori(1, EXPERTS1 // 2 - 1) as q:
                for r in range(2):
                    body(q * 2 + r, r, q)
            for r in range(2):
                body(EXPERTS1 - 2 + r, r, EXPERTS1 // 2 - 1)

        exists = lambda e: not isinstance(e, int) or e < EXPERTS1
        early = lambda e, n: isinstance(e, int) and e < n

        @block.sync
        def _(sp):
            load_mods(sp, d, sh, 1, 1, mods_in)

            def load(e, r, q):
                if not early(e, 2):
                    sp.wait_ge(x_turned, (e - 1) * S1)
                sp.dma_start(xs[:, r], d["slots1"][bass.ds(e * CAP1, CAP1), :].rearrange("(t p) f -> p t f", p=P)).then_inc(x_in[r], 16)
                if not early(e, 2):
                    sp.wait_ge(y_done, (e - 1) * S1)
                one = bass.ds(e, 1)
                sp.dma_start(w1[:, r], d["L1_ffn_w1"][one].rearrange("o (k p) f -> p (o k) f", p=P)).then_inc(w1_in[r], 16)
                sp.dma_start(w2[:, r], d["L1_ffn_w2"][one].rearrange("o (m p) f -> p (o m) f", p=P)).then_inc(w2_in[r], 16)

            def body(e, r, q):
                sp.wait_ge(y_copied, (e + 1) * S1)
                sp.dma_start(d["outs1"][bass.ds(e * CAP1, CAP1), :].rearrange("(t p) f -> p t f", p=P), ys[:, r]).then_inc(y_out[r], 16)
                if exists(e + 2):
                    load(e + 2, r, q + 1)

            load(0, 0, 0)
            load(1, 1, 0)
            experts(sp, body)
            for r in range(2):
                sp.wait_ge(y_out[r], 16 * (EXPERTS1 // 2))
            sp.wait_ge(mods_in, 16)

        @block.tensor
        def _(pe):
            def turn_x(e, r, q, t):
                if t == 0:
                    pe.wait_ge(x_in[r], q * 16 + 16)
                if not early(e, 1) or t >= 2:
                    pe.wait_ge(x_copied, e * S1 + t - 1)
                for k in range(KE):
                    last = nc.tensor.transpose(x_ps[(r + t) % 2][:, k, :], xs[:, r, t, k * P:(k + 1) * P], sh.ident[:])
                last.then_inc(x_turned, 1)

            def hidden(e, r, q):
                pe.wait_ge(x_copied, (e + 1) * S1)
                pe.wait_ge(w1_in[r], q * 16 + 16)
                for n in range(NH):
                    m, part = n // 2, n % 2
                    if not early(e, 1) or n >= 4:
                        pe.wait_ge(h_act, e * NH + n - 3)
                    for k in range(KE):
                        last = nc.tensor.matmul(h_ps[n % 4][:], w1[:, r, k, m * P:(m + 1) * P],
                                                xt[:, k, part * HALF:(part + 1) * HALF], start=(k == 0), stop=(k == KE - 1))
                    last.then_inc(h_done, 1)

            def output(e, r, q, t):
                if t == 0:
                    pe.wait_ge(h_act, (e + 1) * NH)
                    pe.wait_ge(w2_in[r], q * 16 + 16)
                if not early(e, 1) or t >= 2:
                    pe.wait_ge(y_copied, e * S1 + t - 1)
                for m in range(MF1):
                    last = nc.tensor.matmul(y_ps[(r + t) % 2][:], hid[:, m, t * P:(t + 1) * P], w2[:, r, m, :],
                                            start=(m == 0), stop=(m == MF1 - 1))
                last.then_inc(y_done, 1)

            def body(e, r, q):
                hidden(e, r, q)
                for t in range(S1):
                    if exists(e + 1):
                        turn_x(e + 1, 1 - r, q + r, t)
                    output(e, r, q, t)

            for t in range(S1):
                turn_x(0, 0, 0, t)
            experts(pe, body)

        @block.scalar
        def _(act):
            def body(e, r, q):
                for n in range(NH):
                    m, part = n // 2, n % 2
                    act.wait_ge(h_done, e * NH + n + 1)
                    if n == 0 and not early(e, 1):
                        act.wait_ge(y_done, e * S1)
                    nc.scalar.activation(hid[:, m, part * HALF:(part + 1) * HALF], h_ps[n % 4][:], ACT.Gelu).then_inc(h_act, 1)

            experts(act, body)

        @block.vector
        def _(dve):
            def copy_x(e, r, t):
                dve.wait_ge(x_turned, e * S1 + t + 1)
                if t == 0 and not early(e, 1):
                    dve.wait_ge(h_done, e * NH)
                nc.vector.tensor_copy(xt[:, :, t * P:(t + 1) * P], x_ps[(r + t) % 2][:]).then_inc(x_copied, 1)

            def body(e, r, q):
                for t in range(S1):
                    if exists(e + 1):
                        copy_x(e + 1, 1 - r, t)
                    dve.wait_ge(y_done, e * S1 + t + 1)
                    if t == 0 and not early(e, 2):
                        dve.wait_ge(y_out[r], q * 16)
                    nc.vector.tensor_copy(ys[:, r, t, :], y_ps[(r + t) % 2][:]).then_inc(y_copied, 1)

            for t in range(S1):
                copy_x(0, 0, t)
            experts(dve, body)


def phase_combine(nc, d, sh):
    R = 4
    with ExitStack() as ctx:
        sb = lambda name, shape: ctx.enter_context(nc.sbuf_tensor(f"cb_{name}", shape, F32))
        sem = ctx.enter_context(Semaphores(nc, "cb_"))
        y = sb("y", [P, R, 2, E])
        tmp = sb("tmp", [P, 2, E])
        gathered = [sem(f"gathered{r}") for r in range(R)]
        x_ready, chain = sem("x_ready"), sem("chain")
        out_stored = sem("out_stored")
        block = ctx.enter_context(nc.Block())

        @block.gpsimd
        def _(pool):
            for i in range(TILES):
                if i >= R:
                    pool.wait_ge(x_ready, i - R + 1)
                for k in range(2):
                    nc.gpsimd.indirect_dma_start(out=y[:, i % R, k, :], out_offset=None, in_=d["outs1"],
                                                 in_offset=bass.IndirectOffsetOnAxis(ap=sh.slot_of[:, k, i:i + 1], axis=0)
                                                 ).then_inc(gathered[i % R], 16)

        @block.vector
        def _(dve):
            with dve.Fori(0, B) as b:
                for j in range(TPB):
                    tile, r, t = b * TPB + j, j % R, tmp[:, j % 2, :]
                    dve.wait_ge(gathered[r], b * (32 * TPB // R) + 32 * (j // R + 1))
                    nc.vector.tensor_scalar(t, y[:, r, 0, :], sh.weight[:, 0, bass.ds(tile, 1)], None, ALU.mult).then_inc(chain, 1)
                    dve.wait_ge(chain, tile * 3 + 1)
                    nc.vector.scalar_tensor_tensor(out=t, in0=y[:, r, 1, :], scalar=sh.weight[:, 1, bass.ds(tile, 1)], in1=t,
                                                   op0=ALU.mult, op1=ALU.add).then_inc(chain, 1)
                    dve.wait_ge(chain, tile * 3 + 2)
                    nc.vector.tensor_tensor(t, t, sh.mods[:, 2, b, :], ALU.mult).then_inc(chain, 1)
                    dve.wait_ge(chain, tile * 3 + 3)
                    nc.vector.tensor_tensor(sh.x[:, tile, :], sh.x[:, tile, :], t, ALU.add).then_inc(x_ready, 1)

        @block.sync
        def _(sp):
            out = token_tiles(d["out"])
            parts = TILES // CT
            for i in range(parts):
                sp.wait_ge(x_ready, (i + 1) * CT)
                sp.dma_start(out[:, i * CT:(i + 1) * CT], sh.x[:, i * CT:(i + 1) * CT]).then_inc(out_stored, 16)
            sp.wait_ge(out_stored, 16 * parts)


def phase_attention(nc, d, sh):
    R = 2
    SCALE = float(1.0 / np.sqrt(np.float32(DH)))
    N = HEADS * TPB
    PROJECT = (1, 2, 3, 5, 6, 7)
    PAIRS, NE = TPB // 2, EXPERTS1
    PIECES = 3 * CPB
    with ExitStack() as ctx:
        sb = lambda name, shape: ctx.enter_context(nc.sbuf_tensor(f"at_{name}", shape, F32))
        ps = lambda name, shape: ctx.enter_context(nc.psum_tensor(f"at_{name}", shape, F32))
        sem = ctx.enter_context(Semaphores(nc, "at_"))
        w_qkv = sh.w_qkv
        w_o = sb("w_o", [P, HEADS, E])
        pos = sb("pos", [P, T])
        gate0 = sb("gate0", [P, B, E])
        y = sb("y", [P, R, 2, E])
        tmp = sb("tmp", [P, 2, E])
        rows = sb("rows", [P, 4, E])
        hidden_pos = sb("later", [P, P])
        h_b = sb("h_b", [P, CPB, KE, CH])
        v = sb("v", [P, 2, TPB, DH])
        qk = sb("qk", [P, 2, 2, T])
        probs = sb("probs", [P, 3, T])
        pt = sb("pt", [P, 2, TPB, P])
        attn = sb("attn", [P, HEADS, T])
        small = sb("small", [P, 4, 4])
        gated = sb("gated", [P, 2, E])
        r_turned = gated[:].rearrange("p j (k t) -> p j k t", k=KE)
        s_ps = [ps(f"s_ps{i}", [P, T]) for i in range(2)]
        pt_ps = [ps(f"pt_ps{i}", [P, CT, P]) for i in range(2)]
        o_ps = ps("o_ps", [P, P])
        qk_ps = ps("qk_ps", [P, CH])
        mods2 = sb("mods2", [P, 2, B, E])
        r_rows = sb("r_rows", [P, TPB, E])
        gate_w = sb("gate_w", [P, KE, NE])
        tri, ones = sb("tri", [P, P]), sb("ones", [P, P])
        chances, cand, rank, both, iota_e, scores = (sb(n, [P, TPB, NE]) for n in "chances cand rank both iota_e scores".split())
        mask = sb("mask", [P, 2, TPB, NE])
        run_on, plus, before = (sb(n, [P, NE, TPB]) for n in "run_on plus before".split())
        so_far, offs, spare = sb("so_far", [P, NE]), sb("offs", [P, NE]), sb("spare", [P, 1])
        top, slot, valid = (sb(n, [P, 2, TPB]) for n in "top slot valid".split())
        idx, wsum = sb("idx", [P, TPB]), sb("wsum", [P, TPB])
        gathered = [sem(f"gathered{r}") for r in range(R)]
        names = ("route_in stats2_in stats2_chain var2_ready std2_ready rstd2_ready r_half_ready r_row_ready r_turned_done "
                 "r_turn_copied logits_done chances_ready pick_chain masks_ready ranked rank_taken consts_ready slots_ready scattered rows_left "
                 "mods_in pos_in w_o_in combine_chain combined stats_in stats_chain var_ready std_ready rstd_ready half_ready row_ready row_turned "
                 "h_copied later_set qk_done qk_ready scored masked max_taken bias_ready exp_done inverted "
                 "normed turned0 turned1 copied0 copied1 pv_done attn_ready out_done out_added chain").split()
        S = {n: sem(n) for n in names}
        block = ctx.enter_context(nc.Block())

        ADD = tuple(1 + 3 * j for j in range(TPB))
        VAR, ROOT, INVERT = ADD[-1] + 2, ADD[-1] + 4, ADD[-1] + 6
        R_NORM, R_PAIR = tuple(INVERT + 1 + 2 * j for j in range(TPB)), tuple(N // 2 + 4 * p for p in range(PAIRS))
        PICK, RANK = (R_PAIR[-1] + 2, R_PAIR[-1] + 4), N - 12
        SLOTS = (RANK + 1, RANK + 2, RANK + 3)
        NORM, TURN, COPY = N - 11, N - 8, N - 7

        def batches(eng, body):
            body(0, True, False)
            with eng.Fori(1, B - 1) as b:
                body(b, False, False)
            body(B - 1, False, True)

        @block.sync
        def _(sp):
            load_mods(sp, d, sh, 1, 0, S["mods_in"])
            sp.dma_start(gate0[:], d["mod_rows"][0, 5].partition_broadcast(P)).then_inc(S["mods_in"], 16)
            sp.dma_start(mods2[:], d["mod_rows"][1, 3:5].partition_broadcast(P)).then_inc(S["route_in"], 16)
            sp.dma_start(gate_w[:], d["gate_wT"].rearrange("(k p) n -> p k n", p=P)).then_inc(S["route_in"], 16)
            sp.dma_start(pos[:], d["posT"]).then_inc(S["pos_in"], 16)
            sp.dma_start(w_o[:], d["woT"].rearrange("(h p) e -> p h e", p=P)).then_inc(S["w_o_in"], 16)

        @block.gpsimd
        def _(pool):
            def fetch(i):
                if i >= R:
                    pool.wait_ge(S["combined"], i - R + 1)
                for k in range(2):
                    nc.gpsimd.indirect_dma_start(out=y[:, i % R, k, :], out_offset=None, in_=d["outs0"],
                                                 in_offset=bass.IndirectOffsetOnAxis(ap=sh.slot_of[:, k, i:i + 1], axis=0)
                                                 ).then_inc(gathered[i % R], 16)

            for i in range(TPB):
                fetch(i)
            nc.gpsimd.memset(hidden_pos[:], 0.0).then_inc(S["later_set"], 1)
            pool.wait_ge(S["later_set"], 1)
            nc.gpsimd.affine_select(out=hidden_pos[:], in_=hidden_pos[:], compare_op=ALU.is_ge, fill=-3e38, base=0,
                                    pattern=[[-1, P]], channel_multiplier=1).then_inc(S["later_set"], 1)
            consts = S["consts_ready"]
            nc.gpsimd.memset(tri[:], 1.0).then_inc(consts, 1)
            nc.gpsimd.memset(run_on[:], 1.0).then_inc(consts, 1)
            pool.wait_ge(consts, 2)
            nc.gpsimd.affine_select(out=tri[:], in_=tri[:], compare_op=ALU.is_gt, fill=0.0, base=0, pattern=[[1, P]],
                                    channel_multiplier=-1).then_inc(consts, 1)
            nc.gpsimd.memset(run_on[:, :, 0:1], 0.0).then_inc(consts, 1)
            nc.gpsimd.memset(ones[:], 1.0).then_inc(consts, 1)
            nc.gpsimd.memset(so_far[:], 0.0).then_inc(consts, 1)
            for dst, pattern, base, step in ((iota_e, [[0, TPB], [1, NE]], 0, 0), (offs, [[CAP1, NE]], 0, 0), (spare, [[0, 1]], NE * CAP1, 1)):
                nc.gpsimd.iota(dst[:], pattern=pattern, base=base, channel_multiplier=step,
                               allow_small_or_imprecise_dtypes=True).then_inc(consts, 1)

            def scatter(rb):
                pool.wait_ge(S["slots_ready"], rb + 1)
                for j in range(TPB):
                    i = rb * TPB + j
                    for k in range(2):
                        nc.gpsimd.indirect_dma_start(out=d["slots1"], out_offset=bass.IndirectOffsetOnAxis(ap=sh.slot_of[:, k, i:i + 1], axis=0),
                                                     in_=r_rows[:, j, :], in_offset=None).then_inc(S["scattered"], 16)

            for b in range(B):
                if b + 1 < B:
                    for j in range(TPB):
                        fetch((b + 1) * TPB + j)
                if b > 0:
                    scatter(b - 1)
                    pool.wait_ge(S["scattered"], b * 2 * TPB * 16)
                    pool.sem_inc(S["rows_left"], 1)
            scatter(B - 1)
            pool.wait_ge(S["scattered"], 2 * TILES * 16)

        def bank(n):
            return s_ps[n // 2 % 2][:, (n % 2) * CH:(n % 2 + 1) * CH]

        def piece_bank(h, i):
            return qk_ps[:] if h else bank(i)

        @block.tensor
        def _(pe):
            for name in ("qk_done", "qk_ready", "out_added", "pv_done", "attn_ready", "copied0", "copied1", "h_copied"):
                pe.sem_inc(S[name], 1)
            pe.sem_inc(S["row_turned"], 4)
            pe.wait_ge(sh.att_w_in, 16)
            pe.wait_ge(S["w_o_in"], 16)

            def turn_rows(nb, j):
                pe.wait_ge(S["row_ready"], nb * TPB + j + 1)
                pe.wait_ge(S["h_copied"], nb * TPB + j + 1)
                if j == 0:
                    pe.wait_ge(S["qk_ready"], nb * (HEADS * PIECES) + 1)
                for k in range(KE):
                    last = nc.tensor.transpose(qk_ps[:, k * P:(k + 1) * P], rows[:, j % 4, k * P:(k + 1) * P], sh.ident[:])
                last.then_inc(S["row_turned"], 1)

            def turn_pair(rb, pair):
                pe.wait_ge(S["r_row_ready"], rb * TPB + 2 * pair + 2)
                for j in range(2):
                    for k in range(KE):
                        last = nc.tensor.transpose(qk_ps[:, (j * KE + k) * P:(j * KE + k + 1) * P], r_rows[:, 2 * pair + j, k * P:(k + 1) * P],
                                                   sh.ident[:])
                last.then_inc(S["r_turned_done"], 1)

            def logits(rb, pair):
                pe.wait_ge(S["r_turn_copied"], rb * PAIRS + pair + 1)
                for j in range(2):
                    for k in range(KE):
                        last = nc.tensor.matmul(qk_ps[:, j * NE:(j + 1) * NE], r_turned[:, j, k, :], gate_w[:, k, :],
                                                start=(k == 0), stop=(k == KE - 1))
                last.then_inc(S["logits_done"], 1)

            def count_before(rb):
                pe.wait_ge(S["masks_ready"], rb + 1)
                nc.tensor.matmul(qk_ps[:, 0:TPB * NE], tri[:], both[:], start=True, stop=True)
                nc.tensor.matmul(qk_ps[:, TPB * NE:2 * TPB * NE], ones[:], both[:], start=True, stop=True).then_inc(S["ranked"], 1)

            pe.sem_inc(S["rows_left"], 1)
            pe.wait_ge(S["route_in"], 32)
            pe.wait_ge(S["consts_ready"], 9)
            for j in range(TPB):
                turn_rows(0, j)

            def batch(b, first_batch, last_batch):
                def project(h, i):
                    out = piece_bank(h, i)
                    """Piece i of head h: queries (0, 1) and keys (2, 3), turned, and values (4, 5) by tiles of tokens."""
                    if h > 0:
                        pe.wait_ge(S["qk_ready"], b * (HEADS * PIECES) + h * PIECES + i + 1)
                    elif i >= 4:
                        pe.wait_ge(S["qk_ready"], b * (HEADS * PIECES) + i - 2)
                    if i < 4:
                        for k in range(KE):
                            last = nc.tensor.matmul(out, w_qkv[:, k, h, i // 2, :], h_b[:, i % 2, k, :], start=(k == 0), stop=(k == KE - 1))
                    else:
                        for t in range(CT):
                            at = slice(t * P, (t + 1) * P)
                            for k in range(KE):
                                last = nc.tensor.matmul(out[:, at], h_b[:, i % 2, k, at], w_qkv[:, k, h, 2, :], start=(k == 0), stop=(k == KE - 1))
                    last.then_inc(S["qk_done"], 1)

                def score(n):
                    h, i = n // TPB, n % TPB
                    if i == 0:
                        pe.wait_ge(S["qk_ready"], b * (HEADS * PIECES) + h * PIECES + (4 if h else PIECES) + 1)
                    if n >= 2:
                        pe.wait_ge(S["exp_done"], b * N + n - 1)
                    for part in range(i // CT + 1):
                        end = min((i + 1) * P, (part + 1) * CH)
                        last = nc.tensor.matmul(s_ps[n % 2][:, part * CH:end], qk[:, h % 2, 0, i * P:(i + 1) * P],
                                                qk[:, h % 2, 1, part * CH:end], start=True, stop=True)
                    last.then_inc(S["scored"], 1)

                def turn(n):
                    i = n % TPB
                    pe.wait_ge(S["normed"], b * N + n + 1)
                    for half in range(i // CT + 1):
                        pe.wait_ge(S[f"copied{half}"], (b * N + n + 1) if half == 0 else (b * (N // 2) + n // TPB * CT + i - CT + 1))
                        for j in range(half * CT, min(i + 1, (half + 1) * CT)):
                            last = nc.tensor.transpose(pt_ps[half][:, j % CT, :], probs[:, n % 3, j * P:(j + 1) * P], sh.ident[:])
                        last.then_inc(S[f"turned{half}"], 1)

                def weigh(n):
                    h, i = n // TPB, n % TPB
                    pe.wait_ge(S["copied0"], b * N + n + 2)
                    if i >= CT:
                        pe.wait_ge(S["copied1"], b * (N // 2) + h * CT + i - CT + 2)
                    pe.wait_ge(S["attn_ready"], b * N + n + 1)
                    if i == 0:
                        pe.wait_ge(S["qk_ready"], b * (HEADS * PIECES) + (h + 1) * PIECES + 1)
                    for j in range(i + 1):
                        last = nc.tensor.matmul(o_ps[:], v[:, h % 2, j, :], pt[:, n % 2, j, :], start=(j == 0), stop=(j == i))
                    last.then_inc(S["pv_done"], 1)

                def output(t):
                    if t >= 4:
                        pe.wait_ge(S["out_added"], b * TPB + t - 2)
                    for h in range(HEADS):
                        last = nc.tensor.matmul(bank(t)[:, 0:E], attn[:, h, t * P:(t + 1) * P], w_o[:, h, :],
                                                start=(h == 0), stop=(h == HEADS - 1))
                    last.then_inc(S["out_done"], 1)

                pe.wait_ge(S["h_copied"], b * TPB + TPB + 1)
                pe.wait_ge(S["out_added"], b * TPB + 1)
                for i in range(PIECES):
                    project(0, i)
                for n in range(N + 3):
                    if n < N:
                        score(n)
                    if not first_batch and n - 1 in R_PAIR:
                        pe.wait_ge(S["chances_ready"], (b - 1) * PAIRS + R_PAIR.index(n - 1) + 1)
                    if not first_batch and n - 1 == RANK:
                        pe.wait_ge(S["rank_taken"], b)
                    if n < N and n % TPB in PROJECT and n // TPB + 1 < HEADS:
                        project(n // TPB + 1, PROJECT.index(n % TPB))
                    if 2 <= n < N + 2:
                        turn(n - 2)
                    if not first_batch and (n in R_PAIR or n == RANK):
                        pe.wait_ge(S["qk_ready"], b * (HEADS * PIECES) + (n // TPB + 1) * PIECES + (3 if n % TPB else 0) + 1)
                        if n == RANK:
                            count_before(b - 1)
                        else:
                            turn_pair(b - 1, R_PAIR.index(n))
                    if not last_batch and TURN <= n < TURN + TPB:
                        turn_rows(b + 1, n - TURN)
                    if n >= 3:
                        weigh(n - 3)
                    if not first_batch and n in R_PAIR:
                        logits(b - 1, R_PAIR.index(n))
                pe.wait_ge(S["attn_ready"], b * N + N + 1)
                for t in range(TPB):
                    output(t)

            batches(pe, batch)
            for pair in range(PAIRS):
                if pair:
                    pe.wait_ge(S["chances_ready"], (B - 1) * PAIRS + pair)
                turn_pair(B - 1, pair)
                logits(B - 1, pair)
            pe.wait_ge(S["chances_ready"], B * PAIRS)
            count_before(B - 1)

        @block.scalar
        def _(act):
            def root(nb, which=""):
                act.wait_ge(S[f"var{which}_ready"], nb + 1)
                of_batch = bass.ds(nb * TPB, TPB)
                nc.scalar.activation(sh.var[:, of_batch], sh.var[:, of_batch], ACT.Sqrt).then_inc(S[f"std{which}_ready"], 1)

            def copy_pair(rb, pair):
                act.wait_ge(S["r_turned_done"], rb * PAIRS + pair + 1)
                nc.scalar.copy(r_turned, qk_ps[:].rearrange("p (j k t) -> p j k t", j=2, k=KE)).then_inc(S["r_turn_copied"], 1)

            def chance(rb, pair):
                act.wait_ge(S["logits_done"], rb * PAIRS + pair + 1)
                nc.scalar.activation(chances[:, 2 * pair:2 * pair + 2, :], qk_ps[:, 0:2 * NE].rearrange("p (j e) -> p j e", j=2),
                                     ACT.Exp, scale=-1.0).then_inc(S["chances_ready"], 1)

            def copy_rows(nb, j):
                act.wait_ge(S["row_turned"], nb * TPB + j + 5)
                if j == 0:
                    act.wait_ge(S["qk_done"], nb * (HEADS * PIECES) + 1)
                nc.scalar.copy(h_b[:, j // CT, :, (j % CT) * P:(j % CT + 1) * P],
                               qk_ps[:, 0:KE * P].rearrange("p (k t) -> p k t", k=KE)).then_inc(S["h_copied"], 1)

            root(0)
            for j in range(TPB):
                copy_rows(0, j)

            def batch(b, first_batch, last_batch):
                def exponential(n):
                    i = n % TPB
                    act.wait_ge(S["bias_ready"], b * N + n + 1)
                    if n >= 3:
                        act.wait_ge(S[f"turned{(n - 3) % TPB // CT}"],
                                    (b * N + n - 2) if (n - 3) % TPB < CT else (b * (N // 2) + (n - 3) // TPB * CT + (n - 3) % TPB - CT + 1))
                    nc.scalar.activation(probs[:, n % 3, 0:(i + 1) * P], s_ps[n % 2][:, 0:(i + 1) * P], ACT.Exp,
                                         bias=small[:, n % 4, 1:2], scale=SCALE, accum_out=small[:, n % 4, 2:3]).then_inc(S["exp_done"], 1)

                def copy_turned(n):
                    i = n % TPB
                    for half in range(i // CT + 1):
                        m = min(i + 1, (half + 1) * CT) - half * CT
                        act.wait_ge(S[f"turned{half}"], (b * N + n + 1) if half == 0 else (b * (N // 2) + n // TPB * CT + i - CT + 1))
                        if n >= 2 and half == 0:
                            act.wait_ge(S["pv_done"], b * N + n)
                        nc.scalar.copy(pt[:, n % 2, half * CT:half * CT + m, :], pt_ps[half][:, 0:m, :]).then_inc(S[f"copied{half}"], 1)

                for n in range(N + 2):
                    if not first_batch and n - 1 in R_PAIR:
                        chance(b - 1, R_PAIR.index(n - 1))
                    if not last_batch and COPY <= n < COPY + TPB:
                        copy_rows(b + 1, n - COPY)
                    if n >= 2:
                        copy_turned(n - 2)
                    if not first_batch and n in R_PAIR:
                        copy_pair(b - 1, R_PAIR.index(n))
                    if n < N:
                        exponential(n)
                    if n == ROOT:
                        if not last_batch:
                            root(b + 1)
                        if not first_batch:
                            root(b - 1, "2")

            batches(act, batch)
            root(B - 1, "2")
            for pair in range(PAIRS):
                copy_pair(B - 1, pair)
                chance(B - 1, pair)

        @block.vector
        def _(dve):
            STATS_OPS = 6

            def combine(nb, j):
                tile, r, t = nb * TPB + j, j % R, tmp[:, j % 2, :]
                dve.wait_ge(gathered[r], nb * (32 * TPB // R) + 32 * (j // R + 1))
                nc.vector.tensor_scalar(t, y[:, r, 0, :], sh.weight[:, 0, bass.ds(tile, 1)], None, ALU.mult).then_inc(S["combine_chain"], 1)
                dve.wait_ge(S["combine_chain"], tile * 3 + 1)
                nc.vector.scalar_tensor_tensor(out=t, in0=y[:, r, 1, :], scalar=sh.weight[:, 1, bass.ds(tile, 1)], in1=t,
                                               op0=ALU.mult, op1=ALU.add).then_inc(S["combine_chain"], 1)
                dve.wait_ge(S["combine_chain"], tile * 3 + 2)
                nc.vector.tensor_tensor(t, t, gate0[:, nb, :], ALU.mult).then_inc(S["combine_chain"], 1)
                dve.wait_ge(S["combine_chain"], tile * 3 + 3)
                nc.vector.tensor_tensor(sh.x[:, tile, :], sh.x[:, tile, :], t, ALU.add).then_inc(S["combined"], 1)
                dve.wait_ge(S["combined"], tile + 1)
                nc.vector.bn_stats(sh.stats[:, tile, :], sh.x[:, tile, :]).then_inc(S["stats_in"], 1)

            def variance(nb, which=""):
                at = bass.ds(nb * TPB, TPB)
                stat = lambda i: sh.stats[:, at, i]
                mean, dif, var = sh.mean[:, at], sh.dif[:, at], sh.var[:, at]
                count = [0]

                def link(ins):
                    count[0] += 1
                    ins.then_inc(S[f"stats{which}_chain"], 1)
                    dve.wait_ge(S[f"stats{which}_chain"], nb * STATS_OPS + count[0])

                dve.wait_ge(S[f"stats{which}_in"], nb * TPB + TPB)
                link(nc.vector.tensor_tensor(mean, stat(1), stat(4), ALU.add))
                link(nc.vector.tensor_scalar(mean, mean, 0.5, None, ALU.mult))
                link(nc.vector.tensor_tensor(dif, stat(1), stat(4), ALU.subtract))
                link(nc.vector.tensor_tensor(dif, dif, dif, ALU.mult))
                link(nc.vector.tensor_tensor(var, stat(2), stat(5), ALU.add))
                link(nc.vector.tensor_scalar(dif, dif, 0.25, EPS_LN, ALU.mult, ALU.add))
                nc.vector.scalar_tensor_tensor(out=var, in0=var, scalar=1.0 / E, in1=dif, op0=ALU.mult, op1=ALU.add).then_inc(S[f"var{which}_ready"], 1)

            def invert(nb, which=""):
                at = bass.ds(nb * TPB, TPB)
                dve.wait_ge(S[f"std{which}_ready"], nb + 1)
                nc.vector.reciprocal(sh.rstd[:, at], sh.var[:, at]).then_inc(S[f"rstd{which}_ready"], 1)

            def route_row(rb, j):
                tile = rb * TPB + j
                if j == 0:
                    dve.wait_ge(S["rstd2_ready"], rb + 1)
                    dve.wait_ge(S["rows_left"], rb + 1)
                nc.vector.scalar_tensor_tensor(out=r_rows[:, j, :], in0=sh.x[:, tile, :], scalar=sh.mean[:, bass.ds(tile, 1)],
                                               in1=mods2[:, 1, rb, :], op0=ALU.subtract, op1=ALU.mult).then_inc(S["r_half_ready"], 1)
                dve.wait_ge(S["r_half_ready"], tile + 1)
                nc.vector.scalar_tensor_tensor(out=r_rows[:, j, :], in0=r_rows[:, j, :], scalar=sh.rstd[:, bass.ds(tile, 1)],
                                               in1=mods2[:, 0, rb, :], op0=ALU.mult, op1=ALU.add).then_inc(S["r_row_ready"], 1)

            ROUTE_OPS = 37
            link_count = [0]

            def linked(rb, ins):
                link_count[0] += 1
                ins.then_inc(S["pick_chain"], 1)
                dve.wait_ge(S["pick_chain"], rb * ROUTE_OPS + link_count[0])

            over = lambda a: a.rearrange("p (t o) -> p t o", o=1).broadcast_to([P, TPB, NE])

            def pick(rb, k):
                v = nc.vector
                if k == 0:
                    link_count[0] = 0
                    dve.wait_ge(S["chances_ready"], rb * PAIRS + PAIRS)
                    linked(rb, v.tensor_scalar(chances[:], chances[:], 1.0, None, ALU.add))
                    linked(rb, v.reciprocal(chances[:], chances[:]))
                values = scores if k else chances
                linked(rb, v.tensor_reduce(top[:, k], values[:], AX_X, ALU.max))
                linked(rb, v.tensor_tensor(cand[:], values[:], over(top[:, k]), ALU.is_lt))
                linked(rb, v.scalar_tensor_tensor(out=cand[:], in0=cand[:], scalar=float(NE), in1=iota_e[:], op0=ALU.mult, op1=ALU.add))
                linked(rb, v.tensor_reduce(idx[:], cand[:], AX_X, ALU.min))
                linked(rb, v.tensor_tensor(mask[:, k], iota_e[:], over(idx[:]), ALU.is_equal))
                if k == 0:
                    linked(rb, v.scalar_tensor_tensor(out=scores[:], in0=mask[:, 0], scalar=-3e38, in1=chances[:], op0=ALU.mult, op1=ALU.add))
                else:
                    v.tensor_tensor(both[:], mask[:, 0], mask[:, 1], ALU.add).then_inc(S["masks_ready"], 1)

            def take_ranks(rb):
                v = nc.vector
                flat = lambda a: a.rearrange("p e t -> p (e t)")
                in_tile = qk_ps[:, 0:TPB * NE].rearrange("p (t e) -> p t e", t=TPB)
                of_tile = qk_ps[:, TPB * NE:2 * TPB * NE].rearrange("p (t e) -> p e t", t=TPB)
                dve.wait_ge(S["ranked"], rb + 1)
                linked(rb, v.tensor_copy(plus[:], of_tile))
                linked(rb, v.tensor_tensor(plus[:, :, 0], plus[:, :, 0], so_far[:], ALU.add))
                linked(rb, v.tensor_tensor_scan(flat(before[:]), flat(run_on[:]), flat(plus[:]), 0.0, ALU.mult, ALU.add))
                linked(rb, v.tensor_copy(so_far[:], before[:, :, TPB - 1]))
                linked(rb, v.tensor_tensor(before[:], before[:], of_tile, ALU.subtract))
                v.tensor_tensor(rank[:], in_tile, before[:].rearrange("p e t -> p t e"), ALU.add).then_inc(S["rank_taken"], 1)

            def slots(rb):
                v = nc.vector
                dve.wait_ge(S["rank_taken"], rb + 1)
                linked(rb, v.tensor_tensor(cand[:], rank[:], offs[:].rearrange("p (o e) -> p o e", o=1).broadcast_to([P, TPB, NE]), ALU.add))
                for k in range(2):
                    for source, dst in ((cand, slot), (rank, valid)):
                        linked(rb, v.tensor_tensor(scores[:], mask[:, k], source[:], ALU.mult))
                        linked(rb, v.tensor_reduce(dst[:, k], scores[:], AX_X, ALU.add))
                linked(rb, v.tensor_scalar(valid[:], valid[:], float(CAP1), None, ALU.is_lt))
                linked(rb, v.scalar_tensor_tensor(out=slot[:], in0=slot[:], scalar=spare[:, 0:1], in1=valid[:], op0=ALU.subtract, op1=ALU.mult))
                linked(rb, v.tensor_scalar(slot[:], slot[:], spare[:, 0:1], None, ALU.add))
                v.tensor_copy(sh.slot_of[:, :, bass.ds(rb * TPB, TPB)], slot[:]).then_inc(S["slots_ready"], 1)

            def weights(rb):
                v = nc.vector
                linked(rb, v.tensor_tensor(wsum[:], top[:, 0], top[:, 1], ALU.add))
                linked(rb, v.tensor_scalar(wsum[:], wsum[:], 1e-6, None, ALU.add))
                linked(rb, v.reciprocal(wsum[:], wsum[:]))
                for k in range(2):
                    linked(rb, v.tensor_tensor(top[:, k], top[:, k], wsum[:], ALU.mult))
                    linked(rb, v.tensor_tensor(sh.weight[:, k, bass.ds(rb * TPB, TPB)], top[:, k], valid[:, k], ALU.mult))
                assert link_count[0] == ROUTE_OPS, link_count[0]

            def normalise_rows(nb, j):
                tile = nb * TPB + j
                if j == 0:
                    dve.wait_ge(S["rstd_ready"], nb + 1)
                dve.wait_ge(S["row_turned"], tile + 1)
                nc.vector.scalar_tensor_tensor(out=rows[:, j % 4, :], in0=sh.x[:, tile, :], scalar=sh.mean[:, bass.ds(tile, 1)],
                                               in1=sh.mods[:, 1, nb, :], op0=ALU.subtract, op1=ALU.mult).then_inc(S["half_ready"], 1)
                dve.wait_ge(S["half_ready"], tile + 1)
                nc.vector.scalar_tensor_tensor(out=rows[:, j % 4, :], in0=rows[:, j % 4, :], scalar=sh.rstd[:, bass.ds(tile, 1)],
                                               in1=sh.mods[:, 0, nb, :], op0=ALU.mult, op1=ALU.add).then_inc(S["row_ready"], 1)

            dve.wait_ge(S["mods_in"], 32)
            for j in range(TPB):
                combine(0, j)
            variance(0)
            invert(0)
            for j in range(TPB):
                normalise_rows(0, j)
            dve.wait_ge(S["pos_in"], 16)
            dve.wait_ge(S["route_in"], 32)
            dve.wait_ge(S["consts_ready"], 9)
            dve.wait_ge(S["later_set"], 2)

            def batch(b, first_batch, last_batch):
                def take_piece(h, i):
                    dve.wait_ge(S["qk_done"], b * (HEADS * PIECES) + h * PIECES + i + 2)
                    if i == 0 and h >= 2:
                        dve.wait_ge(S["scored"], b * N + (h - 1) * TPB)
                    if i < 4:
                        nc.vector.tensor_tensor(qk[:, h % 2, i // 2, (i % 2) * CH:(i % 2 + 1) * CH], piece_bank(h, i),
                                                pos[:, (i % 2) * CH:(i % 2 + 1) * CH], ALU.add).then_inc(S["qk_ready"], 1)
                    else:
                        dve.wait_ge(S["pv_done"], b * N + max(h - 1, 0) * TPB + 1)
                        nc.vector.tensor_copy(v[:, h % 2, (i % 2) * CT:(i % 2 + 1) * CT, :],
                                              piece_bank(h, i).rearrange("p (t f) -> p t f", t=CT)).then_inc(S["qk_ready"], 1)

                def maximum(n):
                    i = n % TPB
                    diagonal = s_ps[n % 2][:, i * P:(i + 1) * P]
                    dve.wait_ge(S["scored"], b * N + n + 1)
                    nc.vector.tensor_tensor(diagonal, diagonal, hidden_pos[:], ALU.add).then_inc(S["masked"], 1)
                    dve.wait_ge(S["masked"], b * N + n + 1)
                    nc.vector.reduce_max(small[:, n % 4, 0:1], s_ps[n % 2][:, 0:(i + 1) * P], AX_X).then_inc(S["max_taken"], 1)
                    dve.wait_ge(S["max_taken"], b * N + n + 1)
                    nc.vector.tensor_scalar(small[:, n % 4, 1:2], small[:, n % 4, 0:1], -SCALE, None, ALU.mult).then_inc(S["bias_ready"], 1)

                def normalise(n):
                    i = n % TPB
                    dve.wait_ge(S["exp_done"], b * N + n + 1)
                    nc.vector.reciprocal(small[:, n % 4, 3:4], small[:, n % 4, 2:3]).then_inc(S["inverted"], 1)
                    dve.wait_ge(S["inverted"], b * N + n + 1)
                    row = probs[:, n % 3, 0:(i + 1) * P]
                    nc.vector.tensor_scalar(row, row, small[:, n % 4, 3:4], None, ALU.mult).then_inc(S["normed"], 1)

                def keep(n):
                    h, i = n // TPB, n % TPB
                    dve.wait_ge(S["pv_done"], b * N + n + 2)
                    nc.vector.tensor_copy(attn[:, h, i * P:(i + 1) * P], o_ps[:]).then_inc(S["attn_ready"], 1)

                for i in range(PIECES):
                    take_piece(0, i)
                for n in range(N + 4):
                    if n >= 4:
                        keep(n - 4)
                    if not last_batch:
                        if n in ADD:
                            combine(b + 1, ADD.index(n))
                        if n == VAR:
                            variance(b + 1)
                        if n == INVERT:
                            invert(b + 1)
                    if not first_batch:
                        if n == VAR:
                            variance(b - 1, "2")
                        if n == INVERT:
                            invert(b - 1, "2")
                        if n in R_NORM:
                            route_row(b - 1, R_NORM.index(n))
                        if n in PICK:
                            pick(b - 1, PICK.index(n))
                        if n in SLOTS:
                            (take_ranks, slots, weights)[SLOTS.index(n)](b - 1)
                    if not last_batch:
                        if NORM <= n < NORM + TPB:
                            normalise_rows(b + 1, n - NORM)
                    if n < N:
                        maximum(n)
                    if 1 <= n <= N:
                        normalise(n - 1)
                    if n < N and n % TPB in PROJECT and n // TPB + 1 < HEADS:
                        take_piece(n // TPB + 1, PROJECT.index(n % TPB))
                for t in range(TPB):
                    tile = b * TPB + t
                    dve.wait_ge(S["out_done"], tile + 1)
                    nc.vector.tensor_tensor(gated[:, t % 2, :], bank(t)[:, 0:E], sh.mods[:, 2, b, :], ALU.mult).then_inc(S["out_added"], 1)
                    dve.wait_ge(S["out_added"], tile + 2)
                    nc.vector.tensor_tensor(sh.x[:, tile, :], sh.x[:, tile, :], gated[:, t % 2, :], ALU.add).then_inc(S["chain"], 1)
                    dve.wait_ge(S["chain"], tile + 1)
                    nc.vector.bn_stats(sh.stats[:, tile, :], sh.x[:, tile, :]).then_inc(S["stats2_in"], 1)

            batches(dve, batch)
            variance(B - 1, "2")
            invert(B - 1, "2")
            for j in range(TPB):
                route_row(B - 1, j)
            pick(B - 1, 0)
            pick(B - 1, 1)
            take_ranks(B - 1)
            slots(B - 1)
            weights(B - 1)


def program(nc, d):
    sh = Shared()
    with ExitStack() as ctx:
        sb = lambda name, shape, dt=F32: ctx.enter_context(nc.sbuf_tensor(name, shape, dt))
        sh.x = sb("x", [P, TILES, E])
        sh.mods = sb("mods", [P, 3, B, E])
        sh.ident = sb("ident", [P, P])
        sh.stats = sb("stats", [P, TILES, 6])
        sh.mean, sh.var, sh.rstd, sh.dif = (sb(name, [P, TILES]) for name in ("mean", "var", "rstd", "dif"))
        sh.slot_of = sb("slot_of", [P, 2, TILES], U32)
        sh.weight = sb("weight", [P, 2, TILES])
        sh.owner_i = sb("owner_i", [P, TILES0], I32)
        with ExitStack() as first_block:
            sl = lambda name, shape: first_block.enter_context(nc.sbuf_tensor(name, shape, F32))
            sh.zeros = sl("zeros", [P, E])
            sh.w_in = sl("w_in", [P, KE, 2 * DI])
            sh.w_out = sl("w_out", [P, MD, E])
            sh.w_x = sl("w_x", [P, MD, 1 + 2 * NS])
            sh.w_delta = sl("w_delta", [P, MD, P])
            sh.conv_w = sl("conv_w", [P, MD, DC])
            sh.vecs = sl("inner_vecs", [P, 4, MD])
            sh.a_neg = sl("a_neg", [P, MD, NS])
            phase_prepare(nc, d, sh)
            phase_norm_turn(nc, d, sh)
            phase_mamba(nc, d, sh)
        sh.w_qkv = sb("w_qkv", [P, KE, HEADS, 3, DH])
        sh.att_w_in = ctx.enter_context(Semaphores(nc, "aw_"))("loaded")
        with ExitStack() as second_block:
            sw = lambda name, shape: second_block.enter_context(nc.sbuf_tensor(name, shape, F32))
            sh.w13 = sw("w13", [P, EXPERTS0, 2, KE, H0])
            sh.w2_0 = sw("w2_0", [P, EXPERTS0, MH0, E])
            sh.e0_w_in = second_block.enter_context(Semaphores(nc, "ew_"))("loaded")
            phase_route(nc, d, sh)
            phase_experts0(nc, d, sh)
        phase_attention(nc, d, sh)
        phase_experts1(nc, d, sh)
        phase_combine(nc, d, sh)


_PLAIN = ["L0_attn_x", "L0_attn_W_in", "L0_attn_conv_w", "L0_attn_W_x", "L0_attn_A_log", "L0_attn_W_out", "L0_wmod", "L1_wmod",
          "L0_ffn_Wr", "L0_ffn_W1", "L0_ffn_W2", "L0_ffn_W3", "L1_ffn_w1", "L1_ffn_w2"]
_SCRATCH = {
    "mod_rows": [2, 6, B, E],
    "h_turned": [B * CPB, P, KE, CH],
    "bc_rows": [B * CPB, 2 * NS, CH],
    "slots0": [SLOTS0, E],
    "outs0": [SLOTS0, E],
    "slots1": [SLOTS1, E],
    "outs1": [SLOTS1, E],
}


def lay_out(inputs):
    get = lambda n: np.asarray(inputs[n])
    arrays = {n: np.ascontiguousarray(get(n)) for n in _PLAIN}
    cs = np.stack([get("L0_c"), get("L1_c")])
    arrays["cT"] = np.ascontiguousarray(cs.reshape(2, B, KE, P).transpose(3, 0, 2, 1))
    vecs = np.stack([get("L0_attn_conv_b"), get("L0_attn_dt_w"), get("L0_attn_dt_b"), get("L0_attn_D")])
    arrays["vecs"] = np.ascontiguousarray(vecs.reshape(4, MD, P).transpose(2, 0, 1))
    arrays["wqkvT"] = np.ascontiguousarray(get("L1_attn_Wqkv").T)
    arrays["woT"] = np.ascontiguousarray(get("L1_attn_Wo").T)
    arrays["gate_wT"] = np.ascontiguousarray(get("L1_ffn_gate_w").T)
    arrays["posT"] = positions()
    return arrays


def positions():
    t = np.arange(T, dtype=np.float32)[:, None]
    div = np.exp(np.arange(0, DH, 2, dtype=np.float32) * np.float32(-np.log(10000.0) / DH))
    angle = t * div
    return np.ascontiguousarray(np.stack([np.sin(angle), np.cos(angle)], axis=-1).reshape(T, DH).T)


def declare(nc, arrays):
    d = {n: nc.dram_tensor(n, list(a.shape), F32, kind="ExternalInput").ap() for n, a in arrays.items()}
    for n, shape in _SCRATCH.items():
        d[n] = nc.dram_tensor(n, shape, F32).ap()
    d["out"] = nc.dram_tensor("out", [B, T, E], F32, kind="ExternalOutput").ap()
    return d


def kernel(**inputs):
    import concourse.bacc as bacc
    from concourse.bass_utils import run_bass_kernel_spmd

    nc = bacc.Bacc("TRN2", target_bir_lowering=False, num_devices=1)
    arrays = lay_out(inputs)
    program(nc, declare(nc, arrays))
    return run_bass_kernel_spmd(nc, [arrays], core_ids=[0]).results[0]["out"]
```
